# Optimizing a Trainium2 kernel written in Bass

```python
import numpy as np
import jax
import jax.numpy as jnp

def _softmax(x, axis=-1):
    return jax.nn.softmax(x, axis=axis)

def _gelu(x):
    return jax.nn.gelu(x, approximate=True)

def _silu(x):
    return jax.nn.silu(x)

def _sigmoid(x):
    return jax.nn.sigmoid(x)

def _layernorm(x, axis=-1, eps=1e-05):
    m = jnp.mean(x, axis=axis, keepdims=True)
    v = jnp.var(x, axis=axis, keepdims=True)
    return (x - m) / jnp.sqrt(v + eps)

def _scatter_add(tgt, idx, src, axis=0):
    return tgt.at[idx].add(src)

def _segment_sum(src, seg, n):
    return jax.ops.segment_sum(src, seg, n)
kernel_name = 'mk_recurrent_d2_jaxref_r4_bf0de0'

def setup_inputs(seed: int=0):
    np.random.seed(seed)
    _w = jnp.asarray

    def _L0_attn_setup():
        import jax, jax.numpy as jnp
        import numpy as np
        H = 16
        SEG = 512
        DIL = 8
        BLOCK_M = 64
        key = jax.random.key(seed)
        k1, k2, k3 = jax.random.split(key, 3)
        B, M, D = (2, 2048, 256)
        x = jax.random.normal(k1, (B, M, D), dtype=jnp.float32)
        Wqkv = jax.random.normal(k2, (3 * D, D), dtype=jnp.float32) * 0.02
        Wout = jax.random.normal(k3, (D, D), dtype=jnp.float32) * 0.02
        return {'x': x, 'Wqkv': Wqkv, 'Wout': Wout}
    _L0_attn_in = _L0_attn_setup()

    def _L0_ffn_setup():
        import jax, jax.numpy as jnp
        import numpy as np
        FP8_MAX = 448.0
        key = jax.random.key(seed)
        k_x, k_w, k_b = jax.random.split(key, 3)
        B, S, IN, OUT = (4, 2048, 256, 256)
        x = jax.random.normal(k_x, (B, S, IN), dtype=jnp.float32)
        w_fp32 = jax.random.normal(k_w, (OUT, IN), dtype=jnp.float32)
        weight_fp8 = w_fp32.astype(jnp.float8_e4m3fn).astype(jnp.float32)
        bias = jax.random.normal(k_b, (OUT,), dtype=jnp.float32)
        input_scale = jnp.ones((1,), dtype=jnp.float32)
        weight_scale = jnp.ones((1,), dtype=jnp.float32)
        return {'x': x, 'weight_fp8': weight_fp8, 'bias': bias, 'input_scale': input_scale, 'weight_scale': weight_scale}
    _L0_ffn_in = _L0_ffn_setup()

    def _L1_attn_setup():
        import jax, jax.numpy as jnp
        import numpy as np
        D_MODEL = 256
        N_HEADS = 16
        HEAD_DIM = D_MODEL // N_HEADS

        def _rope_sincos(T, head_dim, dtype):
            inv_freq = 1.0 / 10000.0 ** (jnp.arange(0, head_dim, 2, dtype=jnp.float32) / head_dim)
            t = jnp.arange(T, dtype=jnp.float32)
            freqs = jnp.einsum('i,j->ij', t, inv_freq)
            return (jnp.sin(freqs)[None, None].astype(dtype), jnp.cos(freqs)[None, None].astype(dtype))

        def _apply_rope(q, k, sin, cos):
            q1, q2 = (q[..., ::2], q[..., 1::2])
            k1, k2 = (k[..., ::2], k[..., 1::2])
            q_rot = jnp.concatenate([q1 * cos - q2 * sin, q1 * sin + q2 * cos], axis=-1)
            k_rot = jnp.concatenate([k1 * cos - k2 * sin, k1 * sin + k2 * cos], axis=-1)
            return (q_rot, k_rot)
        key = jax.random.key(seed)
        ks = jax.random.split(key, 9)
        B, T, C = (8, 256, D_MODEL)
        s = 1.0 / np.sqrt(C)
        inp = {'x': jax.random.normal(ks[0], (B, T, C), dtype=jnp.float32), 'wq': jax.random.normal(ks[1], (C, C), dtype=jnp.float32) * s, 'bq': jnp.zeros((C,), dtype=jnp.float32), 'wk': jax.random.normal(ks[2], (C, C), dtype=jnp.float32) * s, 'bk': jnp.zeros((C,), dtype=jnp.float32), 'wv': jax.random.normal(ks[3], (C, C), dtype=jnp.float32) * s, 'bv': jnp.zeros((C,), dtype=jnp.float32), 'wo': jax.random.normal(ks[4], (C, C), dtype=jnp.float32) * s, 'bo': jnp.zeros((C,), dtype=jnp.float32)}
        return inp
    _L1_attn_in = _L1_attn_setup()

    def _L1_ffn_setup():
        import jax, jax.numpy as jnp
        import numpy as np
        B, S, D = (2, 512, 256)
        E, K, H = (8, 2, 1024)
        CAP_FACTOR = 1.0

        def _moe_forward(x, wg, w1, b1, w2, b2):
            Bb, Ss, Dd = x.shape
            T = Bb * Ss
            cap = int(K * CAP_FACTOR * ((T + E - 1) // E))
            xt = x.reshape(T, Dd)
            logits = xt @ wg
            scores = jax.nn.softmax(logits, axis=-1)
            gates_k, idx_k = jax.lax.top_k(scores, K)
            gates_k = gates_k / jnp.sum(gates_k, axis=-1, keepdims=True)
            masks = jax.nn.one_hot(idx_k, E, dtype=jnp.int32)
            m = jnp.transpose(masks, (1, 0, 2)).reshape(K * T, E)
            locs_full = jnp.cumsum(m, axis=0) - 1
            loc = jnp.sum(locs_full * m, axis=-1)
            loc = loc.reshape(K, T).T
            valid = (loc < cap).astype(xt.dtype)
            loc_c = jnp.clip(loc, 0, cap - 1)
            contrib = (xt[:, None, :] * valid[:, :, None]).reshape(T * K, Dd)
            disp = jnp.zeros((E, cap, Dd), xt.dtype)
            disp = disp.at[idx_k.reshape(-1), loc_c.reshape(-1)].add(contrib)
            h = jax.nn.relu(jnp.einsum('ecd,edh->ech', disp, w1) + b1[:, None, :])
            out = jnp.einsum('ech,ehd->ecd', h, w2) + b2[:, None, :]
            gathered = out[idx_k, loc_c]
            y = jnp.einsum('tk,tkd->td', gates_k * valid, gathered)
            return y.reshape(Bb, Ss, Dd)
        key = jax.random.key(seed)
        ks = jax.random.split(key, 6)
        scale_in = 1.0 / np.sqrt(D)
        scale_h = 1.0 / np.sqrt(H)
        return {'x': jax.random.normal(ks[0], (B, S, D), jnp.float32), 'wg': jax.random.normal(ks[1], (D, E), jnp.float32) * scale_in, 'w1': jax.random.normal(ks[2], (E, D, H), jnp.float32) * scale_in, 'b1': jnp.zeros((E, H), jnp.float32), 'w2': jax.random.normal(ks[3], (E, H, D), jnp.float32) * scale_h, 'b2': jnp.zeros((E, D), jnp.float32)}
    _L1_ffn_in = _L1_ffn_setup()
    _d = {'L0_attn_x': _L0_attn_in['x'], 'L0_attn_Wqkv': _L0_attn_in['Wqkv'], 'L0_attn_Wout': _L0_attn_in['Wout'], 'L0_ffn_weight_fp8': _L0_ffn_in['weight_fp8'], 'L0_ffn_bias': _L0_ffn_in['bias'], 'L0_ffn_input_scale': _L0_ffn_in['input_scale'], 'L0_ffn_weight_scale': _L0_ffn_in['weight_scale'], 'L1_attn_wq': _L1_attn_in['wq'], 'L1_attn_bq': _L1_attn_in['bq'], 'L1_attn_wk': _L1_attn_in['wk'], 'L1_attn_bk': _L1_attn_in['bk'], 'L1_attn_wv': _L1_attn_in['wv'], 'L1_attn_bv': _L1_attn_in['bv'], 'L1_attn_wo': _L1_attn_in['wo'], 'L1_attn_bo': _L1_attn_in['bo'], 'L1_ffn_wg': _L1_ffn_in['wg'], 'L1_ffn_w1': _L1_ffn_in['w1'], 'L1_ffn_b1': _L1_ffn_in['b1'], 'L1_ffn_w2': _L1_ffn_in['w2'], 'L1_ffn_b2': _L1_ffn_in['b2']}
    _x0 = _d['L0_attn_x']
    _d['L0_attn_x'] = jax.random.normal(jax.random.fold_in(jax.random.key(seed), 1), (4, 2048, 256), dtype=_x0.dtype)
    del _x0
    return _d

def reference(L0_attn_x, L0_attn_Wqkv, L0_attn_Wout, L0_ffn_weight_fp8, L0_ffn_bias, L0_ffn_input_scale, L0_ffn_weight_scale, L1_attn_wq, L1_attn_bq, L1_attn_wk, L1_attn_bk, L1_attn_wv, L1_attn_bv, L1_attn_wo, L1_attn_bo, L1_ffn_wg, L1_ffn_w1, L1_ffn_b1, L1_ffn_w2, L1_ffn_b2):

    def _L0_attn_ref(x, Wqkv, Wout):
        import jax, jax.numpy as jnp
        import numpy as np
        H = 16
        SEG = 512
        DIL = 8
        BLOCK_M = 64
        B, M, D = x.shape
        hd = D // H
        scale = hd ** (-0.5)
        S = M // SEG
        Kn = SEG // DIL
        nb = SEG // BLOCK_M
        qkv = jnp.einsum('bmd,ed->bme', x, Wqkv).reshape(B, M, 3, H, hd)
        qkv = jnp.transpose(qkv, (2, 0, 3, 1, 4))
        q, k, v = (qkv[0] * scale, qkv[1], qkv[2])
        q4 = q.reshape(B, H, S, SEG, hd)
        k4 = k.reshape(B, H, S, SEG, hd)[:, :, :, ::DIL]
        v4 = v.reshape(B, H, S, SEG, hd)[:, :, :, ::DIL]
        scores = jnp.einsum('bhspd,bhskd->bhspk', q4, k4)
        scores = scores.reshape(B, H, S, nb, BLOCK_M, Kn)
        c = jnp.max(scores, axis=4, keepdims=True)
        w = jnp.exp(scores - c)
        den = jnp.sum(w, axis=-1) + 1e-10
        num = jnp.einsum('bhsnmk,bhskd->bhsnmd', w, v4)
        out = num / den[..., None]
        out = out.reshape(B, H, M, hd)
        out = jnp.transpose(out, (0, 2, 1, 3)).reshape(B, M, D)
        return jnp.einsum('bmd,ed->bme', out, Wout)

    def _L0_ffn_ref(x, weight_fp8, bias, input_scale, weight_scale):
        import jax, jax.numpy as jnp
        import numpy as np
        FP8_MAX = 448.0
        x_q = jnp.clip(x / input_scale, -FP8_MAX, FP8_MAX)
        x_dq = x_q.astype(jnp.float8_e4m3fn).astype(x.dtype) * input_scale
        w_dq = weight_fp8 * weight_scale
        out = jnp.einsum('bsi,oi->bso', x_dq, w_dq) + bias
        return out

    def _L1_attn_ref(x, wq, bq, wk, bk, wv, bv, wo, bo):
        import jax, jax.numpy as jnp
        import numpy as np
        D_MODEL = 256
        N_HEADS = 16
        HEAD_DIM = D_MODEL // N_HEADS

        def _rope_sincos(T, head_dim, dtype):
            inv_freq = 1.0 / 10000.0 ** (jnp.arange(0, head_dim, 2, dtype=jnp.float32) / head_dim)
            t = jnp.arange(T, dtype=jnp.float32)
            freqs = jnp.einsum('i,j->ij', t, inv_freq)
            return (jnp.sin(freqs)[None, None].astype(dtype), jnp.cos(freqs)[None, None].astype(dtype))

        def _apply_rope(q, k, sin, cos):
            q1, q2 = (q[..., ::2], q[..., 1::2])
            k1, k2 = (k[..., ::2], k[..., 1::2])
            q_rot = jnp.concatenate([q1 * cos - q2 * sin, q1 * sin + q2 * cos], axis=-1)
            k_rot = jnp.concatenate([k1 * cos - k2 * sin, k1 * sin + k2 * cos], axis=-1)
            return (q_rot, k_rot)
        B, T, C = x.shape
        H, hd = (N_HEADS, HEAD_DIM)
        q = (jnp.einsum('btc,dc->btd', x, wq) + bq).reshape(B, T, H, hd).transpose(0, 2, 1, 3)
        k = (jnp.einsum('btc,dc->btd', x, wk) + bk).reshape(B, T, H, hd).transpose(0, 2, 1, 3)
        v = (jnp.einsum('btc,dc->btd', x, wv) + bv).reshape(B, T, H, hd).transpose(0, 2, 1, 3)
        sin, cos = _rope_sincos(T, hd, x.dtype)
        q, k = _apply_rope(q, k, sin, cos)
        scale = 1.0 / np.sqrt(hd)
        att = jnp.einsum('bhtd,bhsd->bhts', q, k) * scale
        causal = jnp.tril(jnp.ones((T, T), dtype=bool))
        att = jnp.where(causal[None, None], att, -jnp.inf)
        att = jax.nn.softmax(att, axis=-1)
        y = jnp.einsum('bhts,bhsd->bhtd', att, v)
        y = y.transpose(0, 2, 1, 3).reshape(B, T, C)
        return jnp.einsum('btc,dc->btd', y, wo) + bo

    def _L1_ffn_ref(x, wg, w1, b1, w2, b2):
        import jax, jax.numpy as jnp
        import numpy as np
        B, S, D = (2, 512, 256)
        E, K, H = (8, 2, 1024)
        CAP_FACTOR = 1.0

        def _moe_forward(x, wg, w1, b1, w2, b2):
            Bb, Ss, Dd = x.shape
            T = Bb * Ss
            cap = int(K * CAP_FACTOR * ((T + E - 1) // E))
            xt = x.reshape(T, Dd)
            logits = xt @ wg
            scores = jax.nn.softmax(logits, axis=-1)
            gates_k, idx_k = jax.lax.top_k(scores, K)
            gates_k = gates_k / jnp.sum(gates_k, axis=-1, keepdims=True)
            masks = jax.nn.one_hot(idx_k, E, dtype=jnp.int32)
            m = jnp.transpose(masks, (1, 0, 2)).reshape(K * T, E)
            locs_full = jnp.cumsum(m, axis=0) - 1
            loc = jnp.sum(locs_full * m, axis=-1)
            loc = loc.reshape(K, T).T
            valid = (loc < cap).astype(xt.dtype)
            loc_c = jnp.clip(loc, 0, cap - 1)
            contrib = (xt[:, None, :] * valid[:, :, None]).reshape(T * K, Dd)
            disp = jnp.zeros((E, cap, Dd), xt.dtype)
            disp = disp.at[idx_k.reshape(-1), loc_c.reshape(-1)].add(contrib)
            h = jax.nn.relu(jnp.einsum('ecd,edh->ech', disp, w1) + b1[:, None, :])
            out = jnp.einsum('ech,ehd->ecd', h, w2) + b2[:, None, :]
            gathered = out[idx_k, loc_c]
            y = jnp.einsum('tk,tkd->td', gates_k * valid, gathered)
            return y.reshape(Bb, Ss, Dd)
        return _moe_forward(x, wg, w1, b1, w2, b2)
    x = L0_attn_x
    xn = _layernorm(x, axis=-1)
    s = _L0_attn_ref(xn, L0_attn_Wqkv, L0_attn_Wout)
    g = _silu(_L0_ffn_ref(xn, L0_ffn_weight_fp8, L0_ffn_bias, L0_ffn_input_scale, L0_ffn_weight_scale))
    x = x + s * g
    xn = _layernorm(x, axis=-1)
    s = _L1_attn_ref(xn, L1_attn_wq, L1_attn_bq, L1_attn_wk, L1_attn_bk, L1_attn_wv, L1_attn_bv, L1_attn_wo, L1_attn_bo)
    g = _silu(_L1_ffn_ref(xn, L1_ffn_wg, L1_ffn_w1, L1_ffn_b1, L1_ffn_w2, L1_ffn_b2))
    x = x + s * g
    return x

_drawn_inputs = setup_inputs


def setup_inputs(seed=0):
    import zlib

    import numpy as np

    out = dict(_drawn_inputs(seed))
    spreads = {'L1_attn_bq': (0.0, 0.8),
     'L1_attn_bk': (0.0, 0.8),
     'L1_attn_bv': (0.0, 0.275),
     'L1_attn_bo': (0.0, 0.289),
     'L1_ffn_b1': (0.0, 0.8),
     'L1_ffn_b2': (0.0, 0.8)}
    factors = {'L0_ffn_bias': 5.632}
    for name, (base, spread) in spreads.items():
        noise = np.random.default_rng([zlib.crc32(name.encode()), seed]).standard_normal(out[name].shape)
        drawn = base * np.exp(spread * noise) if base else spread * noise
        out[name] = jnp.asarray(drawn.astype(out[name].dtype))
    for name, factor in factors.items():
        out[name] = (out[name] * factor).astype(out[name].dtype)
    return out
```

```python
from contextlib import ExitStack

import numpy as np

import concourse.bass as bass
from concourse import mybir

ALU = mybir.AluOpType
ACT = mybir.ActivationFunctionType
AX = mybir.AxisListType.X
F32 = mybir.dt.float32
BF16 = mybir.dt.bfloat16
F8 = mybir.dt.float8e4
I32 = mybir.dt.int32
U32 = mybir.dt.uint32

P = 128
B, M, D = 4, 2048, 256
T = B * M
H, HD = 16, 16
SEG, DIL, BLK = 512, 8, 64
NSEG = T // SEG
SPB = M // SEG
KN = SEG // DIL
NBLK = SEG // BLK
DC = D // P
TT = SEG // P
NT = T // P
E, TOPK, HID = 8, 2, 1024
CAP = TOPK * ((T + E - 1) // E)
NSLOT = E * CAP
SCALE = HD ** -0.5
LN_EPS = 1e-5
DEN_EPS = 1e-10
FP8_MAX = 448.0
G = 4
NG = H // G
NGROUPS = B * NG
NQT = M // P
HW = 32
PIECE = 3
STACK = 6 * HD
ROWS = STACK + PIECE
Q_PIECES = (0, 0, 1, 0, 1, 2)
K_PIECES = (0, 1, 0, 2, 1, 0)
RSQRT_MAGIC = 0x5F3759DF
LOWEST = -3.0e38
MASKED = -1.0e30


class Events:

    def __init__(self, nc, ctx, prefix, counts, dma, bare=()):
        self.bare = bare
        self.k, self.unit, self.sem = {}, {}, {}
        for name, k in counts.items():
            self.k[name], self.unit[name] = k, 16 if name in dma else 1
            self.sem[name] = ctx.enter_context(nc.semaphore(f"{prefix}_{name}"))

    def start(self, e):
        for name, s in self.sem.items():
            if name not in self.bare:
                e.sem_inc(s, self.unit[name])

    def at(self, name, n, j):
        return (n * self.k[name] + j + (name not in self.bare)) * self.unit[name]

    def wait(self, e, name, n, j):
        e.wait_ge(self.sem[name], self.at(name, n, j))

    def done(self, ins, name):
        return ins.then_inc(self.sem[name], self.unit[name])


class Steps:

    def __init__(self, e, sem, base, ev=None):
        self.e, self.sem, self.base, self.n, self.ev = e, sem, base, 0, ev
        self.last = None

    def step(self, n):
        self.at, self.seen = n, {}

    def then(self, ins):
        self.n += 1
        self.last = self.sem, self.base + self.n
        return ins.then_inc(self.sem, 1)

    def mark(self, ins, name):
        self.seen[name] = self.seen.get(name, 0) + 1
        self.last = self.ev.sem[name], self.ev.at(name, self.at, self.seen[name])
        return self.ev.done(ins, name)

    def settle(self, passed=None):
        self.e.wait_ge(*self.last)
        if passed is not None:
            self.e.sem_inc(passed, 1)


def layers_phase(nc, io, dram):
    with ExitStack() as ctx:
        def sb(name, shape, dt=F32):
            return ctx.enter_context(nc.sbuf_tensor("a_" + name, shape, dt))

        def ps(name, shape, dt=F32):
            return ctx.enter_context(nc.psum_tensor("a_" + name, shape, dt))

        ident = sb("ident", [P, P])
        headmask = sb("headmask", [P, H // DC])
        rope = sb("rope", [P, 2, M])
        wqkv0 = sb("wqkv0", [P, DC, 3 * D])
        wout0 = sb("wout0", [P, DC, D])
        wf = sb("wf", [P, DC, D])
        wf_rest = sb("wf_rest", [P, DC, D])
        wf_piece = [sb(f"wf_piece{i}", [P, DC, D], BF16) for i in range(PIECE)]
        fbias = sb("fbias", [P, D])
        in_scale = sb("in_scale", [P, 1])
        in_inv = sb("in_inv", [P, 1])
        square = sb("square", [P, DC, SEG])
        w_scale = sb("w_scale", [P, 1])
        wqk1 = sb("wqk1", [P, DC, 4 * P])
        bqk1 = sb("bqk1", [P, 4])
        wvg1 = sb("wvg1", [P, DC, D + E])
        bv1 = sb("bv1", [P, D])
        x = sb("x", [P, 2, TT, D])
        stats = sb("stats", [P, 2, TT, 6])
        mv = sb("mv", [P, 2, TT, 2])
        rstd = sb("rstd", [P, 2, TT])
        veps = sb("veps", [P, 2, TT])
        seed = sb("seed", [P, 2, TT], I32)
        newton = sb("newton", [P, 2, TT])
        xn = sb("xn", [P, TT, D])
        xnT = sb("xnT", [P, DC, SEG])
        clipped = sb("clipped", [P, DC, SEG])
        coarse = sb("coarse", [P, DC, SEG], F8)
        half8 = sb("half8", [P, DC, SEG], F8)
        is_big = sb("is_big", [P, DC, SEG], U32)
        doubled = sb("doubled", [P, DC, SEG], BF16)
        xq = sb("xq", [P, DC, SEG], BF16)
        qT = sb("qT", [P, DC, SEG])
        kbd = sb("kbd", [P, DC, H // DC, KN])
        vbd = sb("vbd", [P, H // 2, 2 * HW])
        keymax = sb("keymax", [P, 2, NBLK])
        shifted = sb("shifted", [P, 2, SEG])
        wexp = sb("wexp", [P, 2, SEG])
        oT = sb("oT", [P, 2, SEG])
        den = sb("den", [P, TT, G])
        rden = sb("rden", [P, TT, G])
        y = sb("y", [P, TT, D])
        yT = sb("yT", [P, DC, SEG])
        z = sb("z", [P, TT, D])
        ez = sb("ez", [P, TT, D])
        x1 = sb("x1", [P, TT, D])
        xn1 = sb("xn1", [P, TT, D])
        x1T = sb("x1T", [P, DC, SEG])
        qk = sb("qk", [P, 2, 2, SEG])
        rot = sb("rot", [P, 2, 2, SEG])
        prod = sb("prod", [P, 2, SEG])
        piece = [sb(f"piece{i}", [P, 2, 2, SEG], BF16) for i in range(PIECE)]
        v32 = sb("v32", [P, TT, H, HW])
        logit = sb("logit", [P, TT, E])

        tb = ps("tb", [P, DC, SEG])
        pb = ps("pb", [P, 2, SEG])
        kv = ps("kv", [P, SEG])
        sc = ps("sc", [P, 2, SEG])
        ob = ps("ob", [P, SEG])

        NP0 = H // 2
        counts = dict(
            var=1, rstd=1, xn=1, tr=1, trc=2, q=1, qc=1, kv=1, kvc=1, ff=2, ffc=2, quant=1,
            s=NP0, shift=NP0, wexp=NP0, pv=NP0, oc=4, ot=4, norm=4, ytr=1, ytc=2,
            so=2, sog=2, ez=2, gate=1, x1=1, x1_out=1,
            var1=1, rstd1=1, xn1=1, xn1_out=1, tr1=1, tr1c=2, pj=2, pjc=4, rot=1, p1=1, p2=1, p3=1,
            qk_out=12, vj=4, vjc=4, v_out=NG, l_out=1)
        counts.update(x_in0=1, x_in1=1)
        ev = Events(nc, ctx, "a", counts, {"x_in0", "x_in1", "x1_out", "xn1_out", "qk_out", "v_out", "l_out"})
        consts = ctx.enter_context(nc.semaphore("a_consts"))
        ready = ctx.enter_context(nc.semaphore("a_ready"))
        passed = ctx.enter_context(nc.semaphore("a_passed"))
        dve_step = ctx.enter_context(nc.semaphore("a_dve_step"))
        setup_step = ctx.enter_context(nc.semaphore("a_setup_step"))
        NCONST = 13
        pool_step = ctx.enter_context(nc.semaphore("a_pool_step"))
        DVE_STEPS = 228
        POOL_STEPS = SPB * 2 * (3 * 4 - 1)

        with nc.Block() as block:
            @block.sync
            def _(sp):
                loads = [
                    (ident[:], io["c_ident"]), (headmask[:], io["c_headmask"]),
                    (rope[:], io["c_rope"]),
                    (wqkv0[:], io["wqkv0T"].rearrange("(k p) n -> p k n", p=P)),
                    (wout0[:], io["wout0T"].rearrange("(k p) n -> p k n", p=P)),
                    (wf[:], io["wfT"].rearrange("(k p) n -> p k n", p=P)),
                    (fbias[:], io["fbias"].partition_broadcast(P)),
                    (in_scale[:], io["in_scale"].partition_broadcast(P)),
                    (w_scale[:], io["w_scale"].partition_broadcast(P)),
                    (wqk1[:], io["wqk1T"].rearrange("(k p) n -> p k n", p=P)),
                    (bqk1[:], io["bqk1"]),
                    (wvg1[:], io["wvg1T"].rearrange("(k p) n -> p k n", p=P)),
                    (bv1[:], io["bv1"].partition_broadcast(P)),
                ]
                assert len(loads) == NCONST
                for out, in_ in loads:
                    sp.dma_start(out, in_).then_inc(consts, 16)
                with sp.Fori(0, B) as b:
                    for c in range(SPB):
                        n = b * SPB + c
                        for ahead in range(c if c == 0 else c + 1, min(c + 2, SPB)):
                            ev.wait(sp, "x1", n, 0)
                            src = io["x"][bass.ds(b, 1), ahead * SEG:(ahead + 1) * SEG, :]
                            ev.done(sp.dma_start(x[:, ahead % 2], src.rearrange("o (t p) d -> p (o t) d", p=P)), f"x_in{ahead % 2}")
                        tok = bass.ds(b * M + c * SEG, SEG)
                        ev.wait(sp, "x1", n, 1)
                        ev.done(sp.dma_start(dram["x1"][tok, :].rearrange("(t p) d -> p t d", p=P), x1[:]), "x1_out")
                        ev.wait(sp, "xn1", n, 1)
                        ev.done(sp.dma_start(dram["xn1"][tok, :].rearrange("(t p) d -> p t d", p=P), xn1[:]), "xn1_out")
                        for i in range(PIECE):
                            ev.wait(sp, f"p{i + 1}", n, 1)
                            for m in range(2):
                                for f in range(2):
                                    dst = dram["qk"][m, bass.ds(b * NG, NG), i, f, :, c * SEG:(c + 1) * SEG]
                                    ev.done(sp.dma_start(dst, piece[i][:, m, f, :]), "qk_out")
                        ev.wait(sp, "vjc", n, 4)
                        for hg in range(NG):
                            dst = dram["v"][bass.ds(b * NG + hg, 1), c * SEG:(c + 1) * SEG, :]
                            ev.done(sp.dma_start(dst.rearrange("o (t p) w -> p (o t) w", p=P),
                                                 v32[:, :, hg * G:(hg + 1) * G, :].rearrange("p t h w -> p t (h w)")),
                                    "v_out")
                        ev.done(sp.dma_start(dram["logits"][tok, :].rearrange("(t p) d -> p t d", p=P), logit[:]), "l_out")
                for name in ("x1_out", "xn1_out", "qk_out", "v_out", "l_out"):
                    sp.wait_ge(ev.sem[name], 16 * (NSEG * counts[name] + 1))

            @block.gpsimd
            def _(pool):
                with pool.Fori(0, B) as b:
                    ps_ = Steps(pool, pool_step, b * POOL_STEPS, ev)
                    ps_.last = ev.sem["rstd1"], ev.at("rstd1", b * SPB, 0)
                    for c in range(SPB):
                        n = b * SPB + c
                        ps_.step(n)
                        for var, rs, i in (("var", "rstd", 0), ("var1", "rstd1", 1)):
                            ev.wait(pool, var, n, 1)
                            ps_.settle()
                            v, root, tmp = veps[:, i], rstd[:, i], newton[:, i]
                            for step in range(3):
                                start = seed[:, i].bitcast(F32) if step == 0 else root
                                ps_.then(pool.tensor_tensor(tmp, start, start, ALU.mult))
                                ps_.settle()
                                ps_.then(pool.tensor_tensor(tmp, tmp, v, ALU.mult))
                                ps_.settle(passed)
                                ps_.then(pool.tensor_scalar(tmp, tmp, -0.5, 1.5, ALU.mult, ALU.add))
                                ps_.settle()
                                last = pool.tensor_tensor(root, start, tmp, ALU.mult)
                                if step < 2:
                                    ps_.then(last)
                                    ps_.settle()
                            ps_.mark(last, rs)
                    assert ps_.n == POOL_STEPS, ps_.n

            @block.tensor
            def _(pe):
                pe.wait_ge(consts, 16 * NCONST)
                pe.wait_ge(ready, 1)

                with pe.Fori(0, B) as b:
                    for c in range(SPB):
                        n = b * SPB + c
                        ev.wait(pe, "xn", n, 1)
                        ev.wait(pe, "tr1c", n, 0)
                        for k in range(DC):
                            for t in range(TT):
                                last = pe.transpose(tb[:, k, t * P:(t + 1) * P], xn[:, t, k * P:(k + 1) * P], ident[:])
                        ev.done(last, "tr")
                        ev.wait(pe, "trc", n, 2)
                        ev.wait(pe, "pjc", n, 0)
                        for m in range(DC):
                            for k in range(DC):
                                last = pe.matmul(pb[:, m, :], wqkv0[:, k, m * P:(m + 1) * P], xnT[:, k, :],
                                                 start=(k == 0), stop=(k == DC - 1))
                        ev.done(last, "q")
                        ev.wait(pe, "kvc", n, 0)
                        for m in range(DC):
                            for k in range(DC):
                                pe.matmul(kv[:, m * KN:(m + 1) * KN], wqkv0[:, k, D + m * P:D + (m + 1) * P],
                                          xnT[:, k, ::DIL], start=(k == 0), stop=(k == DC - 1))
                        for half in range(2):
                            for k in range(DC):
                                last = pe.matmul(kv[half * KN:(half + 1) * KN, D:2 * D], xnT[:, k, ::DIL],
                                                 wqkv0[:, k, 2 * D:3 * D], start=(k == 0), stop=(k == DC - 1))
                        ev.done(last, "kv")
                        ev.wait(pe, "kvc", n, 1)
                        ev.wait(pe, "qc", n, 1)

                        def values(p):
                            ev.wait(pe, "wexp", n, p + 1)
                            if p % 2 == 0:
                                ev.wait(pe, "oc", n, p // 2)
                            r = (p % 2) * 2 * HW
                            ev.done(pe.matmul(ob[r:r + 2 * HW, :], vbd[:, p, :], wexp[:, p % 2, :],
                                              start=True, stop=True), "pv")

                        def turn(g):
                            ev.wait(pe, "oc", n, g + 1)
                            ev.wait(pe, "norm", n, g)
                            for t in range(TT):
                                last = pe.transpose(kv[:, t * P:(t + 1) * P], oT[:, g % 2, t * P:(t + 1) * P], ident[:])
                            ev.done(last, "ot")

                        for p in range(NP0 + 1):
                            if p < NP0:
                                m, a = p // (NP0 // DC), 2 * (p % (NP0 // DC))
                                ev.wait(pe, "shift", n, max(p - 1, 0))
                                ev.done(pe.matmul(sc[:, p % 2, :], kbd[:, m, a:a + 2, :].rearrange("p a k -> p (a k)"),
                                                  qT[:, m, :], start=True, stop=True), "s")
                            if 1 <= p <= NP0:
                                values(p - 1)
                            if p >= 3 and p % 2 == 1:
                                turn((p - 3) // 2)
                        turn(3)
                        ev.wait(pe, "quant", n, 1)
                        for f in range(2):
                            if f == 0:
                                ev.wait(pe, "qc", n, 1)
                            ev.wait(pe, "ffc", n, 0)
                            for t in (2 * f, 2 * f + 1):
                                i = 0
                                for w in wf_piece:
                                    for k in range(DC):
                                        last = pe.matmul(pb[:, f, (t % 2) * D:(t % 2 + 1) * D], xq[:, k, t * P:(t + 1) * P],
                                                         w[:, k, :], start=(i == 0), stop=(i == 2 * PIECE - 1))
                                        i += 1
                            ev.done(last, "ff")
                        ev.wait(pe, "norm", n, 4)
                        for k in range(DC):
                            for t in range(TT):
                                last = pe.transpose(tb[:, k, t * P:(t + 1) * P], y[:, t, k * P:(k + 1) * P], ident[:])
                        ev.done(last, "ytr")
                        ev.wait(pe, "ytc", n, 2)
                        for f in range(2):
                            for t in (2 * f, 2 * f + 1):
                                for k in range(DC):
                                    last = pe.matmul(sc[:, f, (t % 2) * D:(t % 2 + 1) * D], yT[:, k, t * P:(t + 1) * P],
                                                     wout0[:, k, :], start=(k == 0), stop=(k == DC - 1))
                            ev.done(last, "so")
                        ev.wait(pe, "xn1", n, 1)
                        for k in range(DC):
                            for t in range(TT):
                                last = pe.transpose(tb[:, k, t * P:(t + 1) * P], xn1[:, t, k * P:(k + 1) * P], ident[:])
                        ev.done(last, "tr1")
                        ev.wait(pe, "tr1c", n, 2)
                        for m in range(2):
                            if m == 0:
                                ev.wait(pe, "ffc", n, 2)
                            else:
                                ev.wait(pe, "pjc", n, 2)
                            for f in range(2):
                                for k in range(DC):
                                    w = (2 * m + f) * P
                                    last = pe.matmul(pb[:, f, :], wqk1[:, k, w:w + P], x1T[:, k, :],
                                                     start=(k == 0), stop=(k == DC - 1))
                            ev.done(last, "pj")
                        for t in range(TT):
                            if t == 0:
                                ev.wait(pe, "sog", n, 2)
                            if t >= 2:
                                ev.wait(pe, "vjc", n, t - 1)
                            for k in range(DC):
                                last = pe.matmul(sc[:, t % 2, 0:D + E], x1T[:, k, t * P:(t + 1) * P], wvg1[:, k, :],
                                                 start=(k == 0), stop=(k == DC - 1))
                            ev.done(last, "vj")
                        ev.wait(pe, "vjc", n, 4)

            @block.scalar
            def _(act):
                act.wait_ge(consts, 16 * NCONST)
                act.wait_ge(ready, 1)
                with act.Fori(0, B) as b:
                    for c in range(SPB):
                        n = b * SPB + c
                        ev.wait(act, "tr", n, 1)
                        ev.wait(act, "kv", n, 0)
                        ev.wait(act, "quant", n, 0)
                        for k in range(DC):
                            ev.done(act.activation(xnT[:, k, :], tb[:, k, :], ACT.Copy), "trc")
                        ev.wait(act, "q", n, 1)
                        ev.done(act.activation(qT[:].rearrange("p k t -> p (k t)"), pb[:].rearrange("p k t -> p (k t)"),
                                               ACT.Copy), "qc")

                        def out_copy(g):
                            ev.wait(act, "pv", n, 2 * g + 2)
                            ev.wait(act, "ot", n, max(g - 1, 0))
                            ev.done(act.activation(oT[:, g % 2, :], ob[:], ACT.Copy), "oc")

                        for p in range(NP0):
                            ev.wait(act, "shift", n, p + 1)
                            ev.wait(act, "pv", n, max(p - 1, 0))
                            ev.done(act.activation(wexp[:, p % 2, :], shifted[:, p % 2, :], ACT.Exp, scale=SCALE), "wexp")
                            if p % 2 == 1:
                                out_copy(p // 2)
                        ev.wait(act, "ytr", n, 1)
                        ev.wait(act, "so", n, 0)
                        for k in range(DC):
                            ev.done(act.activation(yT[:, k, :], tb[:, k, :], ACT.Copy), "ytc")
                        ev.wait(act, "x1", n, 0)
                        for f in range(2):
                            ev.wait(act, "ffc", n, f + 1)
                            ev.done(act.activation(ez[:, 2 * f:2 * f + 2], z[:, 2 * f:2 * f + 2], ACT.Tanh, scale=0.5), "ez")
                        ev.wait(act, "tr1", n, 1)
                        ev.wait(act, "vj", n, 0)
                        for k in range(DC):
                            ev.done(act.activation(x1T[:, k, :], tb[:, k, :], ACT.Copy), "tr1c")
                        for m in range(2):
                            ev.wait(act, "pj", n, m + 1)
                            if m == 0:
                                ev.wait(act, "p3", n, 0)
                            for f in range(2):
                                ev.done(act.activation(qk[:, m, f, :], pb[:, f, :], ACT.Identity,
                                                       bias=bqk1[:, 2 * m + f:2 * m + f + 1]), "pjc")
                        ev.wait(act, "rot", n, 1)
                        ev.wait(act, "qk_out", n, 0)
                        ev.done(act.activation(piece[0][:], rot[:], ACT.Copy), "p1")
                        ev.wait(act, "p2", n, 1)

            @block.vector
            def _(dve):
                ev.start(dve)
                setup = Steps(dve, setup_step, 0)
                dve.wait_ge(consts, 16 * NCONST)
                setup.then(dve.tensor_scalar(wf[:], wf[:], w_scale[:, 0:1], None, ALU.mult))
                setup.settle()
                setup.then(dve.tensor_copy(wf_piece[0][:], wf[:]))
                setup.settle()
                setup.then(dve.tensor_tensor(wf_rest[:], wf[:], wf_piece[0][:], ALU.subtract))
                setup.settle()
                setup.then(dve.tensor_copy(wf_piece[1][:], wf_rest[:]))
                setup.settle()
                setup.then(dve.tensor_tensor(wf_piece[2][:], wf_rest[:], wf_piece[1][:], ALU.subtract))
                setup.then(dve.reciprocal(in_inv[:], in_scale[:]))
                setup.then(dve.memset(vbd[:], 0.0))
                setup.then(dve.memset(v32[:], 1.0))
                setup.settle()
                setup.then(dve.memset(vbd[0:KN, :, HD:HD + 1], 1.0))
                setup.then(dve.memset(vbd[KN:P, :, HW + HD:HW + HD + 1], 1.0))
                setup.settle()
                dve.sem_inc(ready, 1)
                with dve.Fori(0, B) as b:
                    st = Steps(dve, dve_step, b * DVE_STEPS, ev)
                    st.last = ev.sem["vjc"], ev.at("vjc", b * SPB, 0)

                    def norm_tokens(src, dst, i, n, var, rs, done):
                        for t in range(TT):
                            st.then(dve.bn_stats(stats[:, i, t, :], src[:, t, :]))
                        st.settle(passed)
                        for t in range(TT):
                            st.then(dve.bn_aggr(mv[:, i, t, :], stats[:, i, t, :]))
                        st.settle()
                        st.then(dve.tensor_scalar(veps[:, i], mv[:, i, :, 1], LN_EPS, None, ALU.add))
                        st.settle()
                        st.then(dve.tensor_scalar(seed[:, i], veps[:, i].bitcast(I32), 1, None, ALU.arith_shift_right))
                        st.settle()
                        st.mark((dve.tensor_scalar(seed[:, i], seed[:, i], -1.0, float(RSQRT_MAGIC),
                                                          ALU.mult, ALU.add)), var)
                        ev.wait(dve, rs, n, 1)
                        for t in range(TT):
                            last = dve.tensor_scalar(dst[:, t, :], src[:, t, :], mv[:, i, t, 0:1],
                                                     rstd[:, i, t:t + 1], ALU.subtract, ALU.mult)
                            if t == TT - 1:
                                st.mark(last, done)

                    for c in range(SPB):
                        n = b * SPB + c
                        st.step(n)
                        ev.wait(dve, f"x_in{c % 2}", b * (SPB // 2) + c // 2, 1)
                        ev.wait(dve, "tr", n, 0)
                        ev.wait(dve, "rstd", n, 0)
                        st.settle()
                        norm_tokens(x[:, c % 2], xn, 0, n, "var", "rstd", "xn")
                        ev.wait(dve, "kv", n, 1)
                        ev.wait(dve, "pv", n, 0)
                        for m in range(DC):
                            st.then(dve.tensor_tensor(
                                kbd[:, m], kv[:, m * KN:(m + 1) * KN].unsqueeze(1).to_broadcast([P, H // DC, KN]),
                                headmask[:].unsqueeze(2).to_broadcast([P, H // DC, KN]), ALU.mult))
                        heads = kv[:, D:2 * D].rearrange("p (a two d) -> p a two d", two=2, d=HD)
                        st.then(dve.tensor_copy(vbd[0:KN, :, 0:HD], heads[0:KN, :, 0, :]))
                        st.mark((dve.tensor_copy(vbd[KN:P, :, HW:HW + HD], heads[KN:P, :, 1, :])), "kvc")

                        def normalise(g):
                            ev.wait(dve, "ot", n, g + 1)
                            turned = kv[:].rearrange("p (t h w) -> p t h w", t=TT, w=HW)
                            st.then(dve.tensor_scalar(den[:], turned[:, :, :, HD], DEN_EPS, None, ALU.add))
                            st.settle()
                            st.then(dve.reciprocal(rden[:], den[:]))
                            st.settle()
                            if g == 0:
                                ev.wait(dve, "ytr", n, 0)
                            out = y[:, :, g * G * HD:(g + 1) * G * HD].rearrange("p t (h d) -> p t h d", d=HD)
                            st.mark((dve.tensor_tensor(
                                out, turned[:, :, :, 0:HD], rden[:].unsqueeze(3).to_broadcast([P, TT, G, HD]),
                                ALU.mult)), "norm")

                        for p in range(NP0):
                            ev.wait(dve, "s", n, p + 1)
                            ev.wait(dve, "wexp", n, max(p - 1, 0))
                            blocks = sc[:, p % 2, :].rearrange("p (n q) -> p n q", q=BLK)
                            st.then(dve.tensor_reduce(keymax[:, p % 2, :], blocks, AX, ALU.max))
                            st.settle()
                            st.mark(dve.tensor_tensor(
                                shifted[:, p % 2, :].rearrange("p (n q) -> p n q", q=BLK), blocks,
                                keymax[:, p % 2, :].unsqueeze(2).to_broadcast([P, NBLK, BLK]), ALU.subtract), "shift")
                            if p == 0:
                                ev.wait(dve, "trc", n, 2)
                                ev.wait(dve, "ff", n, 0)
                                st.then(dve.tensor_scalar(clipped[:], xnT[:], in_inv[:, 0:1], FP8_MAX, ALU.mult, ALU.min))
                                st.settle()
                                st.then(dve.tensor_scalar(clipped[:], clipped[:], -FP8_MAX, None, ALU.max))
                                st.settle(passed)
                                st.then(dve.tensor_scalar(half8[:], clipped[:], 0.5, None, ALU.mult, saturate=False))
                                st.then(dve.tensor_scalar(coarse[:], clipped[:], 240.0, -240.0, ALU.min, ALU.max,
                                                          saturate=False))
                                st.then(dve.tensor_tensor(square[:], clipped[:], clipped[:], ALU.mult))
                                st.settle()
                                st.then(dve.tensor_scalar(is_big[:], square[:], 2.0 ** -10, None, ALU.is_ge))
                                st.settle(passed)
                                st.then(dve.tensor_copy(xq[:], coarse[:]))
                                st.then(dve.tensor_scalar(doubled[:], half8[:], 2.0, None, ALU.mult))
                                st.settle(passed)
                                st.mark((dve.copy_predicated(xq[:], is_big[:], doubled[:])), "quant")
                            if p >= 3 and p % 2 == 1:
                                normalise((p - 3) // 2)
                        normalise(3)
                        for f in range(2):
                            ev.wait(dve, "ff", n, f + 1)
                            if f == 0:
                                ev.wait(dve, "ez", n, 0)
                            st.mark((dve.scalar_tensor_tensor(
                                out=z[:, 2 * f:2 * f + 2], in0=pb[:, f, :].rearrange("p (t d) -> p t d", d=D),
                                scalar=in_scale[:, 0:1], in1=fbias[:].unsqueeze(1).to_broadcast([P, 2, D]),
                                op0=ALU.mult, op1=ALU.add)), "ffc")
                        ev.wait(dve, "ez", n, 2)
                        st.mark(dve.scalar_tensor_tensor(out=z[:], in0=ez[:], scalar=1.0, in1=z[:],
                                                           op0=ALU.add, op1=ALU.mult), "gate")
                        st.settle()
                        for f in range(2):
                            ev.wait(dve, "so", n, f + 1)
                            st.mark(dve.scalar_tensor_tensor(
                                out=ez[:, 2 * f:2 * f + 2], in0=sc[:, f, :].rearrange("p (t d) -> p t d", d=D),
                                scalar=0.5, in1=z[:, 2 * f:2 * f + 2], op0=ALU.mult, op1=ALU.mult), "sog")
                        st.settle()
                        ev.wait(dve, "x1_out", n, 0)
                        st.mark((dve.tensor_tensor(x1[:], x[:, c % 2], ez[:], ALU.add)), "x1")
                        st.settle()
                        ev.wait(dve, "xn1_out", n, 0)
                        norm_tokens(x1, xn1, 1, n, "var1", "rstd1", "xn1")
                        ev.wait(dve, "pjc", n, 4)
                        cos = rope[:, 0, c * SEG:(c + 1) * SEG].unsqueeze(1).to_broadcast([P, 2, SEG])
                        sin = rope[:, 1, c * SEG:(c + 1) * SEG].unsqueeze(1).to_broadcast([P, 2, SEG])
                        even, odd = qk[:, :, 0, :], qk[:, :, 1, :]
                        ev.wait(dve, "p1", n, 0)
                        st.then(dve.tensor_tensor(rot[:, :, 0, :], even, cos, ALU.mult))
                        st.then(dve.tensor_tensor(prod[:], odd, sin, ALU.mult))
                        st.then(dve.tensor_tensor(rot[:, :, 1, :], even, sin, ALU.mult))
                        st.settle()
                        st.then(dve.tensor_tensor(rot[:, :, 0, :], rot[:, :, 0, :], prod[:], ALU.subtract))
                        st.settle()
                        st.then(dve.tensor_tensor(prod[:], odd, cos, ALU.mult))
                        st.settle()
                        st.mark((dve.tensor_tensor(rot[:, :, 1, :], rot[:, :, 1, :], prod[:], ALU.add)), "rot")
                        ev.wait(dve, "p1", n, 1)
                        ev.wait(dve, "qk_out", n, 0)
                        st.then(dve.tensor_tensor(qk[:], rot[:], piece[0][:], ALU.subtract))
                        st.settle()
                        st.mark((dve.tensor_copy(piece[1][:], qk[:])), "p2")
                        st.settle()
                        st.mark((dve.tensor_tensor(piece[2][:], qk[:], piece[1][:], ALU.subtract)), "p3")
                        for t in range(TT):
                            ev.wait(dve, "vj", n, t + 1)
                            if t == 0:
                                ev.wait(dve, "v_out", n, 0)
                                ev.wait(dve, "l_out", n, 0)
                            st.then(dve.tensor_tensor(
                                v32[:, t, :, 0:HD], sc[:, t % 2, 0:D].rearrange("p (h d) -> p h d", d=HD),
                                bv1[:].rearrange("p (h d) -> p h d", d=HD), ALU.add))
                            st.mark((dve.tensor_copy(logit[:, t, :], sc[:, t % 2, D:D + E])), "vjc")
                    assert st.n == DVE_STEPS, st.n


def route_phase(nc, io, dram, keep):
    with ExitStack() as ctx:
        def sb(name, shape, dt=F32):
            return ctx.enter_context(nc.sbuf_tensor("r_" + name, shape, dt))

        def sem(name):
            return ctx.enter_context(nc.semaphore("r_" + name))

        KT = TOPK * NT
        before = sb("before", [P, P], BF16)
        ones = sb("ones", [P, P], BF16)
        onesf = sb("onesf", [P, KT])
        expert = sb("expert", [P, E])
        spill = sb("spill", [P, TOPK, NT])
        zero = sb("zero", [P, P], I32)
        logit = sb("logit", [P, NT, E])
        score = sb("score", [P, NT, E])
        rest = sb("rest", [P, NT, E])
        best = sb("best", [P, TOPK, NT])
        total = sb("total", [P, NT])
        below = sb("below", [P, NT, E])
        which = sb("which", [P, TOPK, NT])
        hot = sb("hot", [P, TOPK, NT, E])
        hotb = sb("hotb", [P, TOPK * NT * E], BF16)
        count = sb("count", [P, E, KT])
        running = sb("running", [P, E, KT])
        place = sb("place", [P, KT, E])
        loc = sb("loc", [P, KT])
        valid = sb("valid", [P, KT])
        slotf = sb("slotf", [P, KT])
        destf = sb("destf", [P, KT])
        inside = ctx.enter_context(nc.psum_tensor("r_inside", [P, KT * E], F32))
        totals = ctx.enter_context(nc.psum_tensor("r_totals", [P, KT * E], F32))
        loads, zeroed, shifted, weights, hots, prefix, step = map(
            sem, ("loads", "zeroed", "shifted", "weights", "hots", "prefix", "step"))
        table_zero = sem("table_zero")

        with nc.Block() as block:
            @block.sync
            def _(sp):
                for out, in_ in ((before[:], io["c_before"]), (ones[:], io["c_ones"][:, 0:P]),
                                 (expert[:], io["c_expert"]), (spill[:], io["c_spill"]),
                                 (keep["token"][:], io["c_token"]),
                                 (logit[:], dram["logits"].rearrange("(t p) e -> p t e", p=P))):
                    sp.dma_start(out, in_).then_inc(loads, 16)
                sp.wait_ge(zeroed, 1)
                sp.dma_start(dram["table"][0:NSLOT, :].rearrange("(p f) o -> p (f o)", p=P), zero[:]).then_inc(table_zero, 16)
                sp.wait_ge(table_zero, 16)

            @block.tensor
            def _(pe):
                pe.wait_ge(hots, 1)
                for out, w in ((inside, before), (totals, ones)):
                    for f in range(2):
                        cols = slice(f * 512, (f + 1) * 512)
                        last = pe.matmul(out[:, cols], w[:], hotb[:, cols], start=True, stop=True)
                last.then_inc(prefix, 1)

            @block.scalar
            def _(act):
                act.wait_ge(shifted, 1)
                act.activation(score[:], logit[:], ACT.Exp).then_inc(weights, 1)

            @block.vector
            def _(dve):
                steps = [0]

                def then(ins):
                    steps[0] += 1
                    ins.then_inc(step, 1)
                    dve.wait_ge(step, steps[0])

                wide = lambda a: a.unsqueeze(2).to_broadcast([P, NT, E])
                ids = expert[:].unsqueeze(1).to_broadcast([P, NT, E])
                dve.memset(zero[:], 0).then_inc(zeroed, 1)
                then(dve.memset(onesf[:], 1.0))
                dve.wait_ge(loads, 96)
                then(dve.tensor_reduce(total[:], logit[:], AX, ALU.max))
                dve.tensor_tensor(logit[:], logit[:], wide(total[:]), ALU.subtract).then_inc(shifted, 1)
                dve.wait_ge(weights, 1)
                then(dve.tensor_reduce(total[:], score[:], AX, ALU.add))
                then(dve.reciprocal(total[:], total[:]))
                then(dve.tensor_tensor(score[:], score[:], wide(total[:]), ALU.mult))
                for k in range(TOPK):
                    s = score if k == 0 else rest
                    then(dve.tensor_reduce(best[:, k], s[:], AX, ALU.max))
                    then(dve.tensor_tensor(below[:], s[:], wide(best[:, k]), ALU.is_lt))
                    then(dve.scalar_tensor_tensor(out=below[:], in0=below[:], scalar=float(2 * E), in1=ids,
                                                  op0=ALU.mult, op1=ALU.add))
                    then(dve.tensor_reduce(which[:, k], below[:], AX, ALU.min))
                    then(dve.tensor_tensor(hot[:, k], ids, wide(which[:, k]), ALU.is_equal))
                    if k == 0:
                        then(dve.scalar_tensor_tensor(out=rest[:], in0=hot[:, k], scalar=-2.0, in1=score[:],
                                                      op0=ALU.mult, op1=ALU.add))
                dve.tensor_copy(hotb[:], hot[:].rearrange("p k t e -> p (k t e)")).then_inc(hots, 1)
                then(dve.tensor_tensor(total[:], best[:, 0], best[:, 1], ALU.add))
                then(dve.reciprocal(total[:], total[:]))
                gate = keep["gate"]
                for k in range(TOPK):
                    then(dve.tensor_tensor(gate[:, k], best[:, k], total[:], ALU.mult))
                dve.wait_ge(prefix, 1)
                by_expert = totals[:].rearrange("p (n e) -> p e n", e=E)
                then(dve.tensor_copy(count[:], by_expert))
                for e in range(E):
                    then(dve.tensor_tensor_scan(running[:, e], onesf[:], count[:, e], 0.0, ALU.mult, ALU.add))
                then(dve.tensor_tensor(running[:], running[:], count[:], ALU.subtract))
                then(dve.tensor_tensor(place[:], inside[:].rearrange("p (n e) -> p n e", e=E),
                                       running[:].rearrange("p e n -> p n e"), ALU.add))
                then(dve.tensor_tensor(place[:], place[:], hot[:].rearrange("p k t e -> p (k t) e"), ALU.mult))
                then(dve.tensor_reduce(loc[:], place[:], AX, ALU.add))
                flat = lambda a: a[:].rearrange("p k t -> p (k t)")
                then(dve.tensor_scalar(valid[:], loc[:], float(CAP), None, ALU.is_lt))
                then(dve.tensor_scalar(loc[:], loc[:], float(CAP - 1), None, ALU.min))
                then(dve.scalar_tensor_tensor(out=slotf[:], in0=flat(which), scalar=float(CAP), in1=loc[:],
                                              op0=ALU.mult, op1=ALU.add))
                then(dve.tensor_copy(flat(keep["slot"]), slotf[:]))
                then(dve.tensor_tensor(flat(gate), flat(gate), valid[:], ALU.mult))
                then(dve.tensor_tensor(destf[:], slotf[:], flat(spill), ALU.subtract))
                then(dve.tensor_tensor(destf[:], destf[:], valid[:], ALU.mult))
                then(dve.tensor_tensor(destf[:], destf[:], flat(spill), ALU.add))
                then(dve.tensor_copy(flat(keep["dest"]), destf[:]))


def attend_phase(nc, io, dram, keep):
    with ExitStack() as ctx:
        def sb(name, shape, dt=F32):
            return ctx.enter_context(nc.sbuf_tensor("at_" + name, shape, dt))

        def ps(name, shape, dt=F32):
            return ctx.enter_context(nc.psum_tensor("at_" + name, shape, dt))

        NBUF, NE = 3, 2 * G
        ident = sb("ident", [P, P])
        identb = sb("identb", [P, P], BF16)
        mask_q = sb("mask_q", [P, P], BF16)
        mask_k = sb("mask_k", [P, P], BF16)
        qs = sb("qs", [ROWS, NBUF, G, M], BF16)
        ks = sb("ks", [ROWS, NBUF, G, M], BF16)
        vs = sb("vs", [P, NBUF, NQT, G * HW])
        ex = sb("ex", [P, NE, 2 * SEG])
        part = sb("part", [P, G * NQT, SPB])
        negmax = sb("negmax", [P, G * NQT])
        restT = sb("restT", [G * NQT, P])
        mT = sb("mT", [G * NQT, PIECE, P], BF16)
        osb = sb("osb", [P, SEG])
        rden = sb("rden", [P, TT, G])
        yout = sb("yout", [P, 2, TT, G * HD])
        idx = sb("idx", [P, 2], I32)
        tok = sb("tok", [P, 2], I32)
        p1 = ps("p1", [P, 2, SEG])
        st = ps("st", [P, 2, 2 * SEG])
        ob = ps("ob", [P, SEG])
        misc = ps("misc", [P, SEG])

        steps = []
        for qc in range(SPB):
            first = TT * qc
            for j in range(0, first, 2):
                steps.append((qc, [(j, 0, SEG), (j + 1, SEG, SEG)]))
            steps.append((qc, [(first, 0, SEG), (first + 1, SEG, SEG - P), (first + 3, 2 * SEG - P, P)]))
            steps.append((qc, [(first + 2, 0, SEG - 2 * P)]))
        NS = len(steps)
        NU = NS * G
        last_of = [max(s for s in range(NS) if steps[s][0] == qc) for qc in range(SPB)]
        chunks = [(h, qt, ch) for h in range(G) for qt in range(NQT) for ch in range(qt // TT + 1)]
        NC = len(chunks)
        PER = NC // NU
        assert PER * NU == NC
        counts = dict(s1=NC, mx=NC, neg=1, negT=1, mT=1, m_in=PIECE, st=NU, ex=NU, pv=NS, oc=SPB, ot=SPB,
                      norm=SPB, y_out0=SPB // 2, y_out1=SPB // 2, rden=SPB)
        for i in range(NBUF):
            counts[f"in{i}"] = 1
        NLOAD = 2 * 12 + 2
        ev = Events(nc, ctx, "at", counts, {"m_in", "y_out0", "y_out1"})
        for i in range(NBUF):
            ev.unit[f"in{i}"] = 16 * NLOAD
        consts = ctx.enter_context(nc.semaphore("at_consts"))
        ready = ctx.enter_context(nc.semaphore("at_ready"))
        passed = ctx.enter_context(nc.semaphore("at_passed"))
        setup = ctx.enter_context(nc.semaphore("at_setup"))
        mstep = ctx.enter_context(nc.semaphore("at_mstep"))
        scat_copy = ctx.enter_context(nc.semaphore("at_scat_copy"))
        scattered = ctx.enter_context(nc.semaphore("at_scattered"))

        def group_loop(e, body):
            with e.Fori(0, (NGROUPS - 1) // NBUF) as i:
                for r in range(NBUF):
                    body(i * NBUF + r, r, i, True)
            body(NGROUPS - 1, (NGROUPS - 1) % NBUF, (NGROUPS - 1) // NBUF, False)

        def turn_of(g_const, i, r):
            return i + r // NBUF

        with nc.Block() as block:
            @block.sync
            def _(sp):
                for out, in_ in ((ident[:], io["c_ident"]), (identb[:], io["c_identb"]),
                                 (mask_q[:], io["c_mask_q"]), (mask_k[:], io["c_mask_k"])):
                    sp.dma_start(out, in_).then_inc(consts, 16)
                for rows in (qs, ks):
                    for i in range(NBUF):
                        sp.dma_start(rows[STACK:ROWS, i], io["c_ones"][0:PIECE, :].unsqueeze(1).to_broadcast([PIECE, G, M])).then_inc(consts, 16)
                sp.wait_ge(ready, 1)

                def load(g, r):
                    for m, rows, pieces in ((0, qs, Q_PIECES), (1, ks, K_PIECES)):
                        for s, i in enumerate(pieces):
                            for f in range(2):
                                at = s * HD + f * (HD // 2)
                                src = dram["qk"][m, g, i, f, :, :].rearrange("o (h j) t -> j (o h) t", j=HD // 2)
                                sp.dma_start(rows[at:at + HD // 2, r], src).then_inc(ev.sem[f"in{r}"], 16)
                    for f in range(2):
                        src = dram["v"][g, f * (M // 2):(f + 1) * (M // 2), :].rearrange("o (t p) w -> p (o t) w", p=P)
                        sp.dma_start(vs[:, r, f * (NQT // 2):(f + 1) * (NQT // 2)], src).then_inc(ev.sem[f"in{r}"], 16)

                def maxima(g, r):
                    ev.wait(sp, "mT", g, 1)
                    for i in range(PIECE):
                        dst = qs[STACK + i:STACK + i + 1, r].rearrange("o h (t p) -> o (h t) p", p=P)
                        ev.done(sp.dma_start(dst, mT[:, i, :]), "m_in")

                def group(g, r, more):
                    for qc in range(SPB):
                        ev.wait(sp, "norm", g, qc + 1)
                        dst = dram["y"][bass.ds(g, 1), qc * SEG:(qc + 1) * SEG, :]
                        ev.done(sp.dma_start(dst.rearrange("o (t p) d -> p (o t) d", p=P), yout[:, qc % 2]), f"y_out{qc % 2}")

                load(slice(0, 1), 0)
                load(slice(1, 2), 1)
                maxima(0, 0)

                def turn(i, loads):
                    for r in range(NBUF):
                        g = i * NBUF + r
                        if r < loads:
                            ev.wait(sp, "pv", g, 0)
                            sp.sem_inc(passed, 1)
                            load(bass.ds(g + 2, 1), (r + 2) % NBUF)
                        group(g, r, True)
                        maxima(g + 1, (r + 1) % NBUF)

                NTURN = (NGROUPS - 1) // NBUF
                with sp.Fori(0, NTURN - 1) as i:
                    turn(i, NBUF)
                turn(NTURN - 1, NBUF - 1)
                group(NGROUPS - 1, 0, False)
                for k in range(2):
                    sp.wait_ge(ev.sem[f"y_out{k}"], 16 * (NGROUPS * SPB // 2 + 1))

            @block.gpsimd
            def _(pool):
                pool.wait_ge(ready, 1)
                def scatter(i):
                    pool.tensor_copy(idx[:], keep["dest"][:, :, bass.ds(i, 1)].rearrange("p k o -> p (k o)")).then_inc(scat_copy, 1)
                    pool.tensor_copy(tok[:, 0:1], keep["token"][:, bass.ds(i, 1)]).then_inc(scat_copy, 1)
                    pool.wait_ge(scat_copy, 2 * i + 2)
                    pool.sem_inc(passed, 1)
                    for k in range(TOPK):
                        pool.indirect_dma_start(
                            out=dram["table"], out_offset=bass.IndirectOffsetOnAxis(ap=idx[:, k:k + 1], axis=0),
                            in_=tok[:, 0:1], in_offset=None).then_inc(scattered, 16)

                scatter(0)
                with pool.Fori(1, NT) as i:
                    pool.wait_ge(scattered, 16 * TOPK * i)
                    pool.sem_inc(passed, 1)
                    scatter(i)
                pool.wait_ge(scattered, 16 * TOPK * NT)

            @block.tensor
            def _(pe):
                pe.wait_ge(consts, 16 * (4 + 2 * NBUF))
                pe.wait_ge(ready, 1)

                def row_scores(g, r, n):
                    h, qt, ch = chunks[n]
                    w = min(SEG, (qt + 1) * P - ch * SEG)
                    diag = ch == qt // TT
                    ev.wait(pe, "mx", g, max(n - 1, 0))
                    out = p1[:, n % 2, 0:w]
                    last = pe.matmul(out, qs[0:STACK, r, h, qt * P:(qt + 1) * P], ks[0:STACK, r, h, ch * SEG:ch * SEG + w],
                                     start=True, stop=not diag)
                    if diag:
                        last = pe.matmul(out[:, w - P:w], identb[:], mask_q[:], start=False, stop=True)
                    ev.done(last, "s1")

                def turn_maxima(g):
                    ev.wait(pe, "neg", g, 1)
                    pe.sem_inc(passed, 1)
                    ev.done(pe.transpose(misc[0:G * NQT, 0:P], negmax[:], ident[:]), "negT")

                def key_scores(g, r, u):
                    s, h = u // G, u % G
                    qc, tiles = steps[s]
                    ev.wait(pe, "ex", g, max(u - 1, 0))
                    for kt, at, w in tiles:
                        diag = kt >= TT * qc
                        out = st[:, u % 2, at:at + w]
                        q0 = (qc + 1) * SEG - w
                        last = pe.matmul(out, ks[:, r, h, kt * P:(kt + 1) * P], qs[:, r, h, q0:q0 + w],
                                         start=True, stop=not diag)
                        if diag:
                            last = pe.matmul(out[:, 0:P], identb[:], mask_k[:], start=False, stop=True)
                    ev.done(last, "st")

                def values(g, r, s):
                    qc, tiles = steps[s]
                    ev.wait(pe, "ex", g, G * s + G)
                    if s == 0 or steps[s - 1][0] != qc:
                        ev.wait(pe, "oc", g, qc)
                    for kt, at, w in tiles:
                        for h in range(G):
                            last = pe.matmul(ob[h * HW:(h + 1) * HW, SEG - w:SEG], vs[:, r, kt, h * HW:(h + 1) * HW],
                                             ex[:, (G * s + h) % NE, at:at + w], start=(kt == 0),
                                             stop=(s == last_of[qc] and kt == tiles[-1][0]),
                                             skip_group_check=True)
                    ev.done(last, "pv")

                def turn(g, qc):
                    ev.wait(pe, "oc", g, qc + 1)
                    ev.wait(pe, "norm", g, qc)
                    for t in range(TT):
                        last = pe.transpose(misc[:, t * P:(t + 1) * P], osb[:, t * P:(t + 1) * P], ident[:])
                    ev.done(last, "ot")

                def group(g, r, i, more):
                    ev.wait(pe, "m_in", g, PIECE)
                    if more:
                        ev.wait(pe, f"in{(r + 1) % NBUF}", i + (r + 1) // NBUF, 1)
                    for u in range(NU):
                        s, h = u // G, u % G
                        key_scores(g, r, u)
                        if more:
                            for n in range(PER * u, PER * (u + 1)):
                                row_scores(g + 1, (r + 1) % NBUF, n)
                        if h == 1 and s >= 1:
                            values(g, r, s - 1)
                        if h == 3 and s >= 1 and s - 1 in last_of:
                            turn(g, last_of.index(s - 1))
                    values(g, r, NS - 1)
                    turn(g, SPB - 1)
                    if more:
                        ev.wait(pe, "norm", g, SPB)
                        turn_maxima(g + 1)
                    
                ev.wait(pe, "in0", 0, 1)
                for n in range(NC):
                    row_scores(0, 0, n)
                turn_maxima(0)
                group_loop(pe, group)

            @block.scalar
            def _(act):
                act.wait_ge(ready, 1)

                def out_copy(g, qc):
                    ev.wait(act, "pv", g, last_of[qc] + 1)
                    ev.wait(act, "ot", g, qc)
                    ev.done(act.activation(osb[:], ob[:], ACT.Copy), "oc")

                def group(g, r, i, more):
                    for u in range(NU):
                        s, h = u // G, u % G
                        width = steps[s][1][-1][1] + steps[s][1][-1][2]
                        ev.wait(act, "st", g, u + 1)
                        if s >= 2:
                            ev.wait(act, "pv", g, s - 1)
                        elif h == 0 and s == 0:
                            ev.wait(act, "pv", g, 0)
                        ev.done(act.activation(ex[:, u % NE, 0:width], st[:, u % 2, 0:width], ACT.Exp, scale=SCALE), "ex")
                        if h == 1 and s >= 1 and s - 1 in last_of:
                            out_copy(g, last_of.index(s - 1))
                    out_copy(g, SPB - 1)

                group_loop(act, group)

            @block.vector
            def _(dve):
                ev.start(dve)
                dve.memset(part[:], LOWEST).then_inc(setup, 1)
                dve.wait_ge(setup, 1)
                dve.sem_inc(ready, 1)

                def chunk_max(g, n):
                    h, qt, ch = chunks[n]
                    w = min(SEG, (qt + 1) * P - ch * SEG)
                    ev.wait(dve, "s1", g, n + 1)
                    at = h * NQT + qt
                    ev.done(dve.tensor_reduce(part[:, at, ch:ch + 1], p1[:, n % 2, 0:w], AX, ALU.max), "mx")

                def negate(g):
                    ev.wait(dve, "mx", g, NC)
                    dve.tensor_reduce(negmax[:], part[:], AX, ALU.max).then_inc(mstep, 1)
                    dve.wait_ge(mstep, 4 * g + 1)
                    ev.done(dve.tensor_scalar(negmax[:], negmax[:], -1.0, None, ALU.mult), "neg")

                def split(g):
                    ev.wait(dve, "negT", g, 1)
                    ev.wait(dve, "m_in", g, 0)
                    src = misc[0:G * NQT, 0:P]
                    dve.tensor_copy(mT[:, 0], src).then_inc(mstep, 1)
                    dve.wait_ge(mstep, 4 * g + 2)
                    dve.tensor_tensor(restT[:], src, mT[:, 0], ALU.subtract).then_inc(mstep, 1)
                    dve.wait_ge(mstep, 4 * g + 3)
                    dve.tensor_copy(mT[:, 1], restT[:]).then_inc(mstep, 1)
                    dve.wait_ge(mstep, 4 * g + 4)
                    ev.done(dve.tensor_tensor(mT[:, 2], restT[:], mT[:, 1], ALU.subtract), "mT")

                def normalise(g, qc):
                    ev.wait(dve, "ot", g, qc + 1)
                    turned = misc[:].rearrange("p (t h w) -> p t h w", t=TT, w=HW)
                    ev.wait(dve, f"y_out{qc % 2}", g, qc // 2)
                    ev.done(dve.reciprocal(rden[:], turned[:, :, :, HD]), "rden")
                    ev.wait(dve, "rden", g, qc + 1)
                    out = yout[:, qc % 2].rearrange("p t (h d) -> p t h d", d=HD)
                    ev.done(dve.tensor_tensor(out, turned[:, :, :, 0:HD], rden[:].unsqueeze(3).to_broadcast([P, TT, G, HD]),
                                              ALU.mult), "norm")

                def group(g, r, i, more):
                    for u in range(NU):
                        s, h = u // G, u % G
                        if more:
                            for n in range(PER * u, PER * (u + 1)):
                                chunk_max(g + 1, n)
                        if h == 3 and s >= 1 and s - 1 in last_of:
                            normalise(g, last_of.index(s - 1))
                    if more:
                        negate(g + 1)
                    normalise(g, SPB - 1)
                    if more:
                        split(g + 1)

                for n in range(NC):
                    chunk_max(0, n)
                negate(0)
                split(0)
                group_loop(dve, group)


def experts_phase(nc, io, dram):
    with ExitStack() as ctx:
        def sb(name, shape, dt=F32):
            return ctx.enter_context(nc.sbuf_tensor("e_" + name, shape, dt))

        def ps(name, shape, dt=F32):
            return ctx.enter_context(nc.psum_tensor("e_" + name, shape, dt))

        HC = HID // P
        NCH = CAP // SEG
        ident = sb("ident", [P, P])
        b1 = sb("b1", [P, E, HC])
        b2 = sb("b2", [P, E, D])
        w1 = sb("w1", [P, 2, DC, HID])
        w2 = sb("w2", [P, 2, HC, D])
        table = sb("table", [P, 2, CAP // P], I32)
        xg = sb("xg", [P, 2, TT, D])
        xT = sb("xT", [P, 2, DC, SEG])
        hT = sb("hT", [P, 2, HC, SEG])
        og = sb("og", [P, 2, TT, D])
        b2now = sb("b2now", [P, 2, D])
        b1now = sb("b1now", [P, 2, HC])
        tb = ps("tb", [P, DC, SEG])
        hb = ps("hb", [P, 2, SEG])
        ob = ps("ob", [P, 2, SEG])

        TURN = 2 * NCH
        counts = dict(tr=1, trc=DC, h=HC, relu=HC // 2, relu2=HC // 2, o=TT, oc=TT, out0=1, out1=1)
        ev = Events(nc, ctx, "e", counts, {"out0", "out1"})
        wev = Events(nc, ctx, "ew", dict(w0=2, w1=2, t0=1, t1=1, now=4, g0=TT, g1=TT), {"w0", "w1", "t0", "t1", "g0", "g1"}, {"g0", "g1"})
        consts = ctx.enter_context(nc.semaphore("e_consts"))
        ready = ctx.enter_context(nc.semaphore("e_ready"))
        passed = ctx.enter_context(nc.semaphore("e_passed"))

        with nc.Block() as block:
            @block.sync
            def _(sp):
                for out, in_ in ((ident[:], io["c_ident"]), (b1[:], io["b1T"]), (b2[:], io["b2"].partition_broadcast(P))):
                    sp.dma_start(out, in_).then_inc(consts, 16)
                sp.wait_ge(ready, 1)

                def load(i, u, chunks_before):
                    ev.wait(sp, "o", chunks_before, 0)
                    sp.sem_inc(passed, 1)
                    e = bass.ds(2 * i + u, 1)
                    wev.done(sp.dma_start(table[:, u], dram["table"][bass.ds((2 * i + u) * CAP, CAP), :].rearrange("(p c) o -> p (c o)", p=P)), f"t{u}")
                    wev.done(sp.dma_start(w1[:, u], io["w1"][e].rearrange("o (k p) h -> p (o k) h", p=P)), f"w{u}")
                    wev.done(sp.dma_start(w2[:, u], io["w2"][e].rearrange("o (k p) d -> p (o k) d", p=P)), f"w{u}")

                with sp.Fori(0, E // 2) as i:
                    for u in range(2):
                        load(i, u, i * TURN + u * NCH - NCH if u else i * TURN)
                    for u in range(2):
                        for q in range(NCH):
                            n = i * TURN + u * NCH + q
                            ev.wait(sp, "oc", n, TT)
                            sp.sem_inc(passed, 1)
                            rows = dram["eo"][bass.ds((2 * i + u) * CAP, CAP), :].rearrange("(p c) d -> p c d", p=P)
                            ev.done(sp.dma_start(rows[:, q * TT:(q + 1) * TT, :], og[:, q % 2]), f"out{q % 2}")
                for k in range(2):
                    sp.wait_ge(ev.sem[f"out{k}"], 16 * (E * NCH // 2 + 1))

            @block.gpsimd
            def _(pool):
                pool.wait_ge(ready, 1)
                with pool.Fori(0, E // 2) as i:
                    for u in range(2):
                        wev.wait(pool, f"t{u}", i, 1)
                        for q in range(NCH):
                            n = i * TURN + u * NCH + q
                            ev.wait(pool, "tr", n - 1 if u or q else n, 0)
                            pool.sem_inc(passed, 1)
                            for t in range(TT):
                                c = q * TT + t
                                pool.indirect_dma_start(
                                    out=xg[:, q % 2, t, :], out_offset=None, in_=dram["xn1"],
                                    in_offset=bass.IndirectOffsetOnAxis(ap=table[:, u, c:c + 1], axis=0)
                                ).then_inc(wev.sem[f"g{q % 2}"], 16)

            @block.tensor
            def _(pe):
                pe.wait_ge(consts, 48)
                pe.wait_ge(ready, 1)

                def turn(i, c):
                    n = i * TURN + c
                    wev.wait(pe, f"g{c % 2}", i * (TURN // 2) + c // 2, TT)
                    ev.wait(pe, "trc", n, 0)
                    for k in range(DC):
                        for t in range(TT):
                            last = pe.transpose(tb[:, k, t * P:(t + 1) * P], xg[:, c % 2, t, k * P:(k + 1) * P], ident[:])
                    ev.done(last, "tr")

                with pe.Fori(0, E // 2) as i:
                    turn(i, 0)
                    for c in range(TURN):
                        n = i * TURN + c
                        u = c // NCH
                        if c % NCH == 0:
                            wev.wait(pe, f"w{u}", i, 2)
                        ev.wait(pe, "trc", n, DC)
                        for m in range(HC):
                            ev.wait(pe, ("relu", "relu2")[m % 2], n, m // 2)
                            for k in range(DC):
                                last = pe.matmul(hb[:, m % 2, :], w1[:, u, k, m * P:(m + 1) * P], xT[:, c % 2, k, :],
                                                 start=(k == 0), stop=(k == DC - 1))
                            ev.done(last, "h")
                        if c < TURN - 1:
                            turn(i, c + 1)
                        ev.wait(pe, "relu", n, HC // 2)
                        ev.wait(pe, "relu2", n, HC // 2)
                        for t in range(TT):
                            ev.wait(pe, "oc", n, max(t - 1, 0))
                            for m in range(HC):
                                last = pe.matmul(ob[:, t % 2, 0:D], hT[:, c % 2, m, t * P:(t + 1) * P], w2[:, u, m, :],
                                                 start=(m == 0), stop=(m == HC - 1))
                            ev.done(last, "o")

            @block.scalar
            def _(act):
                act.wait_ge(consts, 48)
                act.wait_ge(ready, 1)
                with act.Fori(0, E // 2) as i:
                    for c in range(TURN):
                        n = i * TURN + c
                        u = c // NCH
                        if c % NCH == 0:
                            wev.wait(act, "now", i, 2 * u + 2)
                        ev.wait(act, "tr", n, 1)
                        ev.wait(act, "h", n, 0)
                        for k in range(DC):
                            ev.done(act.activation(xT[:, c % 2, k, :], tb[:, k, :], ACT.Copy), "trc")
                        for m in range(0, HC, 2):
                            ev.wait(act, "h", n, m + 1)
                            if m == 0:
                                ev.wait(act, "o", n, 0)
                            ev.done(act.activation(hT[:, c % 2, m, :], hb[:, 0, :], ACT.Relu, bias=b1now[:, u, m:m + 1]), "relu")

            @block.vector
            def _(dve):
                ev.start(dve)
                wev.start(dve)
                dve.wait_ge(consts, 48)
                dve.sem_inc(ready, 1)
                with dve.Fori(0, E // 2) as i:
                    for c in range(TURN):
                        n = i * TURN + c
                        u = c // NCH
                        if c % NCH == 0:
                            ev.wait(dve, "relu", n, 0)
                            dve.sem_inc(passed, 1)
                            wev.done(dve.tensor_copy(b1now[:, u:u + 1], b1[:, bass.ds(2 * i + u, 1)]), "now")
                            wev.done(dve.tensor_copy(b2now[:, u:u + 1], b2[:, bass.ds(2 * i + u, 1)]), "now")
                            wev.wait(dve, "now", i, 2 * u + 2)
                        for m in range(1, HC, 2):
                            ev.wait(dve, "h", n, m + 1)
                            if m == 1:
                                ev.wait(dve, "o", n, 0)
                            ev.done(dve.tensor_scalar(hT[:, c % 2, m, :], hb[:, 1, :], b1now[:, u, m:m + 1], 0.0,
                                                      ALU.add, ALU.max), "relu2")
                        for t in range(TT):
                            ev.wait(dve, "o", n, t + 1)
                            if t == 0:
                                ev.wait(dve, f"out{c % 2}", i * (TURN // 2) + c // 2, 0)
                            ev.done(dve.tensor_tensor(og[:, c % 2, t, :], ob[:, t % 2, 0:D], b2now[:, u], ALU.add), "oc")


def combine_phase(nc, io, dram, keep, out):
    with ExitStack() as ctx:
        def sb(name, shape, dt=F32):
            return ctx.enter_context(nc.sbuf_tensor("f_" + name, shape, dt))

        def ps(name, shape, dt=F32):
            return ctx.enter_context(nc.psum_tensor("f_" + name, shape, dt))

        ident = sb("ident", [P, P])
        wo = sb("wo", [P, DC, D])
        bo = sb("bo", [P, D])
        y = sb("y", [P, 2, TT, NG, G * HD])
        x1 = sb("x1", [P, 2, TT, D])
        slot = sb("slot", [P, 2, TOPK, TT], I32)
        gate = sb("gate", [P, 2, TOPK, TT])
        rows = sb("rows", [P, 2, TOPK, TT, D])
        yT = sb("yT", [P, DC, SEG])
        z = sb("z", [P, TT, D])
        th = sb("th", [P, TT, D])
        s = sb("s", [P, TT, D])
        res = sb("res", [P, 2, TT, D])
        tb = ps("tb", [P, DC, SEG])
        sc = ps("sc", [P, 2, SEG])

        counts = dict(y_in=1, slot=2, rows=TOPK * TT, tr=1, trc=DC, so=2, sb=2, z=1, th=1, res=1, out=1)
        inputs = {f"{a}{k}": c for a, c in (("in", NG + 1), ("rows", TOPK * TT), ("out", 1)) for k in range(2)}
        ev = Events(nc, ctx, "f", dict(slot=2, tr=1, trc=DC, so=2, sb=2, z=1, th=1, res=1), set())
        par = Events(nc, ctx, "fp", inputs, set(inputs), {"rows0", "rows1"})
        consts = ctx.enter_context(nc.semaphore("f_consts"))
        ready = ctx.enter_context(nc.semaphore("f_ready"))
        passed = ctx.enter_context(nc.semaphore("f_passed"))
        dve_step = ctx.enter_context(nc.semaphore("f_dve_step"))
        DVE_STEPS = SPB * 9
        out_rows = out.rearrange("b m d -> (b m) d")

        with nc.Block() as block:
            @block.sync
            def _(sp):
                for dst, src in ((ident[:], io["c_ident"]), (wo[:], io["wo1T"].rearrange("(k p) n -> p k n", p=P)),
                                 (bo[:], io["bo1"].partition_broadcast(P))):
                    sp.dma_start(dst, src).then_inc(consts, 16)
                sp.wait_ge(ready, 1)
                with sp.Fori(0, B) as b:
                    for c in range(SPB):
                        n = b * SPB + c
                        for ahead in range(c if c == 0 else c + 1, min(c + 2, SPB)):
                            ev.wait(sp, "res", n, 0)
                            k = ahead % 2
                            for hg in range(NG):
                                src = dram["y"][bass.ds(b * NG + hg, 1), ahead * SEG:(ahead + 1) * SEG, :]
                                sp.dma_start(y[:, k, :, hg, :], src.rearrange("o (t p) d -> p (o t) d", p=P)).then_inc(par.sem[f"in{k}"], 16)
                            par.done(sp.dma_start(x1[:, k], dram["x1"][bass.ds(b * M + ahead * SEG, SEG), :].rearrange("(t p) d -> p t d", p=P)), f"in{k}")
                        ev.wait(sp, "res", n, 1)
                        par.done(sp.dma_start(out_rows[bass.ds(b * M + c * SEG, SEG), :].rearrange("(t p) d -> p t d", p=P),
                                              res[:, c % 2]), f"out{c % 2}")
                for k in range(2):
                    sp.wait_ge(par.sem[f"out{k}"], 16 * (NSEG // 2 + 1))

            @block.gpsimd
            def _(pool):
                pool.wait_ge(ready, 1)
                with pool.Fori(0, B) as b:
                    for c in range(SPB):
                        n = b * SPB + c
                        ev.wait(pool, "slot", n, 2)
                        ev.wait(pool, "z", n - 1 if c else n, 0)
                        pool.sem_inc(passed, 1)
                        for k in range(TOPK):
                            for t in range(TT):
                                pool.indirect_dma_start(
                                    out=rows[:, c % 2, k, t, :], out_offset=None, in_=dram["eo"],
                                    in_offset=bass.IndirectOffsetOnAxis(ap=slot[:, c % 2, k, t:t + 1], axis=0)
                                ).then_inc(par.sem[f"rows{c % 2}"], 16)

            @block.tensor
            def _(pe):
                pe.wait_ge(consts, 48)
                pe.wait_ge(ready, 1)
                with pe.Fori(0, B) as b:
                    for c in range(SPB):
                        n = b * SPB + c
                        par.wait(pe, f"in{c % 2}", b * (SPB // 2) + c // 2, NG + 1)
                        ev.wait(pe, "trc", n, 0)
                        ysrc = y[:, c % 2].rearrange("p t g d -> p t (g d)")
                        for k in range(DC):
                            for t in range(TT):
                                last = pe.transpose(tb[:, k, t * P:(t + 1) * P], ysrc[:, t, k * P:(k + 1) * P], ident[:])
                        ev.done(last, "tr")
                        ev.wait(pe, "trc", n, DC)
                        ev.wait(pe, "sb", n, 0)
                        for f in range(2):
                            for t in (2 * f, 2 * f + 1):
                                for k in range(DC):
                                    last = pe.matmul(sc[:, f, (t % 2) * D:(t % 2 + 1) * D], yT[:, k, t * P:(t + 1) * P],
                                                     wo[:, k, :], start=(k == 0), stop=(k == DC - 1))
                            ev.done(last, "so")

            @block.scalar
            def _(act):
                act.wait_ge(ready, 1)
                with act.Fori(0, B) as b:
                    for c in range(SPB):
                        n = b * SPB + c
                        ev.wait(act, "tr", n, 1)
                        ev.wait(act, "so", n, 0)
                        for k in range(DC):
                            ev.done(act.activation(yT[:, k, :], tb[:, k, :], ACT.Copy), "trc")
                        ev.wait(act, "z", n, 1)
                        ev.wait(act, "res", n, 0)
                        ev.done(act.activation(th[:], z[:], ACT.Tanh, scale=0.5), "th")

            @block.vector
            def _(dve):
                ev.start(dve)
                par.start(dve)
                dve.wait_ge(consts, 48)
                dve.sem_inc(ready, 1)
                with dve.Fori(0, B) as b:
                    st = Steps(dve, dve_step, b * DVE_STEPS, ev)
                    st.last = ev.sem["res"], ev.at("res", b * SPB, 0)

                    def places(c):
                        cols = bass.ds(b * (M // P) + c * TT, TT)
                        n = b * SPB + c
                        ev.wait(dve, "z", n - 1 if c else n, 0)
                        dve.sem_inc(passed, 1)
                        ev.done(dve.tensor_copy(slot[:, c % 2], keep["slot"][:, :, cols]), "slot")
                        ev.done(dve.tensor_copy(gate[:, c % 2], keep["gate"][:, :, cols]), "slot")

                    places(0)
                    for c in range(SPB):
                        n = b * SPB + c
                        st.step(n)
                        if c + 1 < SPB:
                            places(c + 1)
                        k = c % 2
                        par.wait(dve, f"rows{k}", b * (SPB // 2) + c // 2, TOPK * TT)
                        ev.wait(dve, "slot", n, 2)
                        ev.wait(dve, "th", n, 0)
                        for t in range(TT):
                            st.then(dve.tensor_scalar(s[:, t], rows[:, k, 1, t], gate[:, k, 1, t:t + 1], None, ALU.mult))
                        st.settle()
                        for t in range(TT):
                            last = dve.scalar_tensor_tensor(out=z[:, t], in0=rows[:, k, 0, t], scalar=gate[:, k, 0, t:t + 1],
                                                            in1=s[:, t], op0=ALU.mult, op1=ALU.add)
                            st.mark(last, "z") if t == TT - 1 else st.then(last)
                        st.settle()
                        for f in range(2):
                            ev.wait(dve, "so", n, f + 1)
                            st.mark(dve.tensor_tensor(s[:, 2 * f:2 * f + 2], sc[:, f, :].rearrange("p (t d) -> p t d", d=D),
                                                        bo[:].unsqueeze(1).to_broadcast([P, 2, D]), ALU.add), "sb")
                        ev.wait(dve, "th", n, 1)
                        st.then(dve.scalar_tensor_tensor(out=z[:], in0=th[:], scalar=1.0, in1=z[:], op0=ALU.add, op1=ALU.mult))
                        st.settle()
                        st.then(dve.scalar_tensor_tensor(out=z[:], in0=z[:], scalar=0.5, in1=s[:], op0=ALU.mult, op1=ALU.mult))
                        st.settle()
                        par.wait(dve, f"out{k}", b * (SPB // 2) + c // 2, 0)
                        par.wait(dve, f"in{k}", b * (SPB // 2) + c // 2, NG + 1)
                        st.mark(dve.tensor_tensor(res[:, k], z[:], x1[:, k], ALU.add), "res")
                        st.settle()
                    assert st.n == DVE_STEPS, st.n


def build(nc, io, out):
    with ExitStack() as ctx:
        dram = {name: nc.dram_tensor("s_" + name, shape, dt, kind="Internal").ap() for name, shape, dt in SCRATCH}
        keep = {name: ctx.enter_context(nc.sbuf_tensor("keep_" + name, shape, dt)) for name, shape, dt in (
            ("slot", [P, TOPK, NT], I32), ("dest", [P, TOPK, NT], I32), ("gate", [P, TOPK, NT], F32),
            ("token", [P, NT], I32))}
        layers_phase(nc, io, dram)
        route_phase(nc, io, dram, keep)
        attend_phase(nc, io, dram, keep)
        experts_phase(nc, io, dram)
        combine_phase(nc, io, dram, keep, out)


SCRATCH = [
    ("x1", (T, D), F32), ("xn1", (T, D), F32), ("qk", (2, NGROUPS, PIECE, 2, G * HD // 2, M), BF16),
    ("v", (NGROUPS, M, G * HW), F32), ("logits", (T, E), F32), ("table", (NSLOT + TOPK * T, 1), I32),
    ("y", (NGROUPS, M, G * HD), F32), ("eo", (NSLOT, D), F32),
]


def constants():
    bf = mybir.dt.np(BF16)
    i = np.arange(P)
    inv_freq = (np.float32(1.0) / np.float32(10000.0) ** (np.arange(0, HD, 2, dtype=np.float32) / np.float32(HD)))
    angle = np.arange(M, dtype=np.float32)[None, :] * inv_freq.astype(np.float32)[i % (HD // 2)][:, None]
    token = (np.arange(NT)[None, :] * P + i[:, None])
    return {
        "c_ident": np.eye(P, dtype=np.float32),
        "c_identb": np.eye(P).astype(bf),
        "c_headmask": (i[:, None] // HD == np.arange(H // DC)[None, :]).astype(np.float32),
        "c_rope": np.stack([np.cos(angle), np.sin(angle)], axis=1).astype(np.float32),
        "c_mask_q": np.where(i[None, :] <= i[:, None], 0.0, MASKED).astype(bf),
        "c_mask_k": np.where(i[:, None] <= i[None, :], 0.0, MASKED).astype(bf),
        "c_before": (i[:, None] < i[None, :]).astype(bf),
        "c_ones": np.ones((P, 2048)).astype(bf),
        "c_expert": np.tile(np.arange(E, dtype=np.float32), (P, 1)),
        "c_token": token.astype(np.int32),
        "c_spill": np.stack([NSLOT + k * T + token for k in range(TOPK)], axis=1).astype(np.float32),
    }


def layout(a):
    t = lambda w: np.ascontiguousarray(np.asarray(w).T)
    pairs = lambda w: np.asarray(w).reshape(H, HD // 2, 2, -1).transpose(2, 0, 1, 3).reshape(D, -1)
    bias = lambda v: pairs(np.asarray(v)[:, None]).reshape(2, P)
    return {
        "x": np.asarray(a["L0_attn_x"]),
        "wqkv0T": t(a["L0_attn_Wqkv"]), "wout0T": t(a["L0_attn_Wout"]), "wfT": t(a["L0_ffn_weight_fp8"]),
        "fbias": np.asarray(a["L0_ffn_bias"]), "in_scale": np.asarray(a["L0_ffn_input_scale"]),
        "w_scale": np.asarray(a["L0_ffn_weight_scale"]),
        "wqk1T": np.ascontiguousarray(np.concatenate([pairs(a["L1_attn_wq"]), pairs(a["L1_attn_wk"])]).T),
        "bqk1": np.ascontiguousarray(np.concatenate([bias(a["L1_attn_bq"]), bias(a["L1_attn_bk"])]).T),
        "wvg1T": np.ascontiguousarray(np.concatenate([t(a["L1_attn_wv"]), np.asarray(a["L1_ffn_wg"])], axis=1)),
        "bv1": np.asarray(a["L1_attn_bv"]), "wo1T": t(a["L1_attn_wo"]), "bo1": np.asarray(a["L1_attn_bo"]),
        "w1": np.asarray(a["L1_ffn_w1"]),
        "b1T": np.ascontiguousarray(np.asarray(a["L1_ffn_b1"]).reshape(E, HID // P, P).transpose(2, 0, 1)),
        "w2": np.asarray(a["L1_ffn_w2"]), "b2": np.asarray(a["L1_ffn_b2"]),
    }


def kernel(**inputs):
    import concourse.bacc as _bacc
    from concourse.bass_utils import run_bass_kernel_spmd as _run

    arrays = {**layout(inputs), **constants()}
    nc = _bacc.Bacc("TRN2", target_bir_lowering=False, num_devices=1)
    io = {name: nc.dram_tensor(name, a.shape, mybir.dt.from_np(a.dtype), kind="ExternalInput").ap()
          for name, a in arrays.items()}
    out = nc.dram_tensor("out", (B, M, D), F32, kind="ExternalOutput").ap()
    build(nc, io, out)
    r = _run(nc, [arrays], core_ids=[0])
    return r.results[0]["out"]
```

```python
from contextlib import ExitStack

import numpy as np

import concourse.bass as bass
from concourse import mybir

ALU = mybir.AluOpType
ACT = mybir.ActivationFunctionType
AX = mybir.AxisListType.X
F32 = mybir.dt.float32
BF16 = mybir.dt.bfloat16
F8 = mybir.dt.float8e4
I32 = mybir.dt.int32
U32 = mybir.dt.uint32

P = 128
B, M, D = 4, 2048, 256
T = B * M
H, HD = 16, 16
SEG, DIL, BLK = 512, 8, 64
NSEG = T // SEG
SPB = M // SEG
KN = SEG // DIL
NBLK = SEG // BLK
DC = D // P
TT = SEG // P
NT = T // P
E, TOPK, HID = 8, 2, 1024
CAP = TOPK * ((T + E - 1) // E)
NSLOT = E * CAP
SCALE = HD ** -0.5
LN_EPS = 1e-5
DEN_EPS = 1e-10
FP8_MAX = 448.0
G = 4
NG = H // G
NGROUPS = B * NG
NQT = M // P
HW = 32
PIECE = 3
STACK = 6 * HD
ROWS = STACK + PIECE
Q_PIECES = (0, 0, 1, 0, 1, 2)
K_PIECES = (0, 1, 0, 2, 1, 0)
RSQRT_MAGIC = 0x5F3759DF
LOWEST = -3.0e38
MASKED = -1.0e30


class Events:

    def __init__(self, nc, ctx, prefix, counts, dma, bare=()):
        self.bare = bare
        self.k, self.unit, self.sem = {}, {}, {}
        for name, k in counts.items():
            self.k[name], self.unit[name] = k, 16 if name in dma else 1
            self.sem[name] = ctx.enter_context(nc.semaphore(f"{prefix}_{name}"))

    def start(self, e):
        for name, s in self.sem.items():
            if name not in self.bare:
                e.sem_inc(s, self.unit[name])

    def at(self, name, n, j):
        return (n * self.k[name] + j + (name not in self.bare)) * self.unit[name]

    def wait(self, e, name, n, j):
        e.wait_ge(self.sem[name], self.at(name, n, j))

    def done(self, ins, name):
        return ins.then_inc(self.sem[name], self.unit[name])


class Steps:

    def __init__(self, e, sem, base, ev=None):
        self.e, self.sem, self.base, self.n, self.ev = e, sem, base, 0, ev
        self.last, self.seen = None, {}

    def then(self, ins):
        self.n += 1
        self.last = self.sem, self.base + self.n
        return ins.then_inc(self.sem, 1)

    def mark(self, ins, name, step=None):
        self.seen[name] = self.seen.get(name, 0) + 1
        self.last = self.ev.sem[name], self.ev.at(name, self.at if step is None else step, self.seen[name])
        return self.ev.done(ins, name)

    def step(self, n):
        self.at, self.seen = n, {}

    def settle(self, passed=None):
        self.e.wait_ge(*self.last)
        if passed is not None:
            self.e.sem_inc(passed, 1)


def layers_phase(nc, io, dram):
    with ExitStack() as ctx:
        def sb(name, shape, dt=F32):
            return ctx.enter_context(nc.sbuf_tensor("a_" + name, shape, dt))

        def ps(name, shape, dt=F32):
            return ctx.enter_context(nc.psum_tensor("a_" + name, shape, dt))

        ident = sb("ident", [P, P])
        headmask = sb("headmask", [P, H // DC])
        rope = sb("rope", [P, 2, M])
        wqkv0 = sb("wqkv0", [P, DC, 3 * D])
        wout0 = sb("wout0", [P, DC, D])
        wf = sb("wf", [P, DC, D])
        wf_rest = sb("wf_rest", [P, DC, D])
        wf_piece = [sb(f"wf_piece{i}", [P, DC, D], BF16) for i in range(PIECE)]
        fbias = sb("fbias", [P, D])
        in_scale = sb("in_scale", [P, 1])
        in_inv = sb("in_inv", [P, 1])
        square = sb("square", [P, DC, SEG])
        w_scale = sb("w_scale", [P, 1])
        wqk1 = sb("wqk1", [P, DC, 4 * P])
        bqk1 = sb("bqk1", [P, 4])
        wvg1 = sb("wvg1", [P, DC, D + E])
        bv1 = sb("bv1", [P, D])
        x = sb("x", [P, 2, TT, D])
        stats = sb("stats", [P, 2, TT, 6])
        mv = sb("mv", [P, 2, TT, 2])
        rstd = sb("rstd", [P, 2, TT])
        veps = sb("veps", [P, 2, TT])
        seed = sb("seed", [P, 2, TT], I32)
        newton = sb("newton", [P, 2, TT])
        xn = sb("xn", [P, TT, D])
        xnT = sb("xnT", [P, DC, SEG])
        clipped = sb("clipped", [P, DC, SEG])
        coarse = sb("coarse", [P, DC, SEG], F8)
        half8 = sb("half8", [P, DC, SEG], F8)
        is_big = sb("is_big", [P, DC, SEG], U32)
        doubled = sb("doubled", [P, DC, SEG], BF16)
        xq = sb("xq", [P, DC, SEG], BF16)
        qT = sb("qT", [P, DC, SEG])
        kbd = sb("kbd", [P, DC, H // DC, KN])
        vbd = sb("vbd", [P, H // 2, 2 * HW])
        keymax = sb("keymax", [P, 2, NBLK])
        shifted = sb("shifted", [P, 2, SEG])
        wexp = sb("wexp", [P, 2, SEG])
        oT = sb("oT", [P, 2, SEG])
        den = sb("den", [P, TT, G])
        rden = sb("rden", [P, TT, G])
        y = sb("y", [P, TT, D])
        yT = sb("yT", [P, DC, SEG])
        z = sb("z", [P, TT, D])
        ez = sb("ez", [P, TT, D])
        x1 = sb("x1", [P, TT, D])
        xn1 = sb("xn1", [P, TT, D])
        x1T = sb("x1T", [P, DC, SEG])
        qk = sb("qk", [P, 2, 2, SEG])
        rot = sb("rot", [P, 2, 2, SEG])
        prod = sb("prod", [P, 2, SEG])
        prod1 = sb("prod1", [P, 2, SEG])
        piece = [sb(f"piece{i}", [P, 2, 2, SEG], BF16) for i in range(PIECE)]
        v32 = sb("v32", [P, TT, H, HW])
        logit = sb("logit", [P, TT, E])

        tb = ps("tb", [P, DC, SEG])
        pb = ps("pb", [P, 2, SEG])
        kv = ps("kv", [P, SEG])
        sc = ps("sc", [P, 2, SEG])
        ob = ps("ob", [P, SEG])

        NP0 = H // 2
        counts = dict(
            var=1, rstd=1, xn=1, tr=1, trc=2, q=1, qc=1, kv=1, kvc=1, ff=2, ffc=2, quant=1,
            s=NP0, shift=NP0, wexp=NP0, pv=NP0, oc=4, ot=4, norm=4, ytr=1, ytc=2,
            so=2, sog=2, ez=2, gate=1, x1=1, x1_out=1,
            var1=1, rstd1=1, xn1=1, xn1_out=1, tr1=1, tr1c=2, pj=2, pjc=4, rot=1, rot1=1, p1=1, rest=1, p2=1, p3=1,
            qk_out=12, vj=4, vjc=4, lc=4, v_out=NG, l_out=1)
        counts.update(x_in0=1, x_in1=1)
        ev = Events(nc, ctx, "a", counts, {"x_in0", "x_in1", "x1_out", "xn1_out", "qk_out", "v_out", "l_out"})
        consts = ctx.enter_context(nc.semaphore("a_consts"))
        ready = ctx.enter_context(nc.semaphore("a_ready"))
        passed = ctx.enter_context(nc.semaphore("a_passed"))
        dve_step = ctx.enter_context(nc.semaphore("a_dve_step"))
        setup_step = ctx.enter_context(nc.semaphore("a_setup_step"))
        NCONST = 13
        pool_step = ctx.enter_context(nc.semaphore("a_pool_step"))
        FIRST_STEPS, TURN_STEPS = 40, 55
        POOL_FIRST, POOL_TURN = 11, 24

        def turns(e, first, both, second):
            first()
            with e.Fori(0, B - 1) as b:
                for c in range(SPB):
                    both(b, c)
            for c in range(SPB - 1):
                both(B - 1, c)
            second()

        def place(b, c):
            return (b, c + 1) if c + 1 < SPB else (b + 1, 0)

        def rotary(c):
            return [rope[:, i, c * SEG:(c + 1) * SEG].unsqueeze(1).to_broadcast([P, 2, SEG]) for i in range(2)]

        with nc.Block() as block:
            @block.sync
            def _(sp):
                loads = [
                    (ident[:], io["c_ident"]), (headmask[:], io["c_headmask"]),
                    (rope[:], io["c_rope"]),
                    (wqkv0[:], io["wqkv0T"].rearrange("(k p) n -> p k n", p=P)),
                    (wout0[:], io["wout0T"].rearrange("(k p) n -> p k n", p=P)),
                    (wf[:], io["wfT"].rearrange("(k p) n -> p k n", p=P)),
                    (fbias[:], io["fbias"].partition_broadcast(P)),
                    (in_scale[:], io["in_scale"].partition_broadcast(P)),
                    (w_scale[:], io["w_scale"].partition_broadcast(P)),
                    (wqk1[:], io["wqk1T"].rearrange("(k p) n -> p k n", p=P)),
                    (bqk1[:], io["bqk1"]),
                    (wvg1[:], io["wvg1T"].rearrange("(k p) n -> p k n", p=P)),
                    (bv1[:], io["bv1"].partition_broadcast(P)),
                ]
                assert len(loads) == NCONST
                for out, in_ in loads:
                    sp.dma_start(out, in_).then_inc(consts, 16)
                def load(b, c, m):
                    src = io["x"][bass.ds(b, 1), c * SEG:(c + 1) * SEG, :]
                    ev.done(sp.dma_start(x[:, c % 2], src.rearrange("o (t p) d -> p (o t) d", p=P)), f"x_in{c % 2}")

                def store_x1(b, c, m):
                    ev.wait(sp, "x1", m, 1)
                    ev.done(sp.dma_start(dram["x1"][bass.ds(b * M + c * SEG, SEG), :].rearrange("(t p) d -> p t d", p=P),
                                         x1[:]), "x1_out")

                def store_layer1(b, c, n):
                    tok = bass.ds(b * M + c * SEG, SEG)
                    ev.wait(sp, "xn1", n, 1)
                    ev.done(sp.dma_start(dram["xn1"][tok, :].rearrange("(t p) d -> p t d", p=P), xn1[:]), "xn1_out")
                    for i in range(PIECE):
                        ev.wait(sp, f"p{i + 1}", n, 1)
                        for m in range(2):
                            for f in range(2):
                                dst = dram["qk"][m, bass.ds(b * NG, NG), i, f, :, c * SEG:(c + 1) * SEG]
                                ev.done(sp.dma_start(dst, piece[i][:, m, f, :]), "qk_out")
                    ev.wait(sp, "vjc", n, 4)
                    for hg in range(NG):
                        dst = dram["v"][bass.ds(b * NG + hg, 1), c * SEG:(c + 1) * SEG, :]
                        ev.done(sp.dma_start(dst.rearrange("o (t p) w -> p (o t) w", p=P),
                                             v32[:, :, hg * G:(hg + 1) * G, :].rearrange("p t h w -> p t (h w)")),
                                "v_out")
                    ev.wait(sp, "lc", n, 4)
                    ev.done(sp.dma_start(dram["logits"][tok, :].rearrange("(t p) d -> p t d", p=P), logit[:]), "l_out")

                def first():
                    load(0, 0, 0)
                    load(0, 1, 1)
                    store_x1(0, 0, 0)

                def both(b, c):
                    n = b * SPB + c
                    b1, c1 = place(b, c)
                    if c + 2 < SPB or not isinstance(b, int):
                        ev.wait(sp, "x1", n, 1)
                        b2, c2 = (b, c + 2) if c + 2 < SPB else (b + 1, c + 2 - SPB)
                        load(b2, c2, n + 2)
                    store_layer1(b, c, n)
                    store_x1(b1, c1, n + 1)

                turns(sp, first, both, lambda: store_layer1(B - 1, SPB - 1, NSEG - 1))
                for name in ("x1_out", "xn1_out", "qk_out", "v_out", "l_out"):
                    sp.wait_ge(ev.sem[name], 16 * (NSEG * counts[name] + 1))

            @block.gpsimd
            def _(pool):
                def inverse_root(st, n, i, var, rs):
                    ev.wait(pool, var, n, 1)
                    st.step(n)
                    v, root, tmp = veps[:, i], rstd[:, i], newton[:, i]
                    for step in range(3):
                        start = seed[:, i].bitcast(F32) if step == 0 else root
                        st.then(pool.tensor_tensor(tmp, start, start, ALU.mult))
                        st.settle()
                        st.then(pool.tensor_tensor(tmp, tmp, v, ALU.mult))
                        st.settle(passed)
                        st.then(pool.tensor_scalar(tmp, tmp, -0.5, 1.5, ALU.mult, ALU.add))
                        st.settle()
                        last = pool.tensor_tensor(root, start, tmp, ALU.mult)
                        if step < 2:
                            st.then(last)
                            st.settle()
                    st.mark(last, rs)

                def rotate(st, n, c):
                    st.step(n)
                    cos, sin = rotary(c)
                    ev.wait(pool, "pjc", n, 4)
                    ev.wait(pool, "p3", n, 0)
                    st.then(pool.tensor_tensor(rot[:, :, 1, :], qk[:, :, 0, :], sin, ALU.mult))
                    st.then(pool.tensor_tensor(prod1[:], qk[:, :, 1, :], cos, ALU.mult))
                    st.settle()
                    st.mark(pool.tensor_tensor(rot[:, :, 1, :], rot[:, :, 1, :], prod1[:], ALU.add), "rot1")

                def first():
                    st = Steps(pool, pool_step, 0, ev)
                    inverse_root(st, 0, 0, "var", "rstd")
                    assert st.n == POOL_FIRST, st.n

                def layer1(st, n, c):
                    inverse_root(st, n, 1, "var1", "rstd1")
                    rotate(st, n, c)

                def both(b, c):
                    n = b * SPB + c
                    st = Steps(pool, pool_step, POOL_FIRST + n * POOL_TURN, ev)
                    ev.wait(pool, "rstd", n, 1)
                    ev.wait(pool, "rot1", n, 0)
                    inverse_root(st, n + 1, 0, "var", "rstd")
                    layer1(st, n, c)
                    assert st.n == POOL_TURN, st.n

                def second():
                    st = Steps(pool, pool_step, POOL_FIRST + (NSEG - 1) * POOL_TURN, ev)
                    ev.wait(pool, "rot1", NSEG - 1, 0)
                    layer1(st, NSEG - 1, SPB - 1)

                turns(pool, first, both, second)

            @block.tensor
            def _(pe):
                pe.wait_ge(consts, 16 * NCONST)
                pe.wait_ge(ready, 1)

                def turn_tokens(src, name):
                    for k in range(DC):
                        for t in range(TT):
                            last = pe.transpose(tb[:, k, t * P:(t + 1) * P], src[:, t, k * P:(k + 1) * P], ident[:])
                    ev.done(last, name)

                def turn_first(m):
                    ev.wait(pe, "xn", m, 1)
                    ev.wait(pe, "ytc", m, 0)
                    turn_tokens(xn, "tr")

                def keys(m):
                    ev.wait(pe, "trc", m, 2)
                    ev.wait(pe, "norm", m, 0)
                    for f in range(DC):
                        for k in range(DC):
                            pe.matmul(kv[:, f * KN:(f + 1) * KN], wqkv0[:, k, D + f * P:D + (f + 1) * P],
                                      xnT[:, k, ::DIL], start=(k == 0), stop=(k == DC - 1))
                    for half in range(2):
                        for k in range(DC):
                            last = pe.matmul(kv[half * KN:(half + 1) * KN, D:2 * D], xnT[:, k, ::DIL],
                                             wqkv0[:, k, 2 * D:3 * D], start=(k == 0), stop=(k == DC - 1))
                    ev.done(last, "kv")

                def queries(m):
                    ev.wait(pe, "ffc", m, 0)
                    for f in range(DC):
                        for k in range(DC):
                            last = pe.matmul(pb[:, f, :], wqkv0[:, k, f * P:(f + 1) * P], xnT[:, k, :],
                                             start=(k == 0), stop=(k == DC - 1))
                    ev.done(last, "q")

                def scores(m, p):
                    if p == 0:
                        ev.wait(pe, "kvc", m, 1)
                        ev.wait(pe, "qc", m, 1)
                        ev.wait(pe, "sog", m, 0)
                    f, a = p // (NP0 // DC), 2 * (p % (NP0 // DC))
                    ev.wait(pe, "shift", m, max(p - 1, 0))
                    ev.done(pe.matmul(sc[:, p % 2, :], kbd[:, f, a:a + 2, :].rearrange("p a k -> p (a k)"),
                                      qT[:, f, :], start=True, stop=True), "s")

                def values(m, p):
                    ev.wait(pe, "wexp", m, p + 1)
                    if p % 2 == 0:
                        ev.wait(pe, "oc", m, p // 2)
                    r = (p % 2) * 2 * HW
                    ev.done(pe.matmul(ob[r:r + 2 * HW, :], vbd[:, p, :], wexp[:, p % 2, :], start=True, stop=True), "pv")

                def turn(m, g):
                    ev.wait(pe, "oc", m, g + 1)
                    ev.wait(pe, "norm", m, g)
                    for t in range(TT):
                        last = pe.transpose(kv[:, t * P:(t + 1) * P], oT[:, g % 2, t * P:(t + 1) * P], ident[:])
                    ev.done(last, "ot")

                def gate(m, f):
                    ev.wait(pe, "quant", m, 1)
                    if f == 0:
                        ev.wait(pe, "qc", m, 1)
                    ev.wait(pe, "vjc", m, 0)
                    ev.wait(pe, "lc", m, 0)
                    for t in (2 * f, 2 * f + 1):
                        i = 0
                        for w in wf_piece:
                            for k in range(DC):
                                last = pe.matmul(pb[:, f, (t % 2) * D:(t % 2 + 1) * D], xq[:, k, t * P:(t + 1) * P],
                                                 w[:, k, :], start=(i == 0), stop=(i == 2 * PIECE - 1))
                                i += 1
                    ev.done(last, "ff")

                def project(m):
                    ev.wait(pe, "norm", m, 4)
                    ev.wait(pe, "tr1c", m, 0)
                    turn_tokens(y, "ytr")
                    ev.wait(pe, "ytc", m, 2)
                    for f in range(2):
                        for t in (2 * f, 2 * f + 1):
                            for k in range(DC):
                                last = pe.matmul(sc[:, f, (t % 2) * D:(t % 2 + 1) * D], yT[:, k, t * P:(t + 1) * P],
                                                 wout0[:, k, :], start=(k == 0), stop=(k == DC - 1))
                        ev.done(last, "so")

                def turn_second(n):
                    ev.wait(pe, "xn1", n, 1)
                    turn_tokens(xn1, "tr1")

                def project1(n, m):
                    if m == 0:
                        ev.wait(pe, "tr1c", n, 2)
                    else:
                        ev.wait(pe, "pjc", n, 2)
                    for f in range(2):
                        for k in range(DC):
                            w = (2 * m + f) * P
                            last = pe.matmul(pb[:, f, :], wqk1[:, k, w:w + P], x1T[:, k, :],
                                             start=(k == 0), stop=(k == DC - 1))
                    ev.done(last, "pj")

                def values1(n, t):
                    if t == 0:
                        ev.wait(pe, "pjc", n, 4)
                    if t >= 2:
                        ev.wait(pe, "vjc", n, t - 1)
                        ev.wait(pe, "lc", n, t - 1)
                    for k in range(DC):
                        last = pe.matmul(pb[:, t % 2, 0:D + E], x1T[:, k, t * P:(t + 1) * P], wvg1[:, k, :],
                                         start=(k == 0), stop=(k == DC - 1))
                    ev.done(last, "vj")

                def turn_both(m, n):
                    turn_first(m)
                    keys(m)
                    queries(m)
                    if n is not None:
                        turn_second(n)
                        ev.wait(pe, "qc", m, 1)
                        project1(n, 0)
                    for p in range(NP0 + 1):
                        if p < NP0:
                            scores(m, p)
                        if n is not None and p == 0:
                            project1(n, 1)
                        if p >= 1:
                            values(m, p - 1)
                        if n is not None and 1 <= p <= TT:
                            values1(n, p - 1)
                        if p >= 3 and p % 2 == 1:
                            turn(m, (p - 3) // 2)
                        if p == NP0 - 1:
                            gate(m, 0)
                    gate(m, 1)
                    turn(m, 3)
                    project(m)

                def both(b, c):
                    turn_both(b * SPB + c + 1, b * SPB + c)

                def second():
                    n = NSEG - 1
                    turn_second(n)
                    ev.wait(pe, "ffc", n, 2)
                    for m in range(2):
                        project1(n, m)
                    for t in range(TT):
                        values1(n, t)

                turns(pe, lambda: turn_both(0, None), both, second)

            @block.scalar
            def _(act):
                act.wait_ge(consts, 16 * NCONST)
                act.wait_ge(ready, 1)

                def copy_turned(dst, name):
                    for k in range(DC):
                        ev.done(act.activation(dst[:, k, :], tb[:, k, :], ACT.Copy), name)

                def out_copy(m, g):
                    ev.wait(act, "pv", m, 2 * g + 2)
                    ev.wait(act, "ot", m, max(g - 1, 0))
                    ev.done(act.activation(oT[:, g % 2, :], ob[:], ACT.Copy), "oc")

                def second_turned(n):
                    ev.wait(act, "tr1", n, 1)
                    ev.wait(act, "vj", n, 0)
                    copy_turned(x1T, "tr1c")

                def projected(n, m):
                    ev.wait(act, "pj", n, m + 1)
                    if m == 0:
                        ev.wait(act, "p3", n, 0)
                    for f in range(2):
                        ev.done(act.activation(qk[:, m, f, :], pb[:, f, :], ACT.Identity,
                                               bias=bqk1[:, 2 * m + f:2 * m + f + 1]), "pjc")

                def part0(n):
                    ev.wait(act, "rot", n, 1)
                    ev.wait(act, "rot1", n, 1)
                    ev.wait(act, "qk_out", n, 0)
                    ev.done(act.activation(piece[0][:], rot[:], ACT.Copy), "p1")

                def part1(n):
                    ev.wait(act, "rest", n, 1)
                    ev.done(act.activation(piece[1][:], qk[:], ACT.Copy), "p2")

                def logits(n, t):
                    ev.wait(act, "vj", n, t + 1)
                    if t == 0:
                        ev.wait(act, "l_out", n, 0)
                    ev.wait(act, "vjc", n, t + 1)
                    ev.done(act.activation(logit[:, t, :], pb[:, t % 2, D:D + E], ACT.Copy), "lc")

                def turn_both(m, n):
                    ev.wait(act, "tr", m, 1)
                    ev.wait(act, "kv", m, 0)
                    ev.wait(act, "quant", m, 0)
                    copy_turned(xnT, "trc")
                    ev.wait(act, "q", m, 1)
                    ev.done(act.activation(qT[:].rearrange("p k t -> p (k t)"), pb[:].rearrange("p k t -> p (k t)"),
                                           ACT.Copy), "qc")
                    if n is not None:
                        second_turned(n)
                        projected(n, 0)
                    for p in range(NP0):
                        ev.wait(act, "shift", m, p + 1)
                        ev.wait(act, "pv", m, max(p - 1, 0))
                        ev.done(act.activation(wexp[:, p % 2, :], shifted[:, p % 2, :], ACT.Exp, scale=SCALE), "wexp")
                        if n is not None and p == 0:
                            projected(n, 1)
                        if p % 2 == 1:
                            out_copy(m, p // 2)
                        if n is not None and 2 <= p < 2 + TT:
                            logits(n, p - 2)
                        if n is not None and p == 4:
                            part0(n)
                        if n is not None and p == 6:
                            part1(n)
                    ev.wait(act, "ytr", m, 1)
                    ev.wait(act, "so", m, 0)
                    copy_turned(yT, "ytc")
                    ev.wait(act, "x1", m, 0)
                    for f in range(2):
                        ev.wait(act, "ffc", m, f + 1)
                        ev.done(act.activation(ez[:, 2 * f:2 * f + 2], z[:, 2 * f:2 * f + 2], ACT.Tanh, scale=0.5), "ez")

                def second():
                    n = NSEG - 1
                    second_turned(n)
                    for m in range(2):
                        projected(n, m)
                    for t in range(TT):
                        logits(n, t)
                    part0(n)
                    part1(n)

                turns(act, lambda: turn_both(0, None), lambda b, c: turn_both(b * SPB + c + 1, b * SPB + c), second)

            @block.vector
            def _(dve):
                ev.start(dve)
                setup = Steps(dve, setup_step, 0)
                dve.wait_ge(consts, 16 * NCONST)
                setup.then(dve.tensor_scalar(wf[:], wf[:], w_scale[:, 0:1], None, ALU.mult))
                setup.settle()
                setup.then(dve.tensor_copy(wf_piece[0][:], wf[:]))
                setup.settle()
                setup.then(dve.tensor_tensor(wf_rest[:], wf[:], wf_piece[0][:], ALU.subtract))
                setup.settle()
                setup.then(dve.tensor_copy(wf_piece[1][:], wf_rest[:]))
                setup.settle()
                setup.then(dve.tensor_tensor(wf_piece[2][:], wf_rest[:], wf_piece[1][:], ALU.subtract))
                setup.then(dve.reciprocal(in_inv[:], in_scale[:]))
                setup.then(dve.memset(vbd[:], 0.0))
                setup.then(dve.memset(v32[:], 1.0))
                setup.settle()
                setup.then(dve.memset(vbd[0:KN, :, HD:HD + 1], 1.0))
                setup.then(dve.memset(vbd[KN:P, :, HW + HD:HW + HD + 1], 1.0))
                setup.settle()
                dve.sem_inc(ready, 1)

                def find_norm(st, src, i, n, var):
                    for t in range(TT):
                        st.then(dve.bn_stats(stats[:, i, t, :], src[:, t, :]))
                    st.settle(passed)
                    for t in range(TT):
                        st.then(dve.bn_aggr(mv[:, i, t, :], stats[:, i, t, :]))
                    st.settle()
                    st.then(dve.tensor_scalar(veps[:, i], mv[:, i, :, 1], LN_EPS, None, ALU.add))
                    st.settle()
                    st.then(dve.tensor_scalar(seed[:, i], veps[:, i].bitcast(I32), 1, None, ALU.arith_shift_right))
                    st.settle()
                    st.mark(dve.tensor_scalar(seed[:, i], seed[:, i], -1.0, float(RSQRT_MAGIC), ALU.mult, ALU.add),
                            var, n)

                def norm_tokens(st, src, dst, i, n, rs, done):
                    ev.wait(dve, rs, n, 1)
                    for t in range(TT):
                        last = dve.tensor_scalar(dst[:, t, :], src[:, t, :], mv[:, i, t, 0:1],
                                                 rstd[:, i, t:t + 1], ALU.subtract, ALU.mult)
                        if t == TT - 1:
                            st.mark(last, done, n)
                        else:
                            st.then(last)

                def quantise(st, m):
                    ev.wait(dve, "trc", m, 2)
                    ev.wait(dve, "ff", m, 0)
                    st.then(dve.tensor_scalar(clipped[:], xnT[:], in_inv[:, 0:1], FP8_MAX, ALU.mult, ALU.min))
                    st.settle()
                    st.then(dve.tensor_scalar(clipped[:], clipped[:], -FP8_MAX, None, ALU.max))
                    st.settle(passed)
                    st.then(dve.tensor_scalar(half8[:], clipped[:], 0.5, None, ALU.mult, saturate=False))
                    st.then(dve.tensor_scalar(coarse[:], clipped[:], 240.0, -240.0, ALU.min, ALU.max,
                                              saturate=False))
                    st.then(dve.tensor_tensor(square[:], clipped[:], clipped[:], ALU.mult))
                    st.settle()
                    st.then(dve.tensor_scalar(is_big[:], square[:], 2.0 ** -10, None, ALU.is_ge))
                    st.settle(passed)
                    st.then(dve.tensor_copy(xq[:], coarse[:]))
                    st.then(dve.tensor_scalar(doubled[:], half8[:], 2.0, None, ALU.mult))
                    st.settle(passed)
                    st.mark(dve.copy_predicated(xq[:], is_big[:], doubled[:]), "quant", m)

                def block_diagonal(st, m):
                    ev.wait(dve, "kv", m, 1)
                    ev.wait(dve, "pv", m, 0)
                    for f in range(DC):
                        st.then(dve.tensor_tensor(
                            kbd[:, f], kv[:, f * KN:(f + 1) * KN].unsqueeze(1).to_broadcast([P, H // DC, KN]),
                            headmask[:].unsqueeze(2).to_broadcast([P, H // DC, KN]), ALU.mult))
                    heads = kv[:, D:2 * D].rearrange("p (a two d) -> p a two d", two=2, d=HD)
                    st.then(dve.tensor_copy(vbd[0:KN, :, 0:HD], heads[0:KN, :, 0, :]))
                    st.mark(dve.tensor_copy(vbd[KN:P, :, HW:HW + HD], heads[KN:P, :, 1, :]), "kvc", m)

                def shift(st, m, p):
                    ev.wait(dve, "s", m, p + 1)
                    ev.wait(dve, "wexp", m, max(p - 1, 0))
                    blocks = sc[:, p % 2, :].rearrange("p (n q) -> p n q", q=BLK)
                    st.then(dve.tensor_reduce(keymax[:, p % 2, :], blocks, AX, ALU.max))
                    st.settle()
                    st.mark(dve.tensor_tensor(
                        shifted[:, p % 2, :].rearrange("p (n q) -> p n q", q=BLK), blocks,
                        keymax[:, p % 2, :].unsqueeze(2).to_broadcast([P, NBLK, BLK]), ALU.subtract), "shift", m)

                def normalise(st, m, g):
                    ev.wait(dve, "ot", m, g + 1)
                    turned = kv[:].rearrange("p (t h w) -> p t h w", t=TT, w=HW)
                    st.then(dve.tensor_scalar(den[:], turned[:, :, :, HD], DEN_EPS, None, ALU.add))
                    st.settle()
                    st.then(dve.reciprocal(rden[:], den[:]))
                    st.settle()
                    if g == 0:
                        ev.wait(dve, "ytr", m, 0)
                    out = y[:, :, g * G * HD:(g + 1) * G * HD].rearrange("p t (h d) -> p t h d", d=HD)
                    st.mark(dve.tensor_tensor(
                        out, turned[:, :, :, 0:HD], rden[:].unsqueeze(3).to_broadcast([P, TT, G, HD]), ALU.mult),
                        "norm", m)

                def residual(st, c, m):
                    for f in range(2):
                        ev.wait(dve, "ff", m, f + 1)
                        if f == 0:
                            ev.wait(dve, "ez", m, 0)
                        st.mark(dve.scalar_tensor_tensor(
                            out=z[:, 2 * f:2 * f + 2], in0=pb[:, f, :].rearrange("p (t d) -> p t d", d=D),
                            scalar=in_scale[:, 0:1], in1=fbias[:].unsqueeze(1).to_broadcast([P, 2, D]),
                            op0=ALU.mult, op1=ALU.add), "ffc", m)
                    normalise(st, m, 3)
                    ev.wait(dve, "ez", m, 2)
                    st.mark(dve.scalar_tensor_tensor(out=z[:], in0=ez[:], scalar=1.0, in1=z[:],
                                                     op0=ALU.add, op1=ALU.mult), "gate", m)
                    st.settle()
                    for f in range(2):
                        ev.wait(dve, "so", m, f + 1)
                        st.mark(dve.scalar_tensor_tensor(
                            out=ez[:, 2 * f:2 * f + 2], in0=sc[:, f, :].rearrange("p (t d) -> p t d", d=D),
                            scalar=0.5, in1=z[:, 2 * f:2 * f + 2], op0=ALU.mult, op1=ALU.mult), "sog", m)
                    st.settle()
                    ev.wait(dve, "x1_out", m, 0)
                    st.mark(dve.tensor_tensor(x1[:], x[:, c % 2], ez[:], ALU.add), "x1", m)

                def rotate(st, n, c):
                    cos, sin = rotary(c)
                    ev.wait(dve, "pjc", n, 4)
                    ev.wait(dve, "p1", n, 0)
                    st.then(dve.tensor_tensor(rot[:, :, 0, :], qk[:, :, 0, :], cos, ALU.mult))
                    st.then(dve.tensor_tensor(prod[:], qk[:, :, 1, :], sin, ALU.mult))
                    st.settle()
                    st.mark(dve.tensor_tensor(rot[:, :, 0, :], rot[:, :, 0, :], prod[:], ALU.subtract), "rot", n)

                def rest(st, n):
                    ev.wait(dve, "p1", n, 1)
                    st.mark(dve.tensor_tensor(qk[:], rot[:], piece[0][:], ALU.subtract), "rest", n)

                def last_part(st, n):
                    ev.wait(dve, "p2", n, 1)
                    ev.wait(dve, "qk_out", n, 0)
                    st.mark(dve.tensor_tensor(piece[2][:], qk[:], piece[1][:], ALU.subtract), "p3", n)

                def values1(st, n, t):
                    ev.wait(dve, "vj", n, t + 1)
                    if t == 0:
                        ev.wait(dve, "v_out", n, 0)
                    st.mark(dve.tensor_tensor(
                        v32[:, t, :, 0:HD], pb[:, t % 2, 0:D].rearrange("p (h d) -> p h d", d=HD),
                        bv1[:].rearrange("p (h d) -> p h d", d=HD), ALU.add), "vjc", n)

                def turn_both(st, m, c1, n, c, use):
                    ev.wait(dve, f"x_in{c1 % 2}", use, 1)
                    ev.wait(dve, "tr", m, 0)
                    ev.wait(dve, "rstd", m, 0)
                    if n is not None:
                        st.settle()
                    find_norm(st, x[:, c1 % 2], 0, m, "var")
                    if n is not None:
                        ev.wait(dve, "rstd1", n, 0)
                        find_norm(st, x1, 1, n, "var1")
                    norm_tokens(st, x[:, c1 % 2], xn, 0, m, "rstd", "xn")
                    if n is not None:
                        ev.wait(dve, "xn1_out", n, 0)
                        norm_tokens(st, x1, xn1, 1, n, "rstd1", "xn1")
                    quantise(st, m)
                    block_diagonal(st, m)
                    for p in range(NP0):
                        shift(st, m, p)
                        if n is not None:
                            if p == 1:
                                rotate(st, n, c)
                            if 2 <= p < 2 + TT:
                                values1(st, n, p - 2)
                            if p == 5:
                                rest(st, n)
                            if p == 7:
                                last_part(st, n)
                        if p >= 3 and p % 2 == 1:
                            normalise(st, m, (p - 3) // 2)
                    residual(st, c1, m)

                def first():
                    st = Steps(dve, dve_step, 0, ev)
                    turn_both(st, 0, 0, None, None, 0)
                    assert st.n == FIRST_STEPS, ("first", st.n)

                def both(b, c):
                    n = b * SPB + c
                    st = Steps(dve, dve_step, FIRST_STEPS + n * TURN_STEPS, ev)
                    st.last = ev.sem["x1"], ev.at("x1", n, 1)
                    turn_both(st, n + 1, place(b, c)[1], n, c, b * (SPB // 2) + (c + 1) // 2)
                    assert st.n == TURN_STEPS, ("turn", st.n)

                def second():
                    n = NSEG - 1
                    st = Steps(dve, dve_step, FIRST_STEPS + n * TURN_STEPS, ev)
                    st.last = ev.sem["x1"], ev.at("x1", n, 1)
                    st.settle()
                    find_norm(st, x1, 1, n, "var1")
                    ev.wait(dve, "xn1_out", n, 0)
                    norm_tokens(st, x1, xn1, 1, n, "rstd1", "xn1")
                    rotate(st, n, SPB - 1)
                    for t in range(TT):
                        values1(st, n, t)
                    rest(st, n)
                    last_part(st, n)

                turns(dve, first, both, second)


def route_phase(nc, io, dram, keep):
    with ExitStack() as ctx:
        def sb(name, shape, dt=F32):
            return ctx.enter_context(nc.sbuf_tensor("r_" + name, shape, dt))

        def sem(name):
            return ctx.enter_context(nc.semaphore("r_" + name))

        KT = TOPK * NT
        before = sb("before", [P, P], BF16)
        ones = sb("ones", [P, P], BF16)
        onesf = sb("onesf", [P, KT])
        expert = sb("expert", [P, E])
        spill = sb("spill", [P, TOPK, NT])
        zero = sb("zero", [P, P], I32)
        logit = sb("logit", [P, NT, E])
        score = sb("score", [P, NT, E])
        rest = sb("rest", [P, NT, E])
        best = sb("best", [P, TOPK, NT])
        total = sb("total", [P, NT])
        below = sb("below", [P, NT, E])
        which = sb("which", [P, TOPK, NT])
        hot = sb("hot", [P, TOPK, NT, E])
        hotb = sb("hotb", [P, TOPK * NT * E], BF16)
        count = sb("count", [P, E, KT])
        running = sb("running", [P, E, KT])
        place = sb("place", [P, KT, E])
        loc = sb("loc", [P, KT])
        valid = sb("valid", [P, KT])
        slotf = sb("slotf", [P, KT])
        destf = sb("destf", [P, KT])
        inside = ctx.enter_context(nc.psum_tensor("r_inside", [P, KT * E], F32))
        totals = ctx.enter_context(nc.psum_tensor("r_totals", [P, KT * E], F32))
        loads, zeroed, shifted, weights, hots, prefix, step = map(
            sem, ("loads", "zeroed", "shifted", "weights", "hots", "prefix", "step"))
        table_zero = sem("table_zero")

        with nc.Block() as block:
            @block.sync
            def _(sp):
                for out, in_ in ((before[:], io["c_before"]), (ones[:], io["c_ones"][:, 0:P]),
                                 (expert[:], io["c_expert"]), (spill[:], io["c_spill"]),
                                 (keep["token"][:], io["c_token"]),
                                 (logit[:], dram["logits"].rearrange("(t p) e -> p t e", p=P))):
                    sp.dma_start(out, in_).then_inc(loads, 16)
                sp.wait_ge(zeroed, 1)
                sp.dma_start(dram["table"][0:NSLOT, :].rearrange("(p f) o -> p (f o)", p=P), zero[:]).then_inc(table_zero, 16)
                sp.wait_ge(table_zero, 16)

            @block.tensor
            def _(pe):
                pe.wait_ge(hots, 1)
                for out, w in ((inside, before), (totals, ones)):
                    for f in range(2):
                        cols = slice(f * 512, (f + 1) * 512)
                        last = pe.matmul(out[:, cols], w[:], hotb[:, cols], start=True, stop=True)
                last.then_inc(prefix, 1)

            @block.scalar
            def _(act):
                act.wait_ge(shifted, 1)
                act.activation(score[:], logit[:], ACT.Exp).then_inc(weights, 1)

            @block.vector
            def _(dve):
                steps = [0]

                def then(ins):
                    steps[0] += 1
                    ins.then_inc(step, 1)
                    dve.wait_ge(step, steps[0])

                wide = lambda a: a.unsqueeze(2).to_broadcast([P, NT, E])
                ids = expert[:].unsqueeze(1).to_broadcast([P, NT, E])
                dve.memset(zero[:], 0).then_inc(zeroed, 1)
                then(dve.memset(onesf[:], 1.0))
                dve.wait_ge(loads, 96)
                then(dve.tensor_reduce(total[:], logit[:], AX, ALU.max))
                dve.tensor_tensor(logit[:], logit[:], wide(total[:]), ALU.subtract).then_inc(shifted, 1)
                dve.wait_ge(weights, 1)
                then(dve.tensor_reduce(total[:], score[:], AX, ALU.add))
                then(dve.reciprocal(total[:], total[:]))
                then(dve.tensor_tensor(score[:], score[:], wide(total[:]), ALU.mult))
                for k in range(TOPK):
                    s = score if k == 0 else rest
                    then(dve.tensor_reduce(best[:, k], s[:], AX, ALU.max))
                    then(dve.tensor_tensor(below[:], s[:], wide(best[:, k]), ALU.is_lt))
                    then(dve.scalar_tensor_tensor(out=below[:], in0=below[:], scalar=float(2 * E), in1=ids,
                                                  op0=ALU.mult, op1=ALU.add))
                    then(dve.tensor_reduce(which[:, k], below[:], AX, ALU.min))
                    then(dve.tensor_tensor(hot[:, k], ids, wide(which[:, k]), ALU.is_equal))
                    if k == 0:
                        then(dve.scalar_tensor_tensor(out=rest[:], in0=hot[:, k], scalar=-2.0, in1=score[:],
                                                      op0=ALU.mult, op1=ALU.add))
                dve.tensor_copy(hotb[:], hot[:].rearrange("p k t e -> p (k t e)")).then_inc(hots, 1)
                then(dve.tensor_tensor(total[:], best[:, 0], best[:, 1], ALU.add))
                then(dve.reciprocal(total[:], total[:]))
                gate = keep["gate"]
                for k in range(TOPK):
                    then(dve.tensor_tensor(gate[:, k], best[:, k], total[:], ALU.mult))
                dve.wait_ge(prefix, 1)
                by_expert = totals[:].rearrange("p (n e) -> p e n", e=E)
                then(dve.tensor_copy(count[:], by_expert))
                for e in range(E):
                    then(dve.tensor_tensor_scan(running[:, e], onesf[:], count[:, e], 0.0, ALU.mult, ALU.add))
                then(dve.tensor_tensor(running[:], running[:], count[:], ALU.subtract))
                then(dve.tensor_tensor(place[:], inside[:].rearrange("p (n e) -> p n e", e=E),
                                       running[:].rearrange("p e n -> p n e"), ALU.add))
                then(dve.tensor_tensor(place[:], place[:], hot[:].rearrange("p k t e -> p (k t) e"), ALU.mult))
                then(dve.tensor_reduce(loc[:], place[:], AX, ALU.add))
                flat = lambda a: a[:].rearrange("p k t -> p (k t)")
                then(dve.tensor_scalar(valid[:], loc[:], float(CAP), None, ALU.is_lt))
                then(dve.tensor_scalar(loc[:], loc[:], float(CAP - 1), None, ALU.min))
                then(dve.scalar_tensor_tensor(out=slotf[:], in0=flat(which), scalar=float(CAP), in1=loc[:],
                                              op0=ALU.mult, op1=ALU.add))
                then(dve.tensor_copy(flat(keep["slot"]), slotf[:]))
                then(dve.tensor_tensor(flat(gate), flat(gate), valid[:], ALU.mult))
                then(dve.tensor_tensor(destf[:], slotf[:], flat(spill), ALU.subtract))
                then(dve.tensor_tensor(destf[:], destf[:], valid[:], ALU.mult))
                then(dve.tensor_tensor(destf[:], destf[:], flat(spill), ALU.add))
                then(dve.tensor_copy(flat(keep["dest"]), destf[:]))


def attend_phase(nc, io, dram, keep):
    with ExitStack() as ctx:
        def sb(name, shape, dt=F32):
            return ctx.enter_context(nc.sbuf_tensor("at_" + name, shape, dt))

        def ps(name, shape, dt=F32):
            return ctx.enter_context(nc.psum_tensor("at_" + name, shape, dt))

        NBUF, NE = 3, 2 * G
        ident = sb("ident", [P, P])
        identb = sb("identb", [P, P], BF16)
        mask_q = sb("mask_q", [P, P], BF16)
        mask_k = sb("mask_k", [P, P], BF16)
        qs = sb("qs", [ROWS, NBUF, G, M], BF16)
        ks = sb("ks", [ROWS, NBUF, G, M], BF16)
        vs = sb("vs", [P, NBUF, NQT, G * HW])
        ex = sb("ex", [P, NE, 2 * SEG])
        part = sb("part", [P, G * NQT, SPB])
        negmax = sb("negmax", [P, G * NQT])
        restT = sb("restT", [G * NQT, P])
        mT = sb("mT", [G * NQT, PIECE, P], BF16)
        osb = sb("osb", [P, SEG])
        rden = sb("rden", [P, TT, G])
        yout = sb("yout", [P, 2, TT, G * HD])
        idx = sb("idx", [P, 2], I32)
        tok = sb("tok", [P, 2], I32)
        NP1 = 3
        p1 = ps("p1", [P, NP1, SEG])
        st = ps("st", [P, 2, 2 * SEG])
        ob = ps("ob", [P, SEG])
        turned_max = p1[0:G * NQT, 0, 0:P]

        steps = []
        for qc in range(SPB):
            first = TT * qc
            for j in range(0, first, 2):
                steps.append((qc, [(j, 0, SEG), (j + 1, SEG, SEG)]))
            steps.append((qc, [(first, 0, SEG), (first + 1, SEG, SEG - P), (first + 3, 2 * SEG - P, P)]))
            steps.append((qc, [(first + 2, 0, SEG - 2 * P)]))
        NS = len(steps)
        NU = NS * G
        last_of = [max(s for s in range(NS) if steps[s][0] == qc) for qc in range(SPB)]
        chunks = [(h, qt, ch) for h in range(G) for qt in range(NQT) for ch in range(qt // TT + 1)]
        NC = len(chunks)
        TURN_AT = NU - 6

        def due(u):
            return range(min(NC, -(-NC * u // TURN_AT)), min(NC, -(-NC * (u + 1) // TURN_AT)))

        counts = dict(s1=NC, mx=NC, neg=1, negT=1, mT=1, m_in=PIECE, st=NU, ex=NU, pv=NS, oc=SPB, ot=SPB,
                      norm=SPB, y_out0=SPB // 2, y_out1=SPB // 2, rden=SPB)
        for i in range(NBUF):
            counts[f"in{i}"] = 1
        NLOAD = 2 * 12 + 2
        ev = Events(nc, ctx, "at", counts, {"m_in", "y_out0", "y_out1"})
        for i in range(NBUF):
            ev.unit[f"in{i}"] = 16 * NLOAD
        consts = ctx.enter_context(nc.semaphore("at_consts"))
        ready = ctx.enter_context(nc.semaphore("at_ready"))
        passed = ctx.enter_context(nc.semaphore("at_passed"))
        setup = ctx.enter_context(nc.semaphore("at_setup"))
        mstep = ctx.enter_context(nc.semaphore("at_mstep"))
        scat_copy = ctx.enter_context(nc.semaphore("at_scat_copy"))
        scattered = ctx.enter_context(nc.semaphore("at_scattered"))

        def group_loop(e, body):
            with e.Fori(0, (NGROUPS - 1) // NBUF) as i:
                for r in range(NBUF):
                    body(i * NBUF + r, r, i, True)
            body(NGROUPS - 1, (NGROUPS - 1) % NBUF, (NGROUPS - 1) // NBUF, False)

        def turn_of(g_const, i, r):
            return i + r // NBUF

        with nc.Block() as block:
            @block.sync
            def _(sp):
                for out, in_ in ((ident[:], io["c_ident"]), (identb[:], io["c_identb"]),
                                 (mask_q[:], io["c_mask_q"]), (mask_k[:], io["c_mask_k"])):
                    sp.dma_start(out, in_).then_inc(consts, 16)
                for rows in (qs, ks):
                    for i in range(NBUF):
                        sp.dma_start(rows[STACK:ROWS, i], io["c_ones"][0:PIECE, :].unsqueeze(1).to_broadcast([PIECE, G, M])).then_inc(consts, 16)
                sp.wait_ge(ready, 1)

                def load(g, r):
                    for m, rows, pieces in ((0, qs, Q_PIECES), (1, ks, K_PIECES)):
                        for s, i in enumerate(pieces):
                            for f in range(2):
                                at = s * HD + f * (HD // 2)
                                src = dram["qk"][m, g, i, f, :, :].rearrange("o (h j) t -> j (o h) t", j=HD // 2)
                                sp.dma_start(rows[at:at + HD // 2, r], src).then_inc(ev.sem[f"in{r}"], 16)
                    for f in range(2):
                        src = dram["v"][g, f * (M // 2):(f + 1) * (M // 2), :].rearrange("o (t p) w -> p (o t) w", p=P)
                        sp.dma_start(vs[:, r, f * (NQT // 2):(f + 1) * (NQT // 2)], src).then_inc(ev.sem[f"in{r}"], 16)

                def maxima(g, r):
                    ev.wait(sp, "mT", g, 1)
                    for i in range(PIECE):
                        dst = qs[STACK + i:STACK + i + 1, r].rearrange("o h (t p) -> o (h t) p", p=P)
                        ev.done(sp.dma_start(dst, mT[:, i, :]), "m_in")

                def group(g, r, more):
                    for qc in range(SPB):
                        if more and qc == SPB - 1:
                            maxima(g + 1, (r + 1) % NBUF)
                        ev.wait(sp, "norm", g, qc + 1)
                        dst = dram["y"][bass.ds(g, 1), qc * SEG:(qc + 1) * SEG, :]
                        ev.done(sp.dma_start(dst.rearrange("o (t p) d -> p (o t) d", p=P), yout[:, qc % 2]), f"y_out{qc % 2}")

                load(slice(0, 1), 0)
                load(slice(1, 2), 1)
                maxima(0, 0)

                def turn(i, loads):
                    for r in range(NBUF):
                        g = i * NBUF + r
                        if r < loads:
                            ev.wait(sp, "pv", g, 0)
                            sp.sem_inc(passed, 1)
                            load(bass.ds(g + 2, 1), (r + 2) % NBUF)
                        group(g, r, True)

                NTURN = (NGROUPS - 1) // NBUF
                with sp.Fori(0, NTURN - 1) as i:
                    turn(i, NBUF)
                turn(NTURN - 1, NBUF - 1)
                group(NGROUPS - 1, 0, False)
                for k in range(2):
                    sp.wait_ge(ev.sem[f"y_out{k}"], 16 * (NGROUPS * SPB // 2 + 1))

            @block.gpsimd
            def _(pool):
                pool.wait_ge(ready, 1)
                def scatter(i):
                    pool.tensor_copy(idx[:], keep["dest"][:, :, bass.ds(i, 1)].rearrange("p k o -> p (k o)")).then_inc(scat_copy, 1)
                    pool.tensor_copy(tok[:, 0:1], keep["token"][:, bass.ds(i, 1)]).then_inc(scat_copy, 1)
                    pool.wait_ge(scat_copy, 2 * i + 2)
                    pool.sem_inc(passed, 1)
                    for k in range(TOPK):
                        pool.indirect_dma_start(
                            out=dram["table"], out_offset=bass.IndirectOffsetOnAxis(ap=idx[:, k:k + 1], axis=0),
                            in_=tok[:, 0:1], in_offset=None).then_inc(scattered, 16)

                scatter(0)
                with pool.Fori(1, NT) as i:
                    pool.wait_ge(scattered, 16 * TOPK * i)
                    pool.sem_inc(passed, 1)
                    scatter(i)
                pool.wait_ge(scattered, 16 * TOPK * NT)

            @block.tensor
            def _(pe):
                pe.wait_ge(consts, 16 * (4 + 2 * NBUF))
                pe.wait_ge(ready, 1)

                def row_scores(g, r, n):
                    h, qt, ch = chunks[n]
                    w = min(SEG, (qt + 1) * P - ch * SEG)
                    diag = ch == qt // TT
                    ev.wait(pe, "mx", g, max(n - NP1 + 1, 0))
                    if n == 0:
                        ev.wait(pe, "mT", g, 0)
                    out = p1[:, n % NP1, 0:w]
                    last = pe.matmul(out, qs[0:STACK, r, h, qt * P:(qt + 1) * P], ks[0:STACK, r, h, ch * SEG:ch * SEG + w],
                                     start=True, stop=not diag)
                    if diag:
                        last = pe.matmul(out[:, w - P:w], identb[:], mask_q[:], start=False, stop=True)
                    ev.done(last, "s1")

                def turn_maxima(g):
                    ev.wait(pe, "neg", g, 1)
                    pe.sem_inc(passed, 1)
                    ev.done(pe.transpose(turned_max, negmax[:], ident[:]), "negT")

                def key_scores(g, r, u):
                    s, h = u // G, u % G
                    qc, tiles = steps[s]
                    ev.wait(pe, "ex", g, max(u - 1, 0))
                    for kt, at, w in tiles:
                        diag = kt >= TT * qc
                        out = st[:, u % 2, at:at + w]
                        q0 = (qc + 1) * SEG - w
                        last = pe.matmul(out, ks[:, r, h, kt * P:(kt + 1) * P], qs[:, r, h, q0:q0 + w],
                                         start=True, stop=not diag)
                        if diag:
                            last = pe.matmul(out[:, 0:P], identb[:], mask_k[:], start=False, stop=True)
                    ev.done(last, "st")

                def values(g, r, s, half):
                    qc, tiles = steps[s]
                    if half == 0:
                        ev.wait(pe, "ex", g, G * s + G)
                        if s == 0 or steps[s - 1][0] != qc:
                            ev.wait(pe, "norm", g, qc)
                    cut = (len(tiles) + 1) // 2
                    for kt, at, w in tiles[:cut] if half == 0 else tiles[cut:]:
                        for h in range(G):
                            last = pe.matmul(ob[h * HW:(h + 1) * HW, SEG - w:SEG], vs[:, r, kt, h * HW:(h + 1) * HW],
                                             ex[:, (G * s + h) % NE, at:at + w], start=(kt == 0),
                                             stop=(s == last_of[qc] and kt == tiles[-1][0]),
                                             skip_group_check=True)
                    if half == (len(tiles) > 1):
                        ev.done(last, "pv")

                def turn(g, qc):
                    ev.wait(pe, "oc", g, qc + 1)
                    for t in range(TT):
                        last = pe.transpose(ob[:, t * P:(t + 1) * P], osb[:, t * P:(t + 1) * P], ident[:])
                    ev.done(last, "ot")

                def group(g, r, i, more):
                    ev.wait(pe, "m_in", g, PIECE)
                    if more:
                        ev.wait(pe, f"in{(r + 1) % NBUF}", i + (r + 1) // NBUF, 1)
                    for u in range(NU):
                        s, h = u // G, u % G
                        now = list(due(u)) if more else []
                        for n in now[:1]:
                            row_scores(g + 1, (r + 1) % NBUF, n)
                        key_scores(g, r, u)
                        for n in now[1:]:
                            row_scores(g + 1, (r + 1) % NBUF, n)
                        if more and u == TURN_AT + 1:
                            turn_maxima(g + 1)
                        if h % 2 == 1 and s >= 1:
                            values(g, r, s - 1, h // 2)
                        if h == 3 and s >= 1 and s - 1 in last_of:
                            turn(g, last_of.index(s - 1))
                    for half in range(2):
                        values(g, r, NS - 1, half)
                    turn(g, SPB - 1)
                    
                ev.wait(pe, "in0", 0, 1)
                for n in range(NC):
                    row_scores(0, 0, n)
                turn_maxima(0)
                group_loop(pe, group)

            @block.scalar
            def _(act):
                act.wait_ge(ready, 1)

                def out_copy(g, qc):
                    ev.wait(act, "pv", g, last_of[qc] + 1)
                    ev.done(act.activation(osb[:], ob[:], ACT.Copy), "oc")

                def group(g, r, i, more):
                    for u in range(NU):
                        s, h = u // G, u % G
                        width = steps[s][1][-1][1] + steps[s][1][-1][2]
                        ev.wait(act, "st", g, u + 1)
                        if s >= 2:
                            ev.wait(act, "pv", g, s - 1)
                        elif h == 0 and s == 0:
                            ev.wait(act, "pv", g, 0)
                        ev.done(act.activation(ex[:, u % NE, 0:width], st[:, u % 2, 0:width], ACT.Exp, scale=SCALE), "ex")
                        if h == 2 and s >= 1 and s - 1 in last_of:
                            out_copy(g, last_of.index(s - 1))
                    out_copy(g, SPB - 1)

                group_loop(act, group)

            @block.vector
            def _(dve):
                ev.start(dve)
                dve.memset(part[:], LOWEST).then_inc(setup, 1)
                dve.wait_ge(setup, 1)
                dve.sem_inc(ready, 1)

                def chunk_max(g, n):
                    h, qt, ch = chunks[n]
                    w = min(SEG, (qt + 1) * P - ch * SEG)
                    ev.wait(dve, "s1", g, n + 1)
                    at = h * NQT + qt
                    ev.done(dve.tensor_reduce(part[:, at, ch:ch + 1], p1[:, n % NP1, 0:w], AX, ALU.max), "mx")

                def negate(g):
                    ev.wait(dve, "mx", g, NC)
                    dve.tensor_reduce(negmax[:], part[:], AX, ALU.max).then_inc(mstep, 1)
                    dve.wait_ge(mstep, 4 * g + 1)
                    ev.done(dve.tensor_scalar(negmax[:], negmax[:], -1.0, None, ALU.mult), "neg")

                def split(g):
                    ev.wait(dve, "negT", g, 1)
                    ev.wait(dve, "m_in", g, 0)
                    src = turned_max
                    dve.tensor_copy(mT[:, 0], src).then_inc(mstep, 1)
                    dve.wait_ge(mstep, 4 * g + 2)
                    dve.tensor_tensor(restT[:], src, mT[:, 0], ALU.subtract).then_inc(mstep, 1)
                    dve.wait_ge(mstep, 4 * g + 3)
                    dve.tensor_copy(mT[:, 1], restT[:]).then_inc(mstep, 1)
                    dve.wait_ge(mstep, 4 * g + 4)
                    ev.done(dve.tensor_tensor(mT[:, 2], restT[:], mT[:, 1], ALU.subtract), "mT")

                def normalise(g, qc):
                    ev.wait(dve, "ot", g, qc + 1)
                    turned = ob[:].rearrange("p (t h w) -> p t h w", t=TT, w=HW)
                    ev.wait(dve, f"y_out{qc % 2}", g, qc // 2)
                    ev.done(dve.reciprocal(rden[:], turned[:, :, :, HD]), "rden")
                    ev.wait(dve, "rden", g, qc + 1)
                    out = yout[:, qc % 2].rearrange("p t (h d) -> p t h d", d=HD)
                    ev.done(dve.tensor_tensor(out, turned[:, :, :, 0:HD], rden[:].unsqueeze(3).to_broadcast([P, TT, G, HD]),
                                              ALU.mult), "norm")

                def group(g, r, i, more):
                    for u in range(NU):
                        s, h = u // G, u % G
                        if more:
                            for n in due(u):
                                chunk_max(g + 1, n)
                            if u == TURN_AT - 1:
                                negate(g + 1)
                            if u == TURN_AT + 1:
                                split(g + 1)
                        if h == 3 and s >= 1 and s - 1 in last_of:
                            normalise(g, last_of.index(s - 1))
                    normalise(g, SPB - 1)

                for n in range(NC):
                    chunk_max(0, n)
                negate(0)
                split(0)
                group_loop(dve, group)


def experts_phase(nc, io, dram):
    with ExitStack() as ctx:
        def sb(name, shape, dt=F32):
            return ctx.enter_context(nc.sbuf_tensor("e_" + name, shape, dt))

        def ps(name, shape, dt=F32):
            return ctx.enter_context(nc.psum_tensor("e_" + name, shape, dt))

        HC = HID // P
        NCH = CAP // SEG
        ident = sb("ident", [P, P])
        b1 = sb("b1", [P, E, HC])
        b2 = sb("b2", [P, E, D])
        w1 = sb("w1", [P, 2, DC, HID])
        w2 = sb("w2", [P, 2, HC, D])
        table = sb("table", [P, 2, CAP // P], I32)
        xg = sb("xg", [P, 2, TT, D])
        xT = sb("xT", [P, 2, DC, SEG])
        hT = sb("hT", [P, 2, HC, SEG])
        og = sb("og", [P, 2, TT, D])
        b2now = sb("b2now", [P, 2, D])
        b1now = sb("b1now", [P, 2, HC])
        tb = ps("tb", [P, DC, SEG])
        hb = ps("hb", [P, 2, SEG])
        ob = ps("ob", [P, 2, SEG])

        TURN = 2 * NCH
        counts = dict(tr=1, trc=DC, h=HC, relu=HC // 2, relu2=HC // 2, o=TT, oc=TT, out0=1, out1=1)
        ev = Events(nc, ctx, "e", counts, {"out0", "out1"})
        wev = Events(nc, ctx, "ew", dict(w0=2, w1=2, t0=1, t1=1, now=4, g0=TT, g1=TT), {"w0", "w1", "t0", "t1", "g0", "g1"}, {"g0", "g1"})
        consts = ctx.enter_context(nc.semaphore("e_consts"))
        ready = ctx.enter_context(nc.semaphore("e_ready"))
        passed = ctx.enter_context(nc.semaphore("e_passed"))

        with nc.Block() as block:
            @block.sync
            def _(sp):
                for out, in_ in ((ident[:], io["c_ident"]), (b1[:], io["b1T"]), (b2[:], io["b2"].partition_broadcast(P))):
                    sp.dma_start(out, in_).then_inc(consts, 16)
                sp.wait_ge(ready, 1)

                def load(i, u, chunks_before):
                    ev.wait(sp, "o", chunks_before, 0)
                    sp.sem_inc(passed, 1)
                    e = bass.ds(2 * i + u, 1)
                    wev.done(sp.dma_start(table[:, u], dram["table"][bass.ds((2 * i + u) * CAP, CAP), :].rearrange("(p c) o -> p (c o)", p=P)), f"t{u}")
                    wev.done(sp.dma_start(w1[:, u], io["w1"][e].rearrange("o (k p) h -> p (o k) h", p=P)), f"w{u}")
                    wev.done(sp.dma_start(w2[:, u], io["w2"][e].rearrange("o (k p) d -> p (o k) d", p=P)), f"w{u}")

                with sp.Fori(0, E // 2) as i:
                    for u in range(2):
                        load(i, u, i * TURN + u * NCH - NCH if u else i * TURN)
                    for u in range(2):
                        for q in range(NCH):
                            n = i * TURN + u * NCH + q
                            ev.wait(sp, "oc", n, TT)
                            sp.sem_inc(passed, 1)
                            rows = dram["eo"][bass.ds((2 * i + u) * CAP, CAP), :].rearrange("(p c) d -> p c d", p=P)
                            ev.done(sp.dma_start(rows[:, q * TT:(q + 1) * TT, :], og[:, q % 2]), f"out{q % 2}")
                for k in range(2):
                    sp.wait_ge(ev.sem[f"out{k}"], 16 * (E * NCH // 2 + 1))

            @block.gpsimd
            def _(pool):
                pool.wait_ge(ready, 1)
                with pool.Fori(0, E // 2) as i:
                    for u in range(2):
                        wev.wait(pool, f"t{u}", i, 1)
                        for q in range(NCH):
                            n = i * TURN + u * NCH + q
                            ev.wait(pool, "tr", n - 1 if u or q else n, 0)
                            pool.sem_inc(passed, 1)
                            for t in range(TT):
                                c = q * TT + t
                                pool.indirect_dma_start(
                                    out=xg[:, q % 2, t, :], out_offset=None, in_=dram["xn1"],
                                    in_offset=bass.IndirectOffsetOnAxis(ap=table[:, u, c:c + 1], axis=0)
                                ).then_inc(wev.sem[f"g{q % 2}"], 16)

            @block.tensor
            def _(pe):
                pe.wait_ge(consts, 48)
                pe.wait_ge(ready, 1)

                def turn(i, c):
                    n = i * TURN + c
                    wev.wait(pe, f"g{c % 2}", i * (TURN // 2) + c // 2, TT)
                    ev.wait(pe, "trc", n, 0)
                    for k in range(DC):
                        for t in range(TT):
                            last = pe.transpose(tb[:, k, t * P:(t + 1) * P], xg[:, c % 2, t, k * P:(k + 1) * P], ident[:])
                    ev.done(last, "tr")

                with pe.Fori(0, E // 2) as i:
                    turn(i, 0)
                    for c in range(TURN):
                        n = i * TURN + c
                        u = c // NCH
                        if c % NCH == 0:
                            wev.wait(pe, f"w{u}", i, 2)
                        ev.wait(pe, "trc", n, DC)
                        for m in range(HC):
                            ev.wait(pe, ("relu", "relu2")[m % 2], n, m // 2)
                            for k in range(DC):
                                last = pe.matmul(hb[:, m % 2, :], w1[:, u, k, m * P:(m + 1) * P], xT[:, c % 2, k, :],
                                                 start=(k == 0), stop=(k == DC - 1))
                            ev.done(last, "h")
                        if c < TURN - 1:
                            turn(i, c + 1)
                        ev.wait(pe, "relu", n, HC // 2)
                        ev.wait(pe, "relu2", n, HC // 2)
                        for t in range(TT):
                            ev.wait(pe, "oc", n, max(t - 1, 0))
                            for m in range(HC):
                                last = pe.matmul(ob[:, t % 2, 0:D], hT[:, c % 2, m, t * P:(t + 1) * P], w2[:, u, m, :],
                                                 start=(m == 0), stop=(m == HC - 1))
                            ev.done(last, "o")

            @block.scalar
            def _(act):
                act.wait_ge(consts, 48)
                act.wait_ge(ready, 1)
                with act.Fori(0, E // 2) as i:
                    for c in range(TURN):
                        n = i * TURN + c
                        u = c // NCH
                        if c % NCH == 0:
                            wev.wait(act, "now", i, 2 * u + 2)
                        ev.wait(act, "tr", n, 1)
                        ev.wait(act, "h", n, 0)
                        for k in range(DC):
                            ev.done(act.activation(xT[:, c % 2, k, :], tb[:, k, :], ACT.Copy), "trc")
                        for m in range(0, HC, 2):
                            ev.wait(act, "h", n, m + 1)
                            if m == 0:
                                ev.wait(act, "o", n, 0)
                            ev.done(act.activation(hT[:, c % 2, m, :], hb[:, 0, :], ACT.Relu, bias=b1now[:, u, m:m + 1]), "relu")

            @block.vector
            def _(dve):
                ev.start(dve)
                wev.start(dve)
                dve.wait_ge(consts, 48)
                dve.sem_inc(ready, 1)
                with dve.Fori(0, E // 2) as i:
                    for c in range(TURN):
                        n = i * TURN + c
                        u = c // NCH
                        if c % NCH == 0:
                            ev.wait(dve, "relu", n, 0)
                            dve.sem_inc(passed, 1)
                            wev.done(dve.tensor_copy(b1now[:, u:u + 1], b1[:, bass.ds(2 * i + u, 1)]), "now")
                            wev.done(dve.tensor_copy(b2now[:, u:u + 1], b2[:, bass.ds(2 * i + u, 1)]), "now")
                            wev.wait(dve, "now", i, 2 * u + 2)
                        for m in range(1, HC, 2):
                            ev.wait(dve, "h", n, m + 1)
                            if m == 1:
                                ev.wait(dve, "o", n, 0)
                            ev.done(dve.tensor_scalar(hT[:, c % 2, m, :], hb[:, 1, :], b1now[:, u, m:m + 1], 0.0,
                                                      ALU.add, ALU.max), "relu2")
                        for t in range(TT):
                            ev.wait(dve, "o", n, t + 1)
                            if t == 0:
                                ev.wait(dve, f"out{c % 2}", i * (TURN // 2) + c // 2, 0)
                            ev.done(dve.tensor_tensor(og[:, c % 2, t, :], ob[:, t % 2, 0:D], b2now[:, u], ALU.add), "oc")


def combine_phase(nc, io, dram, keep, out):
    with ExitStack() as ctx:
        def sb(name, shape, dt=F32):
            return ctx.enter_context(nc.sbuf_tensor("f_" + name, shape, dt))

        def ps(name, shape, dt=F32):
            return ctx.enter_context(nc.psum_tensor("f_" + name, shape, dt))

        ident = sb("ident", [P, P])
        wo = sb("wo", [P, DC, D])
        bo = sb("bo", [P, D])
        y = sb("y", [P, 2, TT, NG, G * HD])
        x1 = sb("x1", [P, 2, TT, D])
        slot = sb("slot", [P, 2, TOPK, TT], I32)
        gate = sb("gate", [P, 2, TOPK, TT])
        rows = sb("rows", [P, 2, TOPK, TT, D])
        yT = sb("yT", [P, DC, SEG])
        z = sb("z", [P, TT, D])
        th = sb("th", [P, TT, D])
        s = sb("s", [P, TT, D])
        res = sb("res", [P, 2, TT, D])
        tb = ps("tb", [P, DC, SEG])
        sc = ps("sc", [P, 2, SEG])

        counts = dict(y_in=1, slot=2, rows=TOPK * TT, tr=1, trc=DC, so=2, sb=2, z=1, th=1, res=1, out=1)
        inputs = {f"{a}{k}": c for a, c in (("in", NG + 1), ("rows", TOPK * TT), ("out", 1)) for k in range(2)}
        ev = Events(nc, ctx, "f", dict(slot=2, tr=1, trc=DC, so=2, sb=2, z=1, th=1, res=1), set())
        par = Events(nc, ctx, "fp", inputs, set(inputs), {"rows0", "rows1"})
        consts = ctx.enter_context(nc.semaphore("f_consts"))
        ready = ctx.enter_context(nc.semaphore("f_ready"))
        passed = ctx.enter_context(nc.semaphore("f_passed"))
        dve_step = ctx.enter_context(nc.semaphore("f_dve_step"))
        DVE_STEPS = SPB * 9
        out_rows = out.rearrange("b m d -> (b m) d")

        with nc.Block() as block:
            @block.sync
            def _(sp):
                for dst, src in ((ident[:], io["c_ident"]), (wo[:], io["wo1T"].rearrange("(k p) n -> p k n", p=P)),
                                 (bo[:], io["bo1"].partition_broadcast(P))):
                    sp.dma_start(dst, src).then_inc(consts, 16)
                sp.wait_ge(ready, 1)
                with sp.Fori(0, B) as b:
                    for c in range(SPB):
                        n = b * SPB + c
                        for ahead in range(c if c == 0 else c + 1, min(c + 2, SPB)):
                            ev.wait(sp, "res", n, 0)
                            k = ahead % 2
                            for hg in range(NG):
                                src = dram["y"][bass.ds(b * NG + hg, 1), ahead * SEG:(ahead + 1) * SEG, :]
                                sp.dma_start(y[:, k, :, hg, :], src.rearrange("o (t p) d -> p (o t) d", p=P)).then_inc(par.sem[f"in{k}"], 16)
                            par.done(sp.dma_start(x1[:, k], dram["x1"][bass.ds(b * M + ahead * SEG, SEG), :].rearrange("(t p) d -> p t d", p=P)), f"in{k}")
                        ev.wait(sp, "res", n, 1)
                        par.done(sp.dma_start(out_rows[bass.ds(b * M + c * SEG, SEG), :].rearrange("(t p) d -> p t d", p=P),
                                              res[:, c % 2]), f"out{c % 2}")
                for k in range(2):
                    sp.wait_ge(par.sem[f"out{k}"], 16 * (NSEG // 2 + 1))

            @block.gpsimd
            def _(pool):
                pool.wait_ge(ready, 1)
                with pool.Fori(0, B) as b:
                    for c in range(SPB):
                        n = b * SPB + c
                        ev.wait(pool, "slot", n, 2)
                        ev.wait(pool, "z", n - 1 if c else n, 0)
                        pool.sem_inc(passed, 1)
                        for k in range(TOPK):
                            for t in range(TT):
                                pool.indirect_dma_start(
                                    out=rows[:, c % 2, k, t, :], out_offset=None, in_=dram["eo"],
                                    in_offset=bass.IndirectOffsetOnAxis(ap=slot[:, c % 2, k, t:t + 1], axis=0)
                                ).then_inc(par.sem[f"rows{c % 2}"], 16)

            @block.tensor
            def _(pe):
                pe.wait_ge(consts, 48)
                pe.wait_ge(ready, 1)
                with pe.Fori(0, B) as b:
                    for c in range(SPB):
                        n = b * SPB + c
                        par.wait(pe, f"in{c % 2}", b * (SPB // 2) + c // 2, NG + 1)
                        ev.wait(pe, "trc", n, 0)
                        ysrc = y[:, c % 2].rearrange("p t g d -> p t (g d)")
                        for k in range(DC):
                            for t in range(TT):
                                last = pe.transpose(tb[:, k, t * P:(t + 1) * P], ysrc[:, t, k * P:(k + 1) * P], ident[:])
                        ev.done(last, "tr")
                        ev.wait(pe, "trc", n, DC)
                        ev.wait(pe, "sb", n, 0)
                        for f in range(2):
                            for t in (2 * f, 2 * f + 1):
                                for k in range(DC):
                                    last = pe.matmul(sc[:, f, (t % 2) * D:(t % 2 + 1) * D], yT[:, k, t * P:(t + 1) * P],
                                                     wo[:, k, :], start=(k == 0), stop=(k == DC - 1))
                            ev.done(last, "so")

            @block.scalar
            def _(act):
                act.wait_ge(ready, 1)
                with act.Fori(0, B) as b:
                    for c in range(SPB):
                        n = b * SPB + c
                        ev.wait(act, "tr", n, 1)
                        ev.wait(act, "so", n, 0)
                        for k in range(DC):
                            ev.done(act.activation(yT[:, k, :], tb[:, k, :], ACT.Copy), "trc")
                        ev.wait(act, "z", n, 1)
                        ev.wait(act, "res", n, 0)
                        ev.done(act.activation(th[:], z[:], ACT.Tanh, scale=0.5), "th")

            @block.vector
            def _(dve):
                ev.start(dve)
                par.start(dve)
                dve.wait_ge(consts, 48)
                dve.sem_inc(ready, 1)
                with dve.Fori(0, B) as b:
                    st = Steps(dve, dve_step, b * DVE_STEPS, ev)
                    st.last = ev.sem["res"], ev.at("res", b * SPB, 0)

                    def places(c):
                        cols = bass.ds(b * (M // P) + c * TT, TT)
                        n = b * SPB + c
                        ev.wait(dve, "z", n - 1 if c else n, 0)
                        dve.sem_inc(passed, 1)
                        ev.done(dve.tensor_copy(slot[:, c % 2], keep["slot"][:, :, cols]), "slot")
                        ev.done(dve.tensor_copy(gate[:, c % 2], keep["gate"][:, :, cols]), "slot")

                    places(0)
                    for c in range(SPB):
                        n = b * SPB + c
                        st.step(n)
                        if c + 1 < SPB:
                            places(c + 1)
                        k = c % 2
                        par.wait(dve, f"rows{k}", b * (SPB // 2) + c // 2, TOPK * TT)
                        ev.wait(dve, "slot", n, 2)
                        ev.wait(dve, "th", n, 0)
                        for t in range(TT):
                            st.then(dve.tensor_scalar(s[:, t], rows[:, k, 1, t], gate[:, k, 1, t:t + 1], None, ALU.mult))
                        st.settle()
                        for t in range(TT):
                            last = dve.scalar_tensor_tensor(out=z[:, t], in0=rows[:, k, 0, t], scalar=gate[:, k, 0, t:t + 1],
                                                            in1=s[:, t], op0=ALU.mult, op1=ALU.add)
                            st.mark(last, "z") if t == TT - 1 else st.then(last)
                        st.settle()
                        for f in range(2):
                            ev.wait(dve, "so", n, f + 1)
                            st.mark(dve.tensor_tensor(s[:, 2 * f:2 * f + 2], sc[:, f, :].rearrange("p (t d) -> p t d", d=D),
                                                        bo[:].unsqueeze(1).to_broadcast([P, 2, D]), ALU.add), "sb")
                        ev.wait(dve, "th", n, 1)
                        st.then(dve.scalar_tensor_tensor(out=z[:], in0=th[:], scalar=1.0, in1=z[:], op0=ALU.add, op1=ALU.mult))
                        st.settle()
                        st.then(dve.scalar_tensor_tensor(out=z[:], in0=z[:], scalar=0.5, in1=s[:], op0=ALU.mult, op1=ALU.mult))
                        st.settle()
                        par.wait(dve, f"out{k}", b * (SPB // 2) + c // 2, 0)
                        par.wait(dve, f"in{k}", b * (SPB // 2) + c // 2, NG + 1)
                        st.mark(dve.tensor_tensor(res[:, k], z[:], x1[:, k], ALU.add), "res")
                        st.settle()
                    assert st.n == DVE_STEPS, st.n


def build(nc, io, out):
    with ExitStack() as ctx:
        dram = {name: nc.dram_tensor("s_" + name, shape, dt, kind="Internal").ap() for name, shape, dt in SCRATCH}
        keep = {name: ctx.enter_context(nc.sbuf_tensor("keep_" + name, shape, dt)) for name, shape, dt in (
            ("slot", [P, TOPK, NT], I32), ("dest", [P, TOPK, NT], I32), ("gate", [P, TOPK, NT], F32),
            ("token", [P, NT], I32))}
        layers_phase(nc, io, dram)
        route_phase(nc, io, dram, keep)
        attend_phase(nc, io, dram, keep)
        experts_phase(nc, io, dram)
        combine_phase(nc, io, dram, keep, out)


SCRATCH = [
    ("x1", (T, D), F32), ("xn1", (T, D), F32), ("qk", (2, NGROUPS, PIECE, 2, G * HD // 2, M), BF16),
    ("v", (NGROUPS, M, G * HW), F32), ("logits", (T, E), F32), ("table", (NSLOT + TOPK * T, 1), I32),
    ("y", (NGROUPS, M, G * HD), F32), ("eo", (NSLOT, D), F32),
]


def constants():
    bf = mybir.dt.np(BF16)
    i = np.arange(P)
    inv_freq = (np.float32(1.0) / np.float32(10000.0) ** (np.arange(0, HD, 2, dtype=np.float32) / np.float32(HD)))
    angle = np.arange(M, dtype=np.float32)[None, :] * inv_freq.astype(np.float32)[i % (HD // 2)][:, None]
    token = (np.arange(NT)[None, :] * P + i[:, None])
    return {
        "c_ident": np.eye(P, dtype=np.float32),
        "c_identb": np.eye(P).astype(bf),
        "c_headmask": (i[:, None] // HD == np.arange(H // DC)[None, :]).astype(np.float32),
        "c_rope": np.stack([np.cos(angle), np.sin(angle)], axis=1).astype(np.float32),
        "c_mask_q": np.where(i[None, :] <= i[:, None], 0.0, MASKED).astype(bf),
        "c_mask_k": np.where(i[:, None] <= i[None, :], 0.0, MASKED).astype(bf),
        "c_before": (i[:, None] < i[None, :]).astype(bf),
        "c_ones": np.ones((P, 2048)).astype(bf),
        "c_expert": np.tile(np.arange(E, dtype=np.float32), (P, 1)),
        "c_token": token.astype(np.int32),
        "c_spill": np.stack([NSLOT + k * T + token for k in range(TOPK)], axis=1).astype(np.float32),
    }


def layout(a):
    t = lambda w: np.ascontiguousarray(np.asarray(w).T)
    pairs = lambda w: np.asarray(w).reshape(H, HD // 2, 2, -1).transpose(2, 0, 1, 3).reshape(D, -1)
    bias = lambda v: pairs(np.asarray(v)[:, None]).reshape(2, P)
    return {
        "x": np.asarray(a["L0_attn_x"]),
        "wqkv0T": t(a["L0_attn_Wqkv"]), "wout0T": t(a["L0_attn_Wout"]), "wfT": t(a["L0_ffn_weight_fp8"]),
        "fbias": np.asarray(a["L0_ffn_bias"]), "in_scale": np.asarray(a["L0_ffn_input_scale"]),
        "w_scale": np.asarray(a["L0_ffn_weight_scale"]),
        "wqk1T": np.ascontiguousarray(np.concatenate([pairs(a["L1_attn_wq"]), pairs(a["L1_attn_wk"])]).T),
        "bqk1": np.ascontiguousarray(np.concatenate([bias(a["L1_attn_bq"]), bias(a["L1_attn_bk"])]).T),
        "wvg1T": np.ascontiguousarray(np.concatenate([t(a["L1_attn_wv"]), np.asarray(a["L1_ffn_wg"])], axis=1)),
        "bv1": np.asarray(a["L1_attn_bv"]), "wo1T": t(a["L1_attn_wo"]), "bo1": np.asarray(a["L1_attn_bo"]),
        "w1": np.asarray(a["L1_ffn_w1"]),
        "b1T": np.ascontiguousarray(np.asarray(a["L1_ffn_b1"]).reshape(E, HID // P, P).transpose(2, 0, 1)),
        "w2": np.asarray(a["L1_ffn_w2"]), "b2": np.asarray(a["L1_ffn_b2"]),
    }


def kernel(**inputs):
    import concourse.bacc as _bacc
    from concourse.bass_utils import run_bass_kernel_spmd as _run

    arrays = {**layout(inputs), **constants()}
    nc = _bacc.Bacc("TRN2", target_bir_lowering=False, num_devices=1)
    io = {name: nc.dram_tensor(name, a.shape, mybir.dt.from_np(a.dtype), kind="ExternalInput").ap()
          for name, a in arrays.items()}
    out = nc.dram_tensor("out", (B, M, D), F32, kind="ExternalOutput").ap()
    build(nc, io, out)
    r = _run(nc, [arrays], core_ids=[0])
    return r.results[0]["out"]
```

```python
from contextlib import ExitStack

import numpy as np

import concourse.bass as bass
from concourse import mybir

ALU = mybir.AluOpType
ACT = mybir.ActivationFunctionType
AX = mybir.AxisListType.X
F32 = mybir.dt.float32
F32R = mybir.dt.float32r
BF16 = mybir.dt.bfloat16
F8 = mybir.dt.float8e4
I32 = mybir.dt.int32
U32 = mybir.dt.uint32

P = 128
B, M, D = 4, 2048, 256
T = B * M
H, HD = 16, 16
SEG, DIL, BLK = 512, 8, 64
NSEG = T // SEG
SPB = M // SEG
KN = SEG // DIL
NBLK = SEG // BLK
DC = D // P
TT = SEG // P
NT = T // P
E, TOPK, HID = 8, 2, 1024
CAP = TOPK * ((T + E - 1) // E)
NSLOT = E * CAP
SCALE = HD ** -0.5
LN_EPS = 1e-5
DEN_EPS = 1e-10
FP8_MAX = 448.0
G = 4
NG = H // G
NGROUPS = B * NG
NQT = M // P
HW = 32
PIECE = 3
STACK = 6 * HD
ROWS = STACK + PIECE
Q_PIECES = (0, 0, 1, 0, 1, 2)
K_PIECES = (0, 1, 0, 2, 1, 0)
RSQRT_MAGIC = 0x5F3759DF
LOWEST = -3.0e38
MASKED = -1.0e30


class Events:

    def __init__(self, nc, ctx, prefix, counts, dma, bare=()):
        self.bare = bare
        self.k, self.unit, self.sem = {}, {}, {}
        for name, k in counts.items():
            self.k[name], self.unit[name] = k, 16 if name in dma else 1
            self.sem[name] = ctx.enter_context(nc.semaphore(f"{prefix}_{name}"))

    def start(self, e):
        for name, s in self.sem.items():
            if name not in self.bare:
                e.sem_inc(s, self.unit[name])

    def at(self, name, n, j):
        return (n * self.k[name] + j + (name not in self.bare)) * self.unit[name]

    def wait(self, e, name, n, j):
        e.wait_ge(self.sem[name], self.at(name, n, j))

    def done(self, ins, name):
        return ins.then_inc(self.sem[name], self.unit[name])


class Steps:

    def __init__(self, e, sem, base, ev=None):
        self.e, self.sem, self.base, self.n, self.ev = e, sem, base, 0, ev
        self.last, self.seen = None, {}

    def then(self, ins):
        self.n += 1
        self.last = self.sem, self.base + self.n
        return ins.then_inc(self.sem, 1)

    def mark(self, ins, name, step=None):
        self.seen[name] = self.seen.get(name, 0) + 1
        self.last = self.ev.sem[name], self.ev.at(name, self.at if step is None else step, self.seen[name])
        return self.ev.done(ins, name)

    def step(self, n):
        self.at, self.seen = n, {}

    def settle(self, passed=None):
        self.e.wait_ge(*self.last)
        if passed is not None:
            self.e.sem_inc(passed, 1)


def layers_phase(nc, io, dram):
    with ExitStack() as ctx:
        def sb(name, shape, dt=F32):
            return ctx.enter_context(nc.sbuf_tensor("a_" + name, shape, dt))

        def ps(name, shape, dt=F32):
            return ctx.enter_context(nc.psum_tensor("a_" + name, shape, dt))

        ident = sb("ident", [P, P])
        headmask = sb("headmask", [P, H // DC])
        rope = sb("rope", [P, 2, M])
        wqkv0 = sb("wqkv0", [P, DC, 3 * D])
        wout0 = sb("wout0", [P, DC, D])
        wf = sb("wf", [P, DC, D])
        wf_rest = sb("wf_rest", [P, DC, D])
        wf_piece = [sb(f"wf_piece{i}", [P, DC, D], BF16) for i in range(PIECE)]
        fbias = sb("fbias", [P, D])
        in_scale = sb("in_scale", [P, 1])
        in_inv = sb("in_inv", [P, 1])
        square = sb("square", [P, DC, SEG])
        w_scale = sb("w_scale", [P, 1])
        wqk1 = sb("wqk1", [P, DC, 4 * P])
        bqk1 = sb("bqk1", [P, 4])
        wvg1 = sb("wvg1", [P, DC, D + E])
        bv1 = sb("bv1", [P, D])
        x = sb("x", [P, 2, TT, D])
        stats = sb("stats", [P, 2, TT, 6])
        mv = sb("mv", [P, 2, TT, 2])
        rstd = sb("rstd", [P, 2, TT])
        veps = sb("veps", [P, 2, TT])
        seed = sb("seed", [P, 2, TT], I32)
        newton = sb("newton", [P, 2, TT])
        xn = sb("xn", [P, TT, D])
        xnT = sb("xnT", [P, DC, SEG])
        clipped = sb("clipped", [P, DC, SEG])
        coarse = sb("coarse", [P, DC, SEG], F8)
        half8 = sb("half8", [P, DC, SEG], F8)
        is_big = sb("is_big", [P, DC, SEG], U32)
        doubled = sb("doubled", [P, DC, SEG], BF16)
        xq = sb("xq", [P, DC, SEG], BF16)
        qT = sb("qT", [P, DC, SEG])
        kbd = sb("kbd", [P, DC, H // DC, KN])
        vbd = sb("vbd", [P, H // 2, 2 * HW])
        keymax = sb("keymax", [P, 2, NBLK])
        shifted = sb("shifted", [P, 2, SEG])
        wexp = sb("wexp", [P, 2, SEG])
        oT = sb("oT", [P, 2, SEG])
        den = sb("den", [P, TT, G])
        rden = sb("rden", [P, TT, G])
        y = sb("y", [P, TT, D])
        yT = sb("yT", [P, DC, SEG])
        z = sb("z", [P, TT, D])
        ez = sb("ez", [P, TT, D])
        x1 = sb("x1", [P, TT, D])
        xn1 = sb("xn1", [P, TT, D])
        x1T = sb("x1T", [P, DC, SEG])
        qk = sb("qk", [P, 2, 2, SEG])
        rot = sb("rot", [P, 2, 2, SEG])
        prod = sb("prod", [P, 2, SEG])
        prod1 = sb("prod1", [P, 2, SEG])
        piece = [sb(f"piece{i}", [P, 2, 2, SEG], BF16) for i in range(PIECE)]
        v32 = sb("v32", [P, TT, H, HW])
        logit = sb("logit", [P, TT, E])

        tb = ps("tb", [P, DC, SEG])
        pb = ps("pb", [P, 2, SEG])
        kv = ps("kv", [P, SEG])
        sc = ps("sc", [P, 2, SEG])
        ob = ps("ob", [P, SEG])

        NP0 = H // 2
        counts = dict(
            var=1, rstd=1, xn=1, tr=1, trc=2, q=1, qc=1, kv=1, kvc=1, ff=2, ffc=2, quant=1, clip=1, round=2, wide=3,
            s=NP0, shift=NP0, wexp=NP0, pv=NP0, oc=4, ot=4, norm=4, ytr=1, ytc=2,
            so=2, sog=2, ez=2, gate=1, x1=1, x1_out=1,
            var1=1, rstd1=1, xn1=1, xn1_out=1, tr1=1, tr1c=2, pj=4, pjc=4, rot=1, rot1=1, p1=1, rest=1, p2=1, p3=1,
            qk_out=12, vj=4, vjc=4, lc=4, v_out=NG, l_out=1)
        counts.update(x_in0=1, x_in1=1)
        ev = Events(nc, ctx, "a", counts, {"x_in0", "x_in1", "x1_out", "xn1_out", "qk_out", "v_out", "l_out"})
        consts = ctx.enter_context(nc.semaphore("a_consts"))
        ready = ctx.enter_context(nc.semaphore("a_ready"))
        passed = ctx.enter_context(nc.semaphore("a_passed"))
        dve_step = ctx.enter_context(nc.semaphore("a_dve_step"))
        setup_step = ctx.enter_context(nc.semaphore("a_setup_step"))
        NCONST = 13
        pool_step = ctx.enter_context(nc.semaphore("a_pool_step"))
        NORM_STEPS = 13
        FIRST_STEPS, TURN_STEPS = 47, 49
        ROOT_STEPS = 11
        NORM_AT = 4
        VALUES_AT = {5: (0,), 6: (1, 2), 7: (3,)}
        POOL_FIRST, POOL_TURN = 2 * ROOT_STEPS, 24

        def turns(e, first, both, second):
            first()
            with e.Fori(0, B - 1) as b:
                for c in range(SPB):
                    both(b, c)
            for c in range(SPB - 1):
                both(B - 1, c)
            second()

        def last_turn(b, c):
            return isinstance(b, int) and b * SPB + c == NSEG - 2

        def place(b, c):
            return (b, c + 1) if c + 1 < SPB else (b + 1, 0)

        def rotary(c):
            return [rope[:, i, c * SEG:(c + 1) * SEG].unsqueeze(1).to_broadcast([P, 2, SEG]) for i in range(2)]

        with nc.Block() as block:
            @block.sync
            def _(sp):
                loads = [
                    (ident[:], io["c_ident"]), (headmask[:], io["c_headmask"]),
                    (rope[:], io["c_rope"]),
                    (wqkv0[:], io["wqkv0T"].rearrange("(k p) n -> p k n", p=P)),
                    (wout0[:], io["wout0T"].rearrange("(k p) n -> p k n", p=P)),
                    (wf[:], io["wfT"].rearrange("(k p) n -> p k n", p=P)),
                    (fbias[:], io["fbias"].partition_broadcast(P)),
                    (in_scale[:], io["in_scale"].partition_broadcast(P)),
                    (w_scale[:], io["w_scale"].partition_broadcast(P)),
                    (wqk1[:], io["wqk1T"].rearrange("(k p) n -> p k n", p=P)),
                    (bqk1[:], io["bqk1"]),
                    (wvg1[:], io["wvg1T"].rearrange("(k p) n -> p k n", p=P)),
                    (bv1[:], io["bv1"].partition_broadcast(P)),
                ]
                assert len(loads) == NCONST
                for out, in_ in loads:
                    sp.dma_start(out, in_).then_inc(consts, 16)
                def load(b, c, m):
                    src = io["x"][bass.ds(b, 1), c * SEG:(c + 1) * SEG, :]
                    ev.done(sp.dma_start(x[:, c % 2], src.rearrange("o (t p) d -> p (o t) d", p=P)), f"x_in{c % 2}")

                def store_x1(b, c, m):
                    ev.wait(sp, "x1", m, 1)
                    ev.done(sp.dma_start(dram["x1"][bass.ds(b * M + c * SEG, SEG), :].rearrange("(t p) d -> p t d", p=P),
                                         x1[:]), "x1_out")

                def store_layer1(b, c, n):
                    tok = bass.ds(b * M + c * SEG, SEG)
                    ev.wait(sp, "xn1", n, 1)
                    ev.done(sp.dma_start(dram["xn1"][tok, :].rearrange("(t p) d -> p t d", p=P), xn1[:]), "xn1_out")
                    for i in range(PIECE):
                        ev.wait(sp, f"p{i + 1}", n, 1)
                        for m in range(2):
                            for f in range(2):
                                dst = dram["qk"][m, bass.ds(b * NG, NG), i, f, :, c * SEG:(c + 1) * SEG]
                                ev.done(sp.dma_start(dst, piece[i][:, m, f, :]), "qk_out")
                    ev.wait(sp, "vjc", n, 4)
                    for hg in range(NG):
                        dst = dram["v"][bass.ds(b * NG + hg, 1), c * SEG:(c + 1) * SEG, :]
                        ev.done(sp.dma_start(dst.rearrange("o (t p) w -> p (o t) w", p=P),
                                             v32[:, :, hg * G:(hg + 1) * G, :].rearrange("p t h w -> p t (h w)")),
                                "v_out")
                    ev.wait(sp, "lc", n, 4)
                    ev.done(sp.dma_start(dram["logits"][:, bass.ds((b * SPB + c) * TT, TT), :], logit[:]), "l_out")

                def first():
                    load(0, 0, 0)
                    load(0, 1, 1)
                    store_x1(0, 0, 0)

                def both(b, c):
                    n = b * SPB + c
                    b1, c1 = place(b, c)
                    if c + 2 < SPB or not isinstance(b, int):
                        ev.wait(sp, "x1", n, 1)
                        b2, c2 = (b, c + 2) if c + 2 < SPB else (b + 1, c + 2 - SPB)
                        load(b2, c2, n + 2)
                    store_layer1(b, c, n)
                    store_x1(b1, c1, n + 1)

                turns(sp, first, both, lambda: store_layer1(B - 1, SPB - 1, NSEG - 1))
                for name in ("x1_out", "xn1_out", "qk_out", "v_out", "l_out"):
                    sp.wait_ge(ev.sem[name], 16 * (NSEG * counts[name] + 1))

            @block.gpsimd
            def _(pool):
                def inverse_root(st, n, i, var, rs):
                    ev.wait(pool, var, n, 1)
                    st.step(n)
                    v, root, tmp = veps[:, i], rstd[:, i], newton[:, i]
                    for step in range(3):
                        start = seed[:, i].bitcast(F32) if step == 0 else root
                        st.then(pool.tensor_tensor(tmp, start, start, ALU.mult))
                        st.settle()
                        st.then(pool.tensor_tensor(tmp, tmp, v, ALU.mult))
                        st.settle(passed)
                        st.then(pool.tensor_scalar(tmp, tmp, -0.5, 1.5, ALU.mult, ALU.add))
                        st.settle()
                        last = pool.tensor_tensor(root, start, tmp, ALU.mult)
                        if step < 2:
                            st.then(last)
                            st.settle()
                    st.mark(last, rs)

                def rotate(st, n, c):
                    st.step(n)
                    cos, sin = rotary(c)
                    ev.wait(pool, "pjc", n, 4)
                    ev.wait(pool, "p3", n, 0)
                    st.then(pool.tensor_tensor(rot[:, :, 1, :], qk[:, :, 0, :], sin, ALU.mult))
                    st.then(pool.tensor_tensor(prod1[:], qk[:, :, 1, :], cos, ALU.mult))
                    st.settle()
                    st.mark(pool.tensor_tensor(rot[:, :, 1, :], rot[:, :, 1, :], prod1[:], ALU.add), "rot1")

                def last_part(st, n):
                    st.step(n)
                    ev.wait(pool, "p2", n, 1)
                    ev.wait(pool, "qk_out", n, 0)
                    st.mark(pool.tensor_tensor(piece[2][:], qk[:], piece[1][:], ALU.subtract), "p3", n)

                def first():
                    st = Steps(pool, pool_step, 0, ev)
                    inverse_root(st, 0, 0, "var", "rstd")
                    st.settle()
                    inverse_root(st, 1, 0, "var", "rstd")
                    assert st.n == POOL_FIRST, st.n

                def both(b, c):
                    n = b * SPB + c
                    st = Steps(pool, pool_step, POOL_FIRST + n * POOL_TURN, ev)
                    more = not last_turn(b, c)
                    ev.wait(pool, "rstd", n + 1, 1)
                    ev.wait(pool, "p3", n, 0)
                    inverse_root(st, n, 1, "var1", "rstd1")
                    rotate(st, n, c)
                    if more:
                        inverse_root(st, n + 2, 0, "var", "rstd")
                    last_part(st, n)
                    assert st.n == POOL_TURN - (0 if more else ROOT_STEPS), st.n

                def second():
                    st = Steps(pool, pool_step, POOL_FIRST + (NSEG - 1) * POOL_TURN - ROOT_STEPS, ev)
                    ev.wait(pool, "rot1", NSEG - 1, 0)
                    inverse_root(st, NSEG - 1, 1, "var1", "rstd1")
                    rotate(st, NSEG - 1, SPB - 1)
                    last_part(st, NSEG - 1)

                turns(pool, first, both, second)

            @block.tensor
            def _(pe):
                pe.wait_ge(consts, 16 * NCONST)
                pe.wait_ge(ready, 1)

                def turn_tokens(src, name):
                    for k in range(DC):
                        for t in range(TT):
                            last = pe.transpose(tb[:, k, t * P:(t + 1) * P], src[:, t, k * P:(k + 1) * P], ident[:])
                    ev.done(last, name)

                def turn_first(m):
                    ev.wait(pe, "xn", m, 1)
                    ev.wait(pe, "ytc", m, 0)
                    turn_tokens(xn, "tr")

                def keys(m):
                    ev.wait(pe, "trc", m, 2)
                    ev.wait(pe, "norm", m, 0)
                    for f in range(DC):
                        for k in range(DC):
                            pe.matmul(kv[:, f * KN:(f + 1) * KN], wqkv0[:, k, D + f * P:D + (f + 1) * P],
                                      xnT[:, k, ::DIL], start=(k == 0), stop=(k == DC - 1))
                    for half in range(2):
                        for k in range(DC):
                            last = pe.matmul(kv[half * KN:(half + 1) * KN, D:2 * D], xnT[:, k, ::DIL],
                                             wqkv0[:, k, 2 * D:3 * D], start=(k == 0), stop=(k == DC - 1))
                    ev.done(last, "kv")

                def queries(m):
                    ev.wait(pe, "ffc", m, 0)
                    for f in range(DC):
                        for k in range(DC):
                            last = pe.matmul(pb[:, f, :], wqkv0[:, k, f * P:(f + 1) * P], xnT[:, k, :],
                                             start=(k == 0), stop=(k == DC - 1))
                    ev.done(last, "q")

                def scores(m, p):
                    if p == 0:
                        ev.wait(pe, "kvc", m, 1)
                        ev.wait(pe, "qc", m, 1)
                        ev.wait(pe, "sog", m, 0)
                    f, a = p // (NP0 // DC), 2 * (p % (NP0 // DC))
                    ev.wait(pe, "shift", m, max(p - 1, 0))
                    ev.done(pe.matmul(sc[:, p % 2, :], kbd[:, f, a:a + 2, :].rearrange("p a k -> p (a k)"),
                                      qT[:, f, :], start=True, stop=True), "s")

                def values(m, p):
                    ev.wait(pe, "wexp", m, p + 1)
                    if p % 2 == 0:
                        ev.wait(pe, "oc", m, p // 2)
                    r = (p % 2) * 2 * HW
                    ev.done(pe.matmul(ob[r:r + 2 * HW, :], vbd[:, p, :], wexp[:, p % 2, :], start=True, stop=True), "pv")

                def turn(m, g):
                    ev.wait(pe, "oc", m, g + 1)
                    ev.wait(pe, "norm", m, g)
                    for t in range(TT):
                        last = pe.transpose(kv[:, t * P:(t + 1) * P], oT[:, g % 2, t * P:(t + 1) * P], ident[:])
                    ev.done(last, "ot")

                def gate(m, f):
                    ev.wait(pe, "quant", m, 1)
                    if f == 0:
                        ev.wait(pe, "qc", m, 1)
                    ev.wait(pe, "vjc", m, 0)
                    ev.wait(pe, "lc", m, 0)
                    for t in (2 * f, 2 * f + 1):
                        i = 0
                        for w in wf_piece:
                            for k in range(DC):
                                last = pe.matmul(pb[:, f, (t % 2) * D:(t % 2 + 1) * D], xq[:, k, t * P:(t + 1) * P],
                                                 w[:, k, :], start=(i == 0), stop=(i == 2 * PIECE - 1))
                                i += 1
                    ev.done(last, "ff")

                def project(m):
                    ev.wait(pe, "norm", m, 4)
                    ev.wait(pe, "tr1c", m, 0)
                    turn_tokens(y, "ytr")
                    ev.wait(pe, "ytc", m, 2)
                    for f in range(2):
                        for t in (2 * f, 2 * f + 1):
                            for k in range(DC):
                                last = pe.matmul(sc[:, f, (t % 2) * D:(t % 2 + 1) * D], yT[:, k, t * P:(t + 1) * P],
                                                 wout0[:, k, :], start=(k == 0), stop=(k == DC - 1))
                        ev.done(last, "so")

                def turn_second(n):
                    ev.wait(pe, "xn1", n, 1)
                    turn_tokens(xn1, "tr1")

                def project1(n, j):
                    if j == 0:
                        ev.wait(pe, "tr1c", n, 2)
                    if j >= 2:
                        ev.wait(pe, "pjc", n, j - 1)
                    for k in range(DC):
                        last = pe.matmul(pb[:, j % 2, :], wqk1[:, k, j * P:(j + 1) * P], x1T[:, k, :],
                                         start=(k == 0), stop=(k == DC - 1))
                    ev.done(last, "pj")

                def values1(n, t):
                    if t < 2:
                        ev.wait(pe, "pjc", n, t + 3)
                    else:
                        ev.wait(pe, "vjc", n, t - 1)
                        ev.wait(pe, "lc", n, t - 1)
                    for k in range(DC):
                        last = pe.matmul(pb[:, t % 2, 0:D + E], x1T[:, k, t * P:(t + 1) * P], wvg1[:, k, :],
                                         start=(k == 0), stop=(k == DC - 1))
                    ev.done(last, "vj")

                def turn_both(m, n):
                    turn_first(m)
                    keys(m)
                    queries(m)
                    for p in range(NP0):
                        scores(m, p)
                        if n is not None:
                            if p == 1:
                                turn_second(n)
                            if 1 <= p < 5:
                                project1(n, p - 1)
                            for t in VALUES_AT.get(p, ()):
                                values1(n, t)
                        if p >= 1:
                            values(m, p - 1)
                        if p >= 3 and p % 2 == 1:
                            turn(m, (p - 3) // 2)
                    values(m, NP0 - 1)
                    gate(m, 0)
                    turn(m, 3)
                    gate(m, 1)
                    project(m)

                def both(b, c):
                    turn_both(b * SPB + c + 1, b * SPB + c)

                def second():
                    n = NSEG - 1
                    turn_second(n)
                    ev.wait(pe, "ffc", n, 2)
                    for j in range(4):
                        project1(n, j)
                    for t in range(TT):
                        values1(n, t)

                turns(pe, lambda: turn_both(0, None), both, second)

            @block.scalar
            def _(act):
                act.wait_ge(consts, 16 * NCONST)
                act.wait_ge(ready, 1)

                def copy_turned(dst, name):
                    for k in range(DC):
                        ev.done(act.activation(dst[:, k, :], tb[:, k, :], ACT.Copy), name)

                def out_copy(m, g):
                    ev.wait(act, "pv", m, 2 * g + 2)
                    ev.wait(act, "ot", m, max(g - 1, 0))
                    ev.done(act.activation(oT[:, g % 2, :], ob[:], ACT.Copy), "oc")

                def second_turned(n):
                    ev.wait(act, "tr1", n, 1)
                    ev.wait(act, "vj", n, 0)
                    copy_turned(x1T, "tr1c")

                def projected(n, j):
                    ev.wait(act, "pj", n, j + 1)
                    if j == 0:
                        ev.wait(act, "p3", n, 0)
                    ev.done(act.activation(qk[:, j // 2, j % 2, :], pb[:, j % 2, :], ACT.Identity,
                                           bias=bqk1[:, j:j + 1]), "pjc")

                def part0(n):
                    ev.wait(act, "rot", n, 1)
                    ev.wait(act, "rot1", n, 1)
                    ev.wait(act, "qk_out", n, 0)
                    ev.done(act.activation(piece[0][:], rot[:], ACT.Copy), "p1")

                def part1(n):
                    ev.wait(act, "rest", n, 1)
                    ev.done(act.activation(piece[1][:], qk[:], ACT.Copy), "p2")

                def logits(n, t):
                    ev.wait(act, "vj", n, t + 1)
                    if t == 0:
                        ev.wait(act, "l_out", n, 0)
                    ev.wait(act, "vjc", n, t + 1)
                    ev.done(act.activation(logit[:, t, :], pb[:, t % 2, D:D + E], ACT.Copy), "lc")

                def turn_both(m, n):
                    ev.wait(act, "tr", m, 1)
                    ev.wait(act, "kv", m, 0)
                    ev.wait(act, "quant", m, 0)
                    copy_turned(xnT, "trc")
                    ev.wait(act, "clip", m, 1)
                    ev.done(act.activation(square[:], clipped[:], ACT.Square), "wide")
                    ev.wait(act, "q", m, 1)
                    ev.done(act.activation(qT[:].rearrange("p k t -> p (k t)"), pb[:].rearrange("p k t -> p (k t)"),
                                           ACT.Copy), "qc")
                    ev.wait(act, "round", m, 1)
                    act.sem_inc(passed, 1)
                    ev.done(act.activation(xq[:], coarse[:], ACT.Copy), "wide")
                    ev.wait(act, "round", m, 2)
                    act.sem_inc(passed, 1)
                    ev.done(act.activation(doubled[:], half8[:], ACT.Copy, scale=2.0), "wide")
                    for p in range(NP0):
                        ev.wait(act, "shift", m, p + 1)
                        ev.wait(act, "pv", m, max(p - 1, 0))
                        ev.done(act.activation(wexp[:, p % 2, :], shifted[:, p % 2, :], ACT.Exp, scale=SCALE), "wexp")
                        if n is not None:
                            if p == 1:
                                second_turned(n)
                            if 1 <= p < 5:
                                projected(n, p - 1)
                            for t in VALUES_AT.get(p, ()):
                                logits(n, t)
                        if p >= 2 and p % 2 == 0:
                            out_copy(m, p // 2 - 1)
                    out_copy(m, 3)
                    if n is not None:
                        part0(n)

                    def half_tanh(f):
                        if f == 0:
                            ev.wait(act, "x1", m, 0)
                        ev.wait(act, "ffc", m, f + 1)
                        ev.done(act.activation(ez[:, 2 * f:2 * f + 2], z[:, 2 * f:2 * f + 2], ACT.Tanh, scale=0.5), "ez")

                    half_tanh(0)
                    ev.wait(act, "ytr", m, 1)
                    ev.wait(act, "so", m, 0)
                    copy_turned(yT, "ytc")
                    half_tanh(1)
                    if n is not None:
                        part1(n)

                def second():
                    n = NSEG - 1
                    second_turned(n)
                    for j in range(4):
                        projected(n, j)
                    for t in range(TT):
                        logits(n, t)
                    part0(n)
                    part1(n)

                turns(act, lambda: turn_both(0, None), lambda b, c: turn_both(b * SPB + c + 1, b * SPB + c), second)

            @block.vector
            def _(dve):
                ev.start(dve)
                setup = Steps(dve, setup_step, 0)
                dve.wait_ge(consts, 16 * NCONST)
                setup.then(dve.tensor_scalar(wf[:], wf[:], w_scale[:, 0:1], None, ALU.mult))
                setup.settle()
                setup.then(dve.tensor_copy(wf_piece[0][:], wf[:]))
                setup.settle()
                setup.then(dve.tensor_tensor(wf_rest[:], wf[:], wf_piece[0][:], ALU.subtract))
                setup.settle()
                setup.then(dve.tensor_copy(wf_piece[1][:], wf_rest[:]))
                setup.settle()
                setup.then(dve.tensor_tensor(wf_piece[2][:], wf_rest[:], wf_piece[1][:], ALU.subtract))
                setup.then(dve.reciprocal(in_inv[:], in_scale[:]))
                setup.then(dve.memset(vbd[:], 0.0))
                setup.then(dve.memset(v32[:], 1.0))
                setup.settle()
                setup.then(dve.memset(vbd[0:KN, :, HD:HD + 1], 1.0))
                setup.then(dve.memset(vbd[KN:P, :, HW + HD:HW + HD + 1], 1.0))
                setup.settle()
                dve.sem_inc(ready, 1)

                def find_norm(st, src, i, n, var):
                    for t in range(TT):
                        st.then(dve.bn_stats(stats[:, i, t, :], src[:, t, :]))
                    st.settle(passed)
                    for t in range(TT):
                        st.then(dve.bn_aggr(mv[:, i, t, :], stats[:, i, t, :]))
                    st.settle()
                    st.then(dve.tensor_scalar(veps[:, i], mv[:, i, :, 1], LN_EPS, None, ALU.add))
                    st.settle()
                    st.then(dve.tensor_scalar(seed[:, i], veps[:, i].bitcast(I32), 1, None, ALU.arith_shift_right))
                    st.settle()
                    st.mark(dve.tensor_scalar(seed[:, i], seed[:, i], -1.0, float(RSQRT_MAGIC), ALU.mult, ALU.add),
                            var, n)

                def norm_tokens(st, src, dst, i, n, rs, done):
                    ev.wait(dve, rs, n, 1)
                    for t in range(TT):
                        last = dve.tensor_scalar(dst[:, t, :], src[:, t, :], mv[:, i, t, 0:1],
                                                 rstd[:, i, t:t + 1], ALU.subtract, ALU.mult)
                        if t == TT - 1:
                            st.mark(last, done, n)
                        else:
                            st.then(last)

                def quantise(st, m):
                    ev.wait(dve, "trc", m, 2)
                    ev.wait(dve, "ff", m, 0)
                    st.then(dve.tensor_scalar(clipped[:], xnT[:], in_inv[:, 0:1], FP8_MAX, ALU.mult, ALU.min))
                    st.settle()
                    st.mark(dve.tensor_scalar(clipped[:], clipped[:], -FP8_MAX, None, ALU.max), "clip", m)
                    st.settle(passed)
                    st.mark(dve.tensor_scalar(coarse[:], clipped[:], 240.0, -240.0, ALU.min, ALU.max,
                                              saturate=False), "round", m)
                    st.mark(dve.tensor_scalar(half8[:], clipped[:], 0.5, None, ALU.mult, saturate=False), "round", m)

                def quantise_rest(st, m):
                    ev.wait(dve, "wide", m, 3)
                    st.then(dve.tensor_scalar(is_big[:], square[:], 2.0 ** -10, None, ALU.is_ge))
                    st.settle(passed)
                    st.mark(dve.copy_predicated(xq[:], is_big[:], doubled[:]), "quant", m)

                def block_diagonal(st, m):
                    ev.wait(dve, "kv", m, 1)
                    ev.wait(dve, "pv", m, 0)
                    for f in range(DC):
                        st.then(dve.tensor_tensor(
                            kbd[:, f], kv[:, f * KN:(f + 1) * KN].unsqueeze(1).to_broadcast([P, H // DC, KN]),
                            headmask[:].unsqueeze(2).to_broadcast([P, H // DC, KN]), ALU.mult))
                    heads = kv[:, D:2 * D].rearrange("p (a two d) -> p a two d", two=2, d=HD)
                    st.then(dve.tensor_copy(vbd[0:KN, :, 0:HD], heads[0:KN, :, 0, :]))
                    st.mark(dve.tensor_copy(vbd[KN:P, :, HW:HW + HD], heads[KN:P, :, 1, :]), "kvc", m)

                def shift(st, m, p):
                    ev.wait(dve, "s", m, p + 1)
                    ev.wait(dve, "wexp", m, max(p - 1, 0))
                    blocks = sc[:, p % 2, :].rearrange("p (n q) -> p n q", q=BLK)
                    st.then(dve.tensor_reduce(keymax[:, p % 2, :], blocks, AX, ALU.max))
                    st.settle()
                    st.mark(dve.tensor_tensor(
                        shifted[:, p % 2, :].rearrange("p (n q) -> p n q", q=BLK), blocks,
                        keymax[:, p % 2, :].unsqueeze(2).to_broadcast([P, NBLK, BLK]), ALU.subtract), "shift", m)

                def normalise(st, m, g):
                    ev.wait(dve, "ot", m, g + 1)
                    turned = kv[:].rearrange("p (t h w) -> p t h w", t=TT, w=HW)
                    st.then(dve.tensor_scalar(den[:], turned[:, :, :, HD], DEN_EPS, None, ALU.add))
                    st.settle()
                    st.then(dve.reciprocal(rden[:], den[:]))
                    st.settle()
                    if g == 0:
                        ev.wait(dve, "ytr", m, 0)
                    out = y[:, :, g * G * HD:(g + 1) * G * HD].rearrange("p t (h d) -> p t h d", d=HD)
                    st.mark(dve.tensor_tensor(
                        out, turned[:, :, :, 0:HD], rden[:].unsqueeze(3).to_broadcast([P, TT, G, HD]), ALU.mult),
                        "norm", m)

                def residual(st, c, m, n, ahead):
                    for f in range(2):
                        ev.wait(dve, "ff", m, f + 1)
                        if f == 0:
                            ev.wait(dve, "ez", m, 0)
                        st.mark(dve.scalar_tensor_tensor(
                            out=z[:, 2 * f:2 * f + 2], in0=pb[:, f, :].rearrange("p (t d) -> p t d", d=D),
                            scalar=in_scale[:, 0:1], in1=fbias[:].unsqueeze(1).to_broadcast([P, 2, D]),
                            op0=ALU.mult, op1=ALU.add), "ffc", m)
                        if f == 0:
                            normalise(st, m, 3)
                    if ahead:
                        normed_tokens(st, m + 1, *ahead, 1)
                    if n is not None:
                        rest(st, n)
                    ev.wait(dve, "ez", m, 2)
                    st.mark(dve.scalar_tensor_tensor(out=z[:], in0=ez[:], scalar=1.0, in1=z[:],
                                                     op0=ALU.add, op1=ALU.mult), "gate", m)
                    st.settle()
                    for f in range(2):
                        ev.wait(dve, "so", m, f + 1)
                        st.mark(dve.scalar_tensor_tensor(
                            out=ez[:, 2 * f:2 * f + 2], in0=sc[:, f, :].rearrange("p (t d) -> p t d", d=D),
                            scalar=0.5, in1=z[:, 2 * f:2 * f + 2], op0=ALU.mult, op1=ALU.mult), "sog", m)
                    st.settle()
                    ev.wait(dve, "x1_out", m, 0)
                    st.mark(dve.tensor_tensor(x1[:], x[:, c % 2], ez[:], ALU.add), "x1", m)

                def rotate(st, n, c):
                    cos, sin = rotary(c)
                    ev.wait(dve, "pjc", n, 4)
                    ev.wait(dve, "p1", n, 0)
                    st.then(dve.tensor_tensor(rot[:, :, 0, :], qk[:, :, 0, :], cos, ALU.mult))
                    st.then(dve.tensor_tensor(prod[:], qk[:, :, 1, :], sin, ALU.mult))
                    st.settle()
                    st.mark(dve.tensor_tensor(rot[:, :, 0, :], rot[:, :, 0, :], prod[:], ALU.subtract), "rot", n)

                def rest(st, n):
                    ev.wait(dve, "p1", n, 1)
                    st.mark(dve.tensor_tensor(qk[:], rot[:], piece[0][:], ALU.subtract), "rest", n)

                def values1(st, n, t):
                    ev.wait(dve, "vj", n, t + 1)
                    if t == 0:
                        ev.wait(dve, "v_out", n, 0)
                    st.mark(dve.tensor_tensor(
                        v32[:, t, :, 0:HD], pb[:, t % 2, 0:D].rearrange("p (h d) -> p h d", d=HD),
                        bv1[:].rearrange("p (h d) -> p h d", d=HD), ALU.add), "vjc", n)

                def normed_tokens(st, m, c, use, part):
                    if part == 0:
                        ev.wait(dve, f"x_in{c % 2}", use, 1)
                        ev.wait(dve, "rstd", m, 0)
                        find_norm(st, x[:, c % 2], 0, m, "var")
                    else:
                        ev.wait(dve, "tr", m, 0)
                        norm_tokens(st, x[:, c % 2], xn, 0, m, "rstd", "xn")

                def turn_both(st, m, c1, n, c, ahead):
                    if n is not None:
                        st.settle()
                        ev.wait(dve, "rstd1", n, 0)
                        find_norm(st, x1, 1, n, "var1")
                    quantise(st, m)
                    block_diagonal(st, m)
                    if n is not None:
                        ev.wait(dve, "xn1_out", n, 0)
                        norm_tokens(st, x1, xn1, 1, n, "rstd1", "xn1")
                    for p in range(NP0):
                        shift(st, m, p)
                        if p == 1:
                            quantise_rest(st, m)
                        if n is not None:
                            if p == 5:
                                rotate(st, n, c)
                            for t in VALUES_AT.get(p, ()):
                                values1(st, n, t)
                        if p >= 3 and p % 2 == 1:
                            normalise(st, m, (p - 3) // 2)
                        if ahead and p == NORM_AT:
                            normed_tokens(st, m + 1, *ahead, 0)
                    residual(st, c1, m, n, ahead)

                def first():
                    st = Steps(dve, dve_step, 0, ev)
                    for part in range(2):
                        normed_tokens(st, 0, 0, 0, part)
                    turn_both(st, 0, 0, None, None, (1, 0))
                    assert st.n == FIRST_STEPS, ("first", st.n)

                def both(b, c):
                    n = b * SPB + c
                    st = Steps(dve, dve_step, FIRST_STEPS + n * TURN_STEPS, ev)
                    st.last = ev.sem["x1"], ev.at("x1", n, 1)
                    b1, c1 = place(b, c)
                    b2, c2 = place(b1, c1)
                    more = not last_turn(b, c)
                    turn_both(st, n + 1, c1, n, c, (c2, b2 * (SPB // 2) + c2 // 2) if more else None)
                    assert st.n == TURN_STEPS - (0 if more else NORM_STEPS), ("turn", st.n)

                def second():
                    n = NSEG - 1
                    st = Steps(dve, dve_step, FIRST_STEPS + n * TURN_STEPS - NORM_STEPS, ev)
                    st.last = ev.sem["x1"], ev.at("x1", n, 1)
                    st.settle()
                    find_norm(st, x1, 1, n, "var1")
                    ev.wait(dve, "xn1_out", n, 0)
                    norm_tokens(st, x1, xn1, 1, n, "rstd1", "xn1")
                    rotate(st, n, SPB - 1)
                    for t in range(TT):
                        values1(st, n, t)
                    rest(st, n)

                turns(dve, first, both, second)


class Route:

    def __init__(self, nc, ctx, io, dram, keep, inside, totals):
        def sb(name, shape, dt=F32):
            return ctx.enter_context(nc.sbuf_tensor("r_" + name, shape, dt))

        def sem(name):
            return ctx.enter_context(nc.semaphore("r_" + name))

        KT = TOPK * NT
        before = sb("before", [P, P], BF16)
        ones = sb("ones", [P, P], BF16)
        onesf = sb("onesf", [P, KT])
        expert = sb("expert", [P, E])
        spill = sb("spill", [P, TOPK, NT])
        zero = sb("zero", [P, P], I32)
        logit = sb("logit", [P, NT, E])
        score = sb("score", [P, NT, E])
        rest = sb("rest", [P, NT, E])
        best = sb("best", [P, TOPK, NT])
        total = sb("total", [P, NT])
        below = sb("below", [P, NT, E])
        which = sb("which", [P, TOPK, NT])
        hot = sb("hot", [P, TOPK, NT, E])
        hotb = sb("hotb", [P, TOPK * NT * E], BF16)
        count = sb("count", [P, E, KT])
        running = sb("running", [P, E, KT])
        place = sb("place", [P, KT, E])
        loc = sb("loc", [P, KT])
        valid = sb("valid", [P, KT])
        slotf = sb("slotf", [P, KT])
        destf = sb("destf", [P, KT])
        loads, zeroed, shifted, weights, hots, prefix, step = map(
            sem, ("loads", "zeroed", "shifted", "weights", "hots", "prefix", "step"))
        table_zero = sem("table_zero")

        placed = sem("placed")

        def load(sp):
            for out, in_ in ((before[:], io["c_before"]), (ones[:], io["c_ones"][:, 0:P]),
                             (expert[:], io["c_expert"]), (spill[:], io["c_spill"]),
                             (keep["token"][:], io["c_token"]),
                             (logit[:], dram["logits"])):
                sp.dma_start(out, in_).then_inc(loads, 16)

        def zero_table(sp):
            sp.wait_ge(zeroed, 1)
            sp.dma_start(dram["table"][0:NSLOT, :].rearrange("(p f) o -> p (f o)", p=P), zero[:]).then_inc(table_zero, 16)

        def wait_placed(pool):
            pool.wait_ge(table_zero, 16)
            pool.wait_ge(placed, 1)

        def prefix_sums(pe):
            pe.wait_ge(hots, 1)
            for out, w in ((inside, before), (totals, ones)):
                for f in range(2):
                    cols = slice(f * 512, (f + 1) * 512)
                    last = pe.matmul(out[:, cols], w[:], hotb[:, cols], start=True, stop=True)
            last.then_inc(prefix, 1)

        def weigh(act):
            act.wait_ge(shifted, 1)
            act.activation(score[:], logit[:], ACT.Exp).then_inc(weights, 1)

        flat = lambda a: a[:].rearrange("p k t -> p (k t)")
        gate = keep["gate"]
        steps = [0]

        def choose(dve):
            def then(ins):
                steps[0] += 1
                ins.then_inc(step, 1)
                dve.wait_ge(step, steps[0])

            wide = lambda a: a.unsqueeze(2).to_broadcast([P, NT, E])
            ids = expert[:].unsqueeze(1).to_broadcast([P, NT, E])
            dve.memset(zero[:], 0).then_inc(zeroed, 1)
            then(dve.memset(onesf[:], 1.0))
            dve.wait_ge(loads, 96)
            then(dve.tensor_reduce(total[:], logit[:], AX, ALU.max))
            dve.tensor_tensor(logit[:], logit[:], wide(total[:]), ALU.subtract).then_inc(shifted, 1)
            dve.wait_ge(weights, 1)
            then(dve.tensor_reduce(total[:], score[:], AX, ALU.add))
            then(dve.reciprocal(total[:], total[:]))
            then(dve.tensor_tensor(score[:], score[:], wide(total[:]), ALU.mult))
            for k in range(TOPK):
                s = score if k == 0 else rest
                then(dve.tensor_reduce(best[:, k], s[:], AX, ALU.max))
                then(dve.tensor_tensor(below[:], s[:], wide(best[:, k]), ALU.is_lt))
                then(dve.scalar_tensor_tensor(out=below[:], in0=below[:], scalar=float(2 * E), in1=ids,
                                              op0=ALU.mult, op1=ALU.add))
                then(dve.tensor_reduce(which[:, k], below[:], AX, ALU.min))
                then(dve.tensor_tensor(hot[:, k], ids, wide(which[:, k]), ALU.is_equal))
                if k == 0:
                    then(dve.scalar_tensor_tensor(out=rest[:], in0=hot[:, k], scalar=-2.0, in1=score[:],
                                                  op0=ALU.mult, op1=ALU.add))
            dve.tensor_copy(hotb[:], hot[:].rearrange("p k t e -> p (k t e)")).then_inc(hots, 1)
            then(dve.tensor_tensor(total[:], best[:, 0], best[:, 1], ALU.add))
            then(dve.reciprocal(total[:], total[:]))
            for k in range(TOPK):
                then(dve.tensor_tensor(gate[:, k], best[:, k], total[:], ALU.mult))

        def find_places(dve):
            def then(ins):
                steps[0] += 1
                ins.then_inc(step, 1)
                dve.wait_ge(step, steps[0])

            dve.wait_ge(prefix, 1)
            by_expert = totals[:].rearrange("p (n e) -> p e n", e=E)
            then(dve.tensor_copy(count[:], by_expert))
            for e in range(E):
                then(dve.tensor_tensor_scan(running[:, e], onesf[:], count[:, e], 0.0, ALU.mult, ALU.add))
            then(dve.tensor_tensor(running[:], running[:], count[:], ALU.subtract))
            then(dve.tensor_tensor(place[:], inside[:].rearrange("p (n e) -> p n e", e=E),
                                   running[:].rearrange("p e n -> p n e"), ALU.add))
            then(dve.tensor_tensor(place[:], place[:], hot[:].rearrange("p k t e -> p (k t) e"), ALU.mult))
            then(dve.tensor_reduce(loc[:], place[:], AX, ALU.add))
            then(dve.tensor_scalar(valid[:], loc[:], float(CAP), None, ALU.is_lt))
            then(dve.tensor_scalar(loc[:], loc[:], float(CAP - 1), None, ALU.min))
            then(dve.scalar_tensor_tensor(out=slotf[:], in0=flat(which), scalar=float(CAP), in1=loc[:],
                                          op0=ALU.mult, op1=ALU.add))
            then(dve.tensor_copy(flat(keep["slot"]), slotf[:]))
            then(dve.tensor_tensor(flat(gate), flat(gate), valid[:], ALU.mult))
            then(dve.tensor_tensor(destf[:], slotf[:], flat(spill), ALU.subtract))
            then(dve.tensor_tensor(destf[:], destf[:], valid[:], ALU.mult))
            then(dve.tensor_tensor(destf[:], destf[:], flat(spill), ALU.add))
            dve.tensor_copy(flat(keep["dest"]), destf[:]).then_inc(placed, 1)

        self.load, self.zero_table, self.wait_placed, self.prefix_sums, self.weigh = (
            load, zero_table, wait_placed, prefix_sums, weigh)
        self.choose, self.find_places = choose, find_places

def attend_phase(nc, io, dram, keep):
    with ExitStack() as ctx:
        def sb(name, shape, dt=F32):
            return ctx.enter_context(nc.sbuf_tensor("at_" + name, shape, dt))

        def ps(name, shape, dt=F32):
            return ctx.enter_context(nc.psum_tensor("at_" + name, shape, dt))

        NBUF, NE = 3, 2 * G
        ident = sb("ident", [P, P])
        identb = sb("identb", [P, P], BF16)
        mask_q = sb("mask_q", [P, P], BF16)
        mask_k = sb("mask_k", [P, P], BF16)
        qs = sb("qs", [ROWS, NBUF, G, M], BF16)
        ks = sb("ks", [ROWS, NBUF, G, M], BF16)
        vs = sb("vs", [P, NBUF, NQT, G * HW])
        ex = sb("ex", [P, NE, 2 * SEG])
        part = sb("part", [P, G * NQT, SPB])
        negmax = sb("negmax", [P, G * NQT])
        restT = sb("restT", [G * NQT, P])
        mT = sb("mT", [G * NQT, PIECE, P], BF16)
        osb = sb("osb", [P, SEG])
        rden = sb("rden", [P, TT, G])
        yout = sb("yout", [P, 2, TT, G * HD])
        idx = sb("idx", [P, 2], I32)
        tok = sb("tok", [P, 2], I32)
        NP1 = 3
        p1 = ps("p1", [P, NP1, SEG])
        st = ps("st", [P, 2, 2 * SEG])
        ob = ps("ob", [P, SEG])
        turned_max = p1[0:G * NQT, 0, 0:P]

        route = Route(nc, ctx, io, dram, keep, st[:, 0, :], st[:, 1, :])

        steps = []
        for qc in range(SPB):
            first = TT * qc
            for j in range(0, first, 2):
                steps.append((qc, [(j, 0, SEG), (j + 1, SEG, SEG)]))
            steps.append((qc, [(first, 0, SEG), (first + 1, SEG, SEG - P), (first + 3, 2 * SEG - P, P)]))
            steps.append((qc, [(first + 2, 0, SEG - 2 * P)]))
        NS = len(steps)
        NU = NS * G
        last_of = [max(s for s in range(NS) if steps[s][0] == qc) for qc in range(SPB)]
        chunks = [(h, qt, ch) for h in range(G) for qt in range(NQT) for ch in range(qt // TT + 1)]
        NC = len(chunks)
        TURN_AT = NU - 6
        FIXED = P // 2
        step_work = np.cumsum([0] + [sum(w for _, _, w in steps[u // G][1]) + 2 * FIXED for u in range(TURN_AT)])
        chunk_work = np.cumsum([min(SEG, (qt + 1) * P - ch * SEG) + FIXED for _, qt, ch in chunks])
        due_at = [min(u for u in range(TURN_AT) if step_work[u + 1] * chunk_work[-1] >= c * step_work[-1])
                  for c in chunk_work]

        def due(u):
            return [n for n in range(NC) if due_at[n] == u]

        counts = dict(s1=NC, mx=NC, neg=1, negT=1, mT=1, m_in=PIECE, st=NU, ex=NU, pv=NS, oc=SPB, ot=SPB,
                      norm=SPB, y_out0=SPB // 2, y_out1=SPB // 2, rden=SPB)
        for i in range(NBUF):
            counts[f"in{i}"] = 1
        NLOAD = 2 * 12 + 2
        ev = Events(nc, ctx, "at", counts, {"m_in", "y_out0", "y_out1"})
        for i in range(NBUF):
            ev.unit[f"in{i}"] = 16 * NLOAD
        consts = ctx.enter_context(nc.semaphore("at_consts"))
        ready = ctx.enter_context(nc.semaphore("at_ready"))
        passed = ctx.enter_context(nc.semaphore("at_passed"))
        setup = ctx.enter_context(nc.semaphore("at_setup"))
        mstep = ctx.enter_context(nc.semaphore("at_mstep"))
        scat_copy = ctx.enter_context(nc.semaphore("at_scat_copy"))
        scattered = ctx.enter_context(nc.semaphore("at_scattered"))

        def group_loop(e, body):
            with e.Fori(0, (NGROUPS - 1) // NBUF) as i:
                for r in range(NBUF):
                    body(i * NBUF + r, r, i, True)
            body(NGROUPS - 1, (NGROUPS - 1) % NBUF, (NGROUPS - 1) // NBUF, False)

        def turn_of(g_const, i, r):
            return i + r // NBUF

        with nc.Block() as block:
            @block.sync
            def _(sp):
                route.load(sp)
                for out, in_ in ((ident[:], io["c_ident"]), (identb[:], io["c_identb"]),
                                 (mask_q[:], io["c_mask_q"]), (mask_k[:], io["c_mask_k"])):
                    sp.dma_start(out, in_).then_inc(consts, 16)
                for rows in (qs, ks):
                    for i in range(NBUF):
                        sp.dma_start(rows[STACK:ROWS, i], io["c_ones"][0:PIECE, :].unsqueeze(1).to_broadcast([PIECE, G, M])).then_inc(consts, 16)
                sp.wait_ge(ready, 1)

                def load(g, r):
                    for m, rows, pieces in ((0, qs, Q_PIECES), (1, ks, K_PIECES)):
                        for s, i in enumerate(pieces):
                            for f in range(2):
                                at = s * HD + f * (HD // 2)
                                src = dram["qk"][m, g, i, f, :, :].rearrange("o (h j) t -> j (o h) t", j=HD // 2)
                                sp.dma_start(rows[at:at + HD // 2, r], src).then_inc(ev.sem[f"in{r}"], 16)
                    for f in range(2):
                        src = dram["v"][g, f * (M // 2):(f + 1) * (M // 2), :].rearrange("o (t p) w -> p (o t) w", p=P)
                        sp.dma_start(vs[:, r, f * (NQT // 2):(f + 1) * (NQT // 2)], src).then_inc(ev.sem[f"in{r}"], 16)

                def maxima(g, r):
                    ev.wait(sp, "mT", g, 1)
                    for i in range(PIECE):
                        dst = qs[STACK + i:STACK + i + 1, r].rearrange("o h (t p) -> o (h t) p", p=P)
                        ev.done(sp.dma_start(dst, mT[:, i, :]), "m_in")

                def group(g, r, more):
                    for qc in range(SPB):
                        if more and qc == SPB - 1:
                            maxima(g + 1, (r + 1) % NBUF)
                        ev.wait(sp, "norm", g, qc + 1)
                        dst = dram["y"][bass.ds(g, 1), qc * SEG:(qc + 1) * SEG, :]
                        ev.done(sp.dma_start(dst.rearrange("o (t p) d -> p (o t) d", p=P), yout[:, qc % 2]), f"y_out{qc % 2}")

                load(slice(0, 1), 0)
                load(slice(1, 2), 1)
                route.zero_table(sp)
                maxima(0, 0)

                def turn(i, loads):
                    for r in range(NBUF):
                        g = i * NBUF + r
                        if r < loads:
                            ev.wait(sp, "pv", g, 0)
                            sp.sem_inc(passed, 1)
                            load(bass.ds(g + 2, 1), (r + 2) % NBUF)
                        group(g, r, True)

                NTURN = (NGROUPS - 1) // NBUF
                with sp.Fori(0, NTURN - 1) as i:
                    turn(i, NBUF)
                turn(NTURN - 1, NBUF - 1)
                group(NGROUPS - 1, 0, False)
                for k in range(2):
                    sp.wait_ge(ev.sem[f"y_out{k}"], 16 * (NGROUPS * SPB // 2 + 1))

            @block.gpsimd
            def _(pool):
                pool.wait_ge(ready, 1)
                route.wait_placed(pool)
                def scatter(i):
                    pool.tensor_copy(idx[:], keep["dest"][:, :, bass.ds(i, 1)].rearrange("p k o -> p (k o)")).then_inc(scat_copy, 1)
                    pool.tensor_copy(tok[:, 0:1], keep["token"][:, bass.ds(i, 1)]).then_inc(scat_copy, 1)
                    pool.wait_ge(scat_copy, 2 * i + 2)
                    pool.sem_inc(passed, 1)
                    for k in range(TOPK):
                        pool.indirect_dma_start(
                            out=dram["table"], out_offset=bass.IndirectOffsetOnAxis(ap=idx[:, k:k + 1], axis=0),
                            in_=tok[:, 0:1], in_offset=None).then_inc(scattered, 16)

                scatter(0)
                with pool.Fori(1, NT) as i:
                    pool.wait_ge(scattered, 16 * TOPK * i)
                    pool.sem_inc(passed, 1)
                    scatter(i)
                pool.wait_ge(scattered, 16 * TOPK * NT)

            @block.tensor
            def _(pe):
                pe.wait_ge(consts, 16 * (4 + 2 * NBUF))
                pe.wait_ge(ready, 1)

                def row_scores(g, r, n):
                    h, qt, ch = chunks[n]
                    w = min(SEG, (qt + 1) * P - ch * SEG)
                    diag = ch == qt // TT
                    ev.wait(pe, "mx", g, max(n - NP1 + 1, 0))
                    if n == 0:
                        ev.wait(pe, "mT", g, 0)
                    out = p1[:, n % NP1, 0:w]
                    last = pe.matmul(out, qs[0:STACK, r, h, qt * P:(qt + 1) * P], ks[0:STACK, r, h, ch * SEG:ch * SEG + w],
                                     start=True, stop=not diag)
                    if diag:
                        last = pe.matmul(out[:, w - P:w], identb[:], mask_q[:], start=False, stop=True)
                    ev.done(last, "s1")

                def turn_maxima(g):
                    ev.wait(pe, "neg", g, 1)
                    pe.sem_inc(passed, 1)
                    ev.done(pe.transpose(turned_max, negmax[:], ident[:]), "negT")

                def key_scores(g, r, u):
                    s, h = u // G, u % G
                    qc, tiles = steps[s]
                    ev.wait(pe, "ex", g, max(u - 1, 0))
                    for kt, at, w in tiles:
                        diag = kt >= TT * qc
                        out = st[:, u % 2, at:at + w]
                        q0 = (qc + 1) * SEG - w
                        last = pe.matmul(out, ks[:, r, h, kt * P:(kt + 1) * P], qs[:, r, h, q0:q0 + w],
                                         start=True, stop=not diag)
                        if diag:
                            last = pe.matmul(out[:, 0:P], identb[:], mask_k[:], start=False, stop=True)
                    ev.done(last, "st")

                def values(g, r, s, half):
                    qc, tiles = steps[s]
                    if half == 0:
                        ev.wait(pe, "ex", g, G * s + G)
                        if s == 0 or steps[s - 1][0] != qc:
                            ev.wait(pe, "norm", g, qc)
                    cut = (len(tiles) + 1) // 2
                    for kt, at, w in tiles[:cut] if half == 0 else tiles[cut:]:
                        for h in range(G):
                            last = pe.matmul(ob[h * HW:(h + 1) * HW, SEG - w:SEG], vs[:, r, kt, h * HW:(h + 1) * HW],
                                             ex[:, (G * s + h) % NE, at:at + w], start=(kt == 0),
                                             stop=(s == last_of[qc] and kt == tiles[-1][0]),
                                             skip_group_check=True)
                    if half == (len(tiles) > 1):
                        ev.done(last, "pv")

                def turn(g, qc):
                    ev.wait(pe, "oc", g, qc + 1)
                    for t in range(TT):
                        last = pe.transpose(ob[:, t * P:(t + 1) * P], osb[:, t * P:(t + 1) * P], ident[:])
                    ev.done(last, "ot")

                def group(g, r, i, more):
                    ev.wait(pe, "m_in", g, PIECE)
                    if more:
                        ev.wait(pe, f"in{(r + 1) % NBUF}", i + (r + 1) // NBUF, 1)
                    for u in range(NU):
                        s, h = u // G, u % G
                        now = list(due(u)) if more else []
                        for n in now[:1]:
                            row_scores(g + 1, (r + 1) % NBUF, n)
                        key_scores(g, r, u)
                        for n in now[1:]:
                            row_scores(g + 1, (r + 1) % NBUF, n)
                        if more and u == TURN_AT + 1:
                            turn_maxima(g + 1)
                        if h % 2 == 1 and s >= 1:
                            values(g, r, s - 1, h // 2)
                        if h == 3 and s >= 1 and s - 1 in last_of:
                            turn(g, last_of.index(s - 1))
                    for half in range(2):
                        values(g, r, NS - 1, half)
                    turn(g, SPB - 1)
                    
                route.prefix_sums(pe)
                ev.wait(pe, "in0", 0, 1)
                for n in range(NC):
                    row_scores(0, 0, n)
                turn_maxima(0)
                group_loop(pe, group)

            @block.scalar
            def _(act):
                act.wait_ge(ready, 1)
                route.weigh(act)

                def out_copy(g, qc):
                    ev.wait(act, "pv", g, last_of[qc] + 1)
                    ev.done(act.activation(osb[:], ob[:], ACT.Copy), "oc")

                def group(g, r, i, more):
                    for u in range(NU):
                        s, h = u // G, u % G
                        width = steps[s][1][-1][1] + steps[s][1][-1][2]
                        ev.wait(act, "st", g, u + 1)
                        if s >= 2:
                            ev.wait(act, "pv", g, s - 1)
                        elif h == 0 and s == 0:
                            ev.wait(act, "pv", g, 0)
                        ev.done(act.activation(ex[:, u % NE, 0:width], st[:, u % 2, 0:width], ACT.Exp, scale=SCALE), "ex")
                        if h == 2 and s >= 1 and s - 1 in last_of:
                            out_copy(g, last_of.index(s - 1))
                    out_copy(g, SPB - 1)

                group_loop(act, group)

            @block.vector
            def _(dve):
                ev.start(dve)
                dve.memset(part[:], LOWEST).then_inc(setup, 1)
                dve.wait_ge(setup, 1)
                dve.sem_inc(ready, 1)

                def chunk_max(g, n):
                    h, qt, ch = chunks[n]
                    w = min(SEG, (qt + 1) * P - ch * SEG)
                    ev.wait(dve, "s1", g, n + 1)
                    at = h * NQT + qt
                    ev.done(dve.tensor_reduce(part[:, at, ch:ch + 1], p1[:, n % NP1, 0:w], AX, ALU.max), "mx")

                def negate(g):
                    ev.wait(dve, "mx", g, NC)
                    dve.tensor_reduce(negmax[:], part[:], AX, ALU.max).then_inc(mstep, 1)
                    dve.wait_ge(mstep, 4 * g + 1)
                    ev.done(dve.tensor_scalar(negmax[:], negmax[:], -1.0, None, ALU.mult), "neg")

                def split(g):
                    ev.wait(dve, "negT", g, 1)
                    ev.wait(dve, "m_in", g, 0)
                    src = turned_max
                    dve.tensor_copy(mT[:, 0], src).then_inc(mstep, 1)
                    dve.wait_ge(mstep, 4 * g + 2)
                    dve.tensor_tensor(restT[:], src, mT[:, 0], ALU.subtract).then_inc(mstep, 1)
                    dve.wait_ge(mstep, 4 * g + 3)
                    dve.tensor_copy(mT[:, 1], restT[:]).then_inc(mstep, 1)
                    dve.wait_ge(mstep, 4 * g + 4)
                    ev.done(dve.tensor_tensor(mT[:, 2], restT[:], mT[:, 1], ALU.subtract), "mT")

                def normalise(g, qc):
                    ev.wait(dve, "ot", g, qc + 1)
                    turned = ob[:].rearrange("p (t h w) -> p t h w", t=TT, w=HW)
                    ev.wait(dve, f"y_out{qc % 2}", g, qc // 2)
                    ev.done(dve.reciprocal(rden[:], turned[:, :, :, HD]), "rden")
                    ev.wait(dve, "rden", g, qc + 1)
                    out = yout[:, qc % 2].rearrange("p t (h d) -> p t h d", d=HD)
                    ev.done(dve.tensor_tensor(out, turned[:, :, :, 0:HD], rden[:].unsqueeze(3).to_broadcast([P, TT, G, HD]),
                                              ALU.mult), "norm")

                def group(g, r, i, more):
                    for u in range(NU):
                        s, h = u // G, u % G
                        if more:
                            for n in due(u):
                                chunk_max(g + 1, n)
                            if u == TURN_AT - 1:
                                negate(g + 1)
                            if u == TURN_AT + 1:
                                split(g + 1)
                        if h == 3 and s >= 1 and s - 1 in last_of:
                            normalise(g, last_of.index(s - 1))
                    normalise(g, SPB - 1)

                route.choose(dve)
                for n in range(NC):
                    chunk_max(0, n)
                    if n == NP1:
                        route.find_places(dve)
                negate(0)
                split(0)
                group_loop(dve, group)




def experts_phase(nc, io, dram):
    with ExitStack() as ctx:
        def sb(name, shape, dt=F32):
            return ctx.enter_context(nc.sbuf_tensor("e_" + name, shape, dt))

        def ps(name, shape, dt=F32):
            return ctx.enter_context(nc.psum_tensor("e_" + name, shape, dt))

        HC = HID // P
        NCH = CAP // SEG
        NH = 4
        ident = sb("ident", [P, P])
        b1 = sb("b1", [P, E, HC])
        b2 = sb("b2", [P, E, D])
        w1 = sb("w1", [P, 2, DC, HID])
        w2 = sb("w2", [P, 2, HC, D])
        w1h = sb("w1h", [P, 2, DC, HID], F32R)
        w2h = sb("w2h", [P, 2, HC, D], F32R)
        w1l = sb("w1l", [P, 2, DC, HID], F32R)
        w2l = sb("w2l", [P, 2, HC, D], F32R)
        table = sb("table", [P, 2, CAP // P], I32)
        xg = sb("xg", [P, 2, TT, D])
        xh = sb("xh", [P, DC, SEG], F32R)
        xl = sb("xl", [P, DC, SEG], F32R)
        h = sb("h", [P, 2, SEG])
        hh = sb("hh", [P, 2, HC, SEG], F32R)
        hl = sb("hl", [P, 2, HC, SEG], F32R)
        og = sb("og", [P, 2, TT, D])
        b2now = sb("b2now", [P, 2, D])
        b1now = sb("b1now", [P, 2, HC])
        tb = ps("tb", [P, DC, SEG])
        hb = ps("hb", [P, NH, SEG])
        ob = ps("ob", [P, 2, SEG])

        TURN = 2 * NCH
        NTURN = E // 2
        counts = dict(tr=1, xh=DC, xl=DC, h=HC, hh=HC, hraw=HC, hl=HC, o=TT, oc=TT)
        ev = Events(nc, ctx, "e", counts, set())
        pev = Events(nc, ctx, "ew", dict(w0=2, w1=2, t0=1, t1=1, g0=TT, g1=TT, out0=1, out1=1),
                     {"w0", "w1", "t0", "t1", "g0", "g1", "out0", "out1"}, {"g0", "g1"})
        xev = Events(nc, ctx, "ex", dict(now=2, wh=2, wl=2), set())
        consts = ctx.enter_context(nc.semaphore("e_consts"))
        ready = ctx.enter_context(nc.semaphore("e_ready"))
        passed = ctx.enter_context(nc.semaphore("e_passed"))

        def turns(e, body):
            with e.Fori(0, NTURN - 1) as i:
                body(i, True)
            body(NTURN - 1, False)

        def at(i, u):
            return bass.ds(2 * i + u, 1)

        with nc.Block() as block:
            @block.sync
            def _(sp):
                for out, in_ in ((ident[:], io["c_ident"]), (b1[:], io["b1T"]), (b2[:], io["b2"].partition_broadcast(P))):
                    sp.dma_start(out, in_).then_inc(consts, 16)
                sp.wait_ge(ready, 1)

                def load(i, u):
                    pev.done(sp.dma_start(table[:, u], dram["table"][bass.ds((2 * i + u) * CAP, CAP), :].rearrange("(p c) o -> p (c o)", p=P)), f"t{u}")
                    pev.done(sp.dma_start(w1[:, u], io["w1"][at(i, u)].rearrange("o (k p) h -> p (o k) h", p=P)), f"w{u}")
                    pev.done(sp.dma_start(w2[:, u], io["w2"][at(i, u)].rearrange("o (k p) d -> p (o k) d", p=P)), f"w{u}")

                for u in range(2):
                    load(0, u)

                def turn(i, more):
                    for u in range(2):
                        for q in range(NCH):
                            n = i * TURN + u * NCH + q
                            ev.wait(sp, "oc", n, TT)
                            sp.sem_inc(passed, 1)
                            rows = dram["eo"][bass.ds((2 * i + u) * CAP, CAP), :].rearrange("(p c) d -> p c d", p=P)
                            pev.done(sp.dma_start(rows[:, q * TT:(q + 1) * TT, :], og[:, q % 2]), f"out{q % 2}")
                        if more:
                            load(i + 1, u)

                turns(sp, turn)
                for k in range(2):
                    sp.wait_ge(pev.sem[f"out{k}"], 16 * (E * NCH // 2 + 1))

            @block.gpsimd
            def _(pool):
                pool.wait_ge(ready, 1)
                with pool.Fori(0, NTURN) as i:
                    for u in range(2):
                        pev.wait(pool, f"t{u}", i, 1)
                        for q in range(NCH):
                            n = i * TURN + u * NCH + q
                            ev.wait(pool, "tr", n - 1 if u or q else n, 0)
                            pool.sem_inc(passed, 1)
                            for t in range(TT):
                                c = q * TT + t
                                pool.indirect_dma_start(
                                    out=xg[:, q % 2, t, :], out_offset=None, in_=dram["xn1"],
                                    in_offset=bass.IndirectOffsetOnAxis(ap=table[:, u, c:c + 1], axis=0)
                                ).then_inc(pev.sem[f"g{q % 2}"], 16)

            @block.tensor
            def _(pe):
                pe.wait_ge(consts, 48)
                pe.wait_ge(ready, 1)

                def turn_tokens(i, c):
                    n = i * TURN + c
                    pev.wait(pe, f"g{c % 2}", i * (TURN // 2) + c // 2, TT)
                    ev.wait(pe, "xl", n, 0)
                    for k in range(DC):
                        for t in range(TT):
                            last = pe.transpose(tb[:, k, t * P:(t + 1) * P], xg[:, c % 2, t, k * P:(k + 1) * P], ident[:])
                    ev.done(last, "tr")

                def product(out, pairs):
                    for j, (ah, al, bh, bl) in enumerate(pairs):
                        pe.matmul(out, ah, bh, start=(j == 0), stop=False)
                        pe.matmul(out, ah, bl, start=False, stop=False)
                        last = pe.matmul(out, al, bh, start=False, stop=(j == len(pairs) - 1))
                    return last

                def turn(i, more):
                    for c in range(TURN):
                        n = i * TURN + c
                        u = c // NCH
                        if c % NCH == 0:
                            xev.wait(pe, "wl", 2 * i + u, 1)
                        ev.wait(pe, "xl", n, DC)
                        for m in range(HC):
                            ev.wait(pe, "hraw", n, max(m - NH + 1, 0))
                            cols = slice(m * P, (m + 1) * P)
                            last = product(hb[:, m % NH, :], [
                                (w1h[:, u, k, cols], w1l[:, u, k, cols], xh[:, k, :], xl[:, k, :])
                                for k in range(DC)])
                            ev.done(last, "h")
                        if c < TURN - 1 or more:
                            turn_tokens(i, c + 1)
                        if c % NCH == 0:
                            xev.wait(pe, "wl", 2 * i + u, 2)
                        for t in range(TT):
                            ev.wait(pe, "oc", n, max(t - 1, 0))
                            rows = slice(t * P, (t + 1) * P)
                            for m in range(HC):
                                if t == 0:
                                    ev.wait(pe, "hl", n, m + 1)
                                out = ob[:, t % 2, 0:D]
                                high, low = hh[:, c % 2, m, rows], hl[:, c % 2, m, rows]
                                pe.matmul(out, high, w2h[:, u, m, :], start=(m == 0), stop=False)
                                pe.matmul(out, high, w2l[:, u, m, :], start=False, stop=False)
                                last = pe.matmul(out, low, w2h[:, u, m, :], start=False, stop=(m == HC - 1))
                            ev.done(last, "o")

                turn_tokens(0, 0)
                turns(pe, turn)

            @block.scalar
            def _(act):
                act.wait_ge(consts, 48)
                act.wait_ge(ready, 1)

                def split_tokens(n):
                    ev.wait(act, "tr", n, 1)
                    ev.wait(act, "h", n, 0)
                    for k in range(DC):
                        ev.done(act.activation(xh[:, k, :], tb[:, k, :], ACT.Copy), "xh")

                def split_weights(i, u):
                    pev.wait(act, f"w{u}", i, 2)
                    for dst, src in ((w1h, w1), (w2h, w2)):
                        xev.done(act.activation(dst[:, u], src[:, u], ACT.Copy), "wh")

                def turn(i, more):
                    for c in range(TURN):
                        n = i * TURN + c
                        u = c // NCH
                        if c % NCH == 0:
                            xev.wait(act, "now", 2 * i + u, 2)
                        for m in range(HC):
                            ev.wait(act, "h", n, m + 1)
                            if m == 0:
                                ev.wait(act, "o", n, 0)
                            ev.done(act.activation(hh[:, c % 2, m, :], hb[:, m % NH, :], ACT.Relu, bias=b1now[:, u, m:m + 1]), "hh")
                        if c < TURN - 1 or more:
                            split_tokens(n + 1)
                        if c == NCH - 2:
                            split_weights(i, 1)
                        if c == TURN - 2 and more:
                            split_weights(i + 1, 0)

                split_weights(0, 0)
                split_tokens(0)
                turns(act, turn)

            @block.vector
            def _(dve):
                for one in (ev, pev, xev):
                    one.start(dve)
                dve.wait_ge(consts, 48)
                dve.sem_inc(ready, 1)

                def split_tokens(n):
                    for k in range(DC):
                        ev.wait(dve, "xh", n, k + 1)
                        ev.done(dve.tensor_tensor(xl[:, k, :], tb[:, k, :], xh[:, k, :].bitcast(F32), ALU.subtract), "xl")

                def split_weights(i, u):
                    for j, (high, low, w) in enumerate(((w1h, w1l, w1), (w2h, w2l, w2))):
                        xev.wait(dve, "wh", 2 * i + u, j + 1)
                        xev.done(dve.tensor_tensor(low[:, u], w[:, u], high[:, u].bitcast(F32), ALU.subtract), "wl")

                def turn(i, more):
                    for c in range(TURN):
                        n = i * TURN + c
                        u = c // NCH
                        if c % NCH == 0:
                            ev.wait(dve, "hh", n, 0)
                            dve.sem_inc(passed, 1)
                            xev.done(dve.tensor_copy(b1now[:, u:u + 1], b1[:, at(i, u)]), "now")
                            xev.done(dve.tensor_copy(b2now[:, u:u + 1], b2[:, at(i, u)]), "now")
                            xev.wait(dve, "now", 2 * i + u, 2)
                        for m in range(HC):
                            ev.wait(dve, "hh", n, m + 1)
                            ev.wait(dve, "hl", n, max(m - 1, 0))
                            ev.done(dve.tensor_scalar(h[:, m % 2], hb[:, m % NH, :], b1now[:, u, m:m + 1], 0.0,
                                                      ALU.add, ALU.max), "hraw")
                            ev.wait(dve, "hraw", n, m + 1)
                            ev.done(dve.tensor_tensor(hl[:, c % 2, m, :], h[:, m % 2], hh[:, c % 2, m, :].bitcast(F32),
                                                      ALU.subtract), "hl")
                        if c < TURN - 1 or more:
                            split_tokens(n + 1)
                        if c == NCH - 2:
                            split_weights(i, 1)
                        if c == TURN - 2 and more:
                            split_weights(i + 1, 0)
                        for t in range(TT):
                            ev.wait(dve, "o", n, t + 1)
                            if t == 0:
                                pev.wait(dve, f"out{c % 2}", i * (TURN // 2) + c // 2, 0)
                            ev.done(dve.tensor_tensor(og[:, c % 2, t, :], ob[:, t % 2, 0:D], b2now[:, u], ALU.add), "oc")

                split_weights(0, 0)
                split_tokens(0)
                turns(dve, turn)


def combine_phase(nc, io, dram, keep, out):
    with ExitStack() as ctx:
        def sb(name, shape, dt=F32):
            return ctx.enter_context(nc.sbuf_tensor("f_" + name, shape, dt))

        def ps(name, shape, dt=F32):
            return ctx.enter_context(nc.psum_tensor("f_" + name, shape, dt))

        ident = sb("ident", [P, P])
        wo = sb("wo", [P, DC, D])
        bo = sb("bo", [P, D])
        y = sb("y", [P, 2, TT, NG, G * HD])
        x1 = sb("x1", [P, 2, TT, D])
        slot = sb("slot", [P, TOPK, NQT], I32)
        gate = sb("gate", [P, TOPK, NQT])
        rows = sb("rows", [P, SPB, TOPK, TT, D])
        yT = sb("yT", [P, DC, SEG])
        z = sb("z", [P, TT, D])
        th = sb("th", [P, TT, D])
        s = sb("s", [P, TT, D])
        res = sb("res", [P, 2, TT, D])
        tb = ps("tb", [P, DC, SEG])
        sc = ps("sc", [P, 2, SEG])

        inputs = {f"{a}{k}": c for a, c in (("in", NG + 1), ("out", 1)) for k in range(2)}
        ev = Events(nc, ctx, "f", dict(tr=1, trc=DC, so=2, sb=2, z=1, th=1, res=1), set())
        par = Events(nc, ctx, "fp", inputs, set(inputs))
        gathers = {f"rows{c}": TOPK * TT for c in range(SPB)}
        bev = Events(nc, ctx, "fb", dict(gate=1, **gathers), set(gathers), set(gathers))
        consts = ctx.enter_context(nc.semaphore("f_consts"))
        ready = ctx.enter_context(nc.semaphore("f_ready"))
        passed = ctx.enter_context(nc.semaphore("f_passed"))
        dve_step = ctx.enter_context(nc.semaphore("f_dve_step"))
        slots = ctx.enter_context(nc.semaphore("f_slots"))
        DVE_STEPS = SPB * 9
        out_rows = out.rearrange("b m d -> (b m) d")

        with nc.Block() as block:
            @block.sync
            def _(sp):
                for dst, src in ((ident[:], io["c_ident"]), (wo[:], io["wo1T"].rearrange("(k p) n -> p k n", p=P)),
                                 (bo[:], io["bo1"].partition_broadcast(P))):
                    sp.dma_start(dst, src).then_inc(consts, 16)
                sp.wait_ge(ready, 1)

                def load(b, c):
                    k = c % 2
                    for hg in range(NG):
                        src = dram["y"][bass.ds(b * NG + hg, 1), c * SEG:(c + 1) * SEG, :]
                        par.done(sp.dma_start(y[:, k, :, hg, :], src.rearrange("o (t p) d -> p (o t) d", p=P)), f"in{k}")
                    par.done(sp.dma_start(x1[:, k], dram["x1"][bass.ds(b * M + c * SEG, SEG), :].rearrange("(t p) d -> p t d", p=P)), f"in{k}")

                def batch(b, more):
                    for c in range(SPB):
                        n = b * SPB + c
                        ev.wait(sp, "res", n, 1)
                        par.done(sp.dma_start(out_rows[bass.ds(b * M + c * SEG, SEG), :].rearrange("(t p) d -> p t d", p=P),
                                              res[:, c % 2]), f"out{c % 2}")
                        if c + 2 < SPB:
                            load(b, c + 2)
                        elif more:
                            load(b + 1, c + 2 - SPB)

                load(0, 0)
                load(0, 1)
                with sp.Fori(0, B - 1) as b:
                    batch(b, True)
                batch(B - 1, False)
                for k in range(2):
                    sp.wait_ge(par.sem[f"out{k}"], 16 * (NSEG // 2 + 1))

            @block.gpsimd
            def _(pool):
                pool.wait_ge(ready, 1)

                def gather(b, again):
                    if again:
                        bev.wait(pool, f"rows{SPB - 1}", b, 0)
                        pool.sem_inc(passed, 1)
                    pool.tensor_copy(slot[:], keep["slot"][:, :, bass.ds(b * NQT, NQT)]).then_inc(slots, 1)
                    pool.wait_ge(slots, b + 1)
                    for c in range(SPB):
                        n = b * SPB + c
                        if again:
                            ev.wait(pool, "z", n, 1 - SPB)
                        pool.sem_inc(passed, 1)
                        for k in range(TOPK):
                            for t in range(TT):
                                at = c * TT + t
                                pool.indirect_dma_start(
                                    out=rows[:, c, k, t, :], out_offset=None, in_=dram["eo"],
                                    in_offset=bass.IndirectOffsetOnAxis(ap=slot[:, k, at:at + 1], axis=0)
                                ).then_inc(bev.sem[f"rows{c}"], 16)

                gather(0, False)
                with pool.Fori(1, B) as b:
                    gather(b, True)

            @block.tensor
            def _(pe):
                pe.wait_ge(consts, 48)
                pe.wait_ge(ready, 1)
                with pe.Fori(0, B) as b:
                    for c in range(SPB):
                        n = b * SPB + c
                        par.wait(pe, f"in{c % 2}", b * (SPB // 2) + c // 2, NG + 1)
                        ev.wait(pe, "trc", n, 0)
                        ysrc = y[:, c % 2].rearrange("p t g d -> p t (g d)")
                        for k in range(DC):
                            for t in range(TT):
                                last = pe.transpose(tb[:, k, t * P:(t + 1) * P], ysrc[:, t, k * P:(k + 1) * P], ident[:])
                        ev.done(last, "tr")
                        ev.wait(pe, "trc", n, DC)
                        ev.wait(pe, "sb", n, 0)
                        for f in range(2):
                            for t in (2 * f, 2 * f + 1):
                                for k in range(DC):
                                    last = pe.matmul(sc[:, f, (t % 2) * D:(t % 2 + 1) * D], yT[:, k, t * P:(t + 1) * P],
                                                     wo[:, k, :], start=(k == 0), stop=(k == DC - 1))
                            ev.done(last, "so")

            @block.scalar
            def _(act):
                act.wait_ge(ready, 1)
                with act.Fori(0, B) as b:
                    for c in range(SPB):
                        n = b * SPB + c
                        ev.wait(act, "tr", n, 1)
                        ev.wait(act, "so", n, 0)
                        for k in range(DC):
                            ev.done(act.activation(yT[:, k, :], tb[:, k, :], ACT.Copy), "trc")
                        ev.wait(act, "z", n, 1)
                        ev.wait(act, "res", n, 0)
                        ev.done(act.activation(th[:], z[:], ACT.Tanh, scale=0.5), "th")

            @block.vector
            def _(dve):
                ev.start(dve)
                par.start(dve)
                bev.start(dve)
                dve.wait_ge(consts, 48)
                dve.sem_inc(ready, 1)

                with dve.Fori(0, B) as b:
                    st = Steps(dve, dve_step, b * DVE_STEPS, ev)
                    st.last = ev.sem["res"], ev.at("res", b * SPB, 0)
                    for c in range(SPB):
                        n = b * SPB + c
                        st.step(n)
                        k = c % 2
                        bev.wait(dve, f"rows{c}", b, TOPK * TT)
                        if c == 0:
                            ev.wait(dve, "z", n, 0)
                            dve.sem_inc(passed, 1)
                            bev.done(dve.tensor_copy(gate[:], keep["gate"][:, :, bass.ds(b * NQT, NQT)]), "gate")
                            bev.wait(dve, "gate", b, 1)
                        ev.wait(dve, "th", n, 0)
                        ev.wait(dve, "sb", n, 0)
                        for t in range(TT):
                            st.then(dve.tensor_scalar(s[:, t], rows[:, c, 1, t], gate[:, 1, c * TT + t:c * TT + t + 1], None, ALU.mult))
                        st.settle()
                        for t in range(TT):
                            last = dve.scalar_tensor_tensor(out=z[:, t], in0=rows[:, c, 0, t], scalar=gate[:, 0, c * TT + t:c * TT + t + 1],
                                                            in1=s[:, t], op0=ALU.mult, op1=ALU.add)
                            st.mark(last, "z") if t == TT - 1 else st.then(last)
                        st.settle()
                        for f in range(2):
                            ev.wait(dve, "so", n, f + 1)
                            st.mark(dve.tensor_tensor(s[:, 2 * f:2 * f + 2], sc[:, f, :].rearrange("p (t d) -> p t d", d=D),
                                                        bo[:].unsqueeze(1).to_broadcast([P, 2, D]), ALU.add), "sb")
                        ev.wait(dve, "th", n, 1)
                        st.then(dve.scalar_tensor_tensor(out=z[:], in0=th[:], scalar=1.0, in1=z[:], op0=ALU.add, op1=ALU.mult))
                        st.settle()
                        st.then(dve.scalar_tensor_tensor(out=z[:], in0=z[:], scalar=0.5, in1=s[:], op0=ALU.mult, op1=ALU.mult))
                        st.settle()
                        par.wait(dve, f"out{k}", b * (SPB // 2) + c // 2, 0)
                        par.wait(dve, f"in{k}", b * (SPB // 2) + c // 2, NG + 1)
                        st.mark(dve.tensor_tensor(res[:, k], z[:], x1[:, k], ALU.add), "res")
                        st.settle()
                    assert st.n == DVE_STEPS, st.n


def build(nc, io, out):
    with ExitStack() as ctx:
        dram = {name: nc.dram_tensor("s_" + name, shape, dt, kind="Internal").ap() for name, shape, dt in SCRATCH}
        keep = {name: ctx.enter_context(nc.sbuf_tensor("keep_" + name, shape, dt)) for name, shape, dt in (
            ("slot", [P, TOPK, NT], I32), ("dest", [P, TOPK, NT], I32), ("gate", [P, TOPK, NT], F32),
            ("token", [P, NT], I32))}
        layers_phase(nc, io, dram)
        attend_phase(nc, io, dram, keep)
        experts_phase(nc, io, dram)
        combine_phase(nc, io, dram, keep, out)


SCRATCH = [
    ("x1", (T, D), F32), ("xn1", (T, D), F32), ("qk", (2, NGROUPS, PIECE, 2, G * HD // 2, M), BF16),
    ("v", (NGROUPS, M, G * HW), F32), ("logits", (P, NT, E), F32), ("table", (NSLOT + TOPK * T, 1), I32),
    ("y", (NGROUPS, M, G * HD), F32), ("eo", (NSLOT, D), F32),
]


def constants():
    bf = mybir.dt.np(BF16)
    i = np.arange(P)
    inv_freq = (np.float32(1.0) / np.float32(10000.0) ** (np.arange(0, HD, 2, dtype=np.float32) / np.float32(HD)))
    angle = np.arange(M, dtype=np.float32)[None, :] * inv_freq.astype(np.float32)[i % (HD // 2)][:, None]
    token = (np.arange(NT)[None, :] * P + i[:, None])
    return {
        "c_ident": np.eye(P, dtype=np.float32),
        "c_identb": np.eye(P).astype(bf),
        "c_headmask": (i[:, None] // HD == np.arange(H // DC)[None, :]).astype(np.float32),
        "c_rope": np.stack([np.cos(angle), np.sin(angle)], axis=1).astype(np.float32),
        "c_mask_q": np.where(i[None, :] <= i[:, None], 0.0, MASKED).astype(bf),
        "c_mask_k": np.where(i[:, None] <= i[None, :], 0.0, MASKED).astype(bf),
        "c_before": (i[:, None] < i[None, :]).astype(bf),
        "c_ones": np.ones((P, 2048)).astype(bf),
        "c_expert": np.tile(np.arange(E, dtype=np.float32), (P, 1)),
        "c_token": token.astype(np.int32),
        "c_spill": np.stack([NSLOT + k * T + token for k in range(TOPK)], axis=1).astype(np.float32),
    }


def layout(a):
    t = lambda w: np.ascontiguousarray(np.asarray(w).T)
    pairs = lambda w: np.asarray(w).reshape(H, HD // 2, 2, -1).transpose(2, 0, 1, 3).reshape(D, -1)
    bias = lambda v: pairs(np.asarray(v)[:, None]).reshape(2, P)
    return {
        "x": np.asarray(a["L0_attn_x"]),
        "wqkv0T": t(a["L0_attn_Wqkv"]), "wout0T": t(a["L0_attn_Wout"]), "wfT": t(a["L0_ffn_weight_fp8"]),
        "fbias": np.asarray(a["L0_ffn_bias"]), "in_scale": np.asarray(a["L0_ffn_input_scale"]),
        "w_scale": np.asarray(a["L0_ffn_weight_scale"]),
        "wqk1T": np.ascontiguousarray(np.concatenate([pairs(a["L1_attn_wq"]), pairs(a["L1_attn_wk"])]).T),
        "bqk1": np.ascontiguousarray(np.concatenate([bias(a["L1_attn_bq"]), bias(a["L1_attn_bk"])]).T),
        "wvg1T": np.ascontiguousarray(np.concatenate([t(a["L1_attn_wv"]), np.asarray(a["L1_ffn_wg"])], axis=1)),
        "bv1": np.asarray(a["L1_attn_bv"]), "wo1T": t(a["L1_attn_wo"]), "bo1": np.asarray(a["L1_attn_bo"]),
        "w1": np.asarray(a["L1_ffn_w1"]),
        "b1T": np.ascontiguousarray(np.asarray(a["L1_ffn_b1"]).reshape(E, HID // P, P).transpose(2, 0, 1)),
        "w2": np.asarray(a["L1_ffn_w2"]), "b2": np.asarray(a["L1_ffn_b2"]),
    }


def kernel(**inputs):
    import concourse.bacc as _bacc
    from concourse.bass_utils import run_bass_kernel_spmd as _run

    arrays = {**layout(inputs), **constants()}
    nc = _bacc.Bacc("TRN2", target_bir_lowering=False, num_devices=1)
    io = {name: nc.dram_tensor(name, a.shape, mybir.dt.from_np(a.dtype), kind="ExternalInput").ap()
          for name, a in arrays.items()}
    out = nc.dram_tensor("out", (B, M, D), F32, kind="ExternalOutput").ap()
    build(nc, io, out)
    r = _run(nc, [arrays], core_ids=[0])
    return r.results[0]["out"]
```
